# Optimizing a Trainium2 kernel written in Bass

```python
import numpy as np
import jax
import jax.numpy as jnp

def _softmax(x, axis=-1):
    return jax.nn.softmax(x, axis=axis)

def _gelu(x):
    return jax.nn.gelu(x, approximate=True)

def _silu(x):
    return jax.nn.silu(x)

def _sigmoid(x):
    return jax.nn.sigmoid(x)

def _layernorm(x, axis=-1, eps=1e-05):
    m = jnp.mean(x, axis=axis, keepdims=True)
    v = jnp.var(x, axis=axis, keepdims=True)
    return (x - m) / jnp.sqrt(v + eps)

def _scatter_add(tgt, idx, src, axis=0):
    return tgt.at[idx].add(src)

def _segment_sum(src, seg, n):
    return jax.ops.segment_sum(src, seg, n)
kernel_name = 'mk_lm_tower_d2_tok_ids256_r4_7f9437'

def setup_inputs(seed: int=0):
    np.random.seed(seed)
    _w = jnp.asarray

    def _rec_inputs():
        import jax
        import jax.numpy as jnp
        _rk = jax.random.key(seed)
        x = jax.random.randint(jax.random.fold_in(_rk, 1), (16, 256), 0, 31993, jnp.int32)
        return x
    x = _rec_inputs()

    def _L0_tok_setup():
        import jax, jax.numpy as jnp
        import numpy as np
        VOCAB = 8000
        EMBED_DIM = 64
        NUM_RULES = 100
        BATCH, SEQ = (4, 512)
        key = jax.random.key(seed)
        k1, k2, k3, k4 = jax.random.split(key, 4)
        token_ids = jax.random.randint(k1, (BATCH, SEQ), 0, VOCAB)
        base_embeddings = jax.random.normal(k2, (VOCAB, EMBED_DIM), dtype=jnp.float32)
        rule_transform = jax.random.normal(k3, (NUM_RULES, EMBED_DIM, EMBED_DIM), dtype=jnp.float32)
        token_rules = jax.random.randint(k4, (VOCAB,), 0, NUM_RULES)
        return {'token_ids': token_ids, 'base_embeddings': base_embeddings, 'rule_transform': rule_transform, 'token_rules': token_rules}
    _L0_tok_all = _L0_tok_setup()
    _L0_tok_in = {k: v for k, v in _L0_tok_all.items() if k in ('base_embeddings', 'rule_transform', 'token_rules')}
    del _L0_tok_all

    def _L0_attn_setup():
        import jax, jax.numpy as jnp
        import numpy as np
        SEQ_LEN = 512
        EMBED_DIM = 64
        BATCH = 8
        LN_EPS = 1e-05

        def _layernorm(x, g, b):
            mu = jnp.mean(x, axis=-1, keepdims=True)
            var = jnp.mean(jnp.square(x - mu), axis=-1, keepdims=True)
            return (x - mu) * jax.lax.rsqrt(var + LN_EPS) * g + b
        key = jax.random.key(seed)
        ks = jax.random.split(key, 8)
        C = EMBED_DIM
        x = jax.random.normal(ks[0], (BATCH, SEQ_LEN, C), dtype=jnp.float32)
        qkv_w = jax.random.normal(ks[1], (C, 3 * C), dtype=jnp.float32) * 0.02
        qkv_b = jnp.zeros((3 * C,), dtype=jnp.float32)
        proj_w = jax.random.normal(ks[2], (C, C), dtype=jnp.float32) * 0.02
        proj_b = jnp.zeros((C,), dtype=jnp.float32)
        ln1_g = jnp.ones((C,), dtype=jnp.float32)
        ln1_b = jnp.zeros((C,), dtype=jnp.float32)
        ln2_g = jnp.ones((C,), dtype=jnp.float32)
        ln2_b = jnp.zeros((C,), dtype=jnp.float32)
        bias_table = jax.random.truncated_normal(ks[3], -2.0, 2.0, (2 * SEQ_LEN - 1,), dtype=jnp.float32) * 0.02
        scale = jnp.asarray(1.0 / np.sqrt(C), dtype=jnp.float32)
        return {'x': x, 'ln1_g': ln1_g, 'ln1_b': ln1_b, 'qkv_w': qkv_w, 'qkv_b': qkv_b, 'bias_table': bias_table, 'scale': scale, 'proj_w': proj_w, 'proj_b': proj_b, 'ln2_g': ln2_g, 'ln2_b': ln2_b}
    _L0_attn_all = _L0_attn_setup()
    _L0_attn_in = {k: v for k, v in _L0_attn_all.items() if k in ('ln1_g', 'ln1_b', 'qkv_w', 'qkv_b', 'bias_table', 'scale', 'proj_w', 'proj_b', 'ln2_g', 'ln2_b')}
    del _L0_attn_all

    def _L0_ffn_setup():
        import jax, jax.numpy as jnp
        import numpy as np
        B, T, D, H, L = (16, 1024, 64, 64, 2)

        def _lstm(x, W_ih, W_hh, b_ih, b_hh):
            x_proj = jnp.einsum('btd,gd->btg', x, W_ih) + b_ih + b_hh
            h0 = jnp.zeros((x.shape[0], W_hh.shape[1]), x.dtype)
            c0 = jnp.zeros_like(h0)

            def step(carry, xp):
                h, c = carry
                gates = xp + h @ W_hh.T
                i, f, g, o = jnp.split(gates, 4, axis=-1)
                c = jax.nn.sigmoid(f) * c + jax.nn.sigmoid(i) * jnp.tanh(g)
                h = jax.nn.sigmoid(o) * jnp.tanh(c)
                return ((h, c), h)
            _, hs = jax.lax.scan(step, (h0, c0), jnp.swapaxes(x_proj, 0, 1))
            return jnp.swapaxes(hs, 0, 1)
        key = jax.random.key(seed)
        ks = jax.random.split(key, 9)
        s = 1.0 / np.sqrt(H)
        u = lambda k, shape: jax.random.uniform(k, shape, jnp.float32, -s, s)
        return {'x': jax.random.normal(ks[0], (B, T, D), jnp.float32), 'W_ih': u(ks[1], (4 * H, D)), 'W_hh': u(ks[2], (4 * H, H)), 'b_ih': u(ks[3], (4 * H,)), 'b_hh': u(ks[4], (4 * H,)), 'W_lin': u(ks[5], (L, H)), 'b_lin': u(ks[6], (L,)), 'fw_att': jnp.full((1, H), 0.001, jnp.float32), 'bw_att': jnp.full((1, H), 0.001, jnp.float32)}
    _L0_ffn_all = _L0_ffn_setup()
    _L0_ffn_in = {k: v for k, v in _L0_ffn_all.items() if k in ('W_ih', 'W_hh', 'b_ih', 'b_hh', 'W_lin', 'b_lin', 'fw_att', 'bw_att')}
    del _L0_ffn_all

    def _L1_attn_setup():
        import jax, jax.numpy as jnp
        import numpy as np
        key = jax.random.key(seed)
        k1, k2 = jax.random.split(key)
        B, N, F = (4, 1024, 64)
        nodes = jax.random.normal(k1, (B, N, F), dtype=jnp.float32)
        limit = np.sqrt(6.0 / (F + F)).astype(np.float32)
        W = jax.random.uniform(k2, (F, F), dtype=jnp.float32, minval=-limit, maxval=limit)
        return {'nodes': nodes, 'W': W}
    _L1_attn_all = _L1_attn_setup()
    _L1_attn_in = {k: v for k, v in _L1_attn_all.items() if k in ('W',)}
    del _L1_attn_all

    def _L1_ffn_setup():
        import jax, jax.numpy as jnp
        import numpy as np
        D_IN, D_HID, D_OUT = (64, 128, 64)
        N_EXPERTS, TOP_K = (64, 2)
        B, S = (8, 1024)
        key = jax.random.key(seed)
        ks = jax.random.split(key, 8)
        scale_in = 1.0 / np.sqrt(D_IN)
        scale_hid = 1.0 / np.sqrt(D_HID)
        return {'x': jax.random.normal(ks[0], (B, S, D_IN), dtype=jnp.float32), 'Wr': jax.random.uniform(ks[1], (D_IN, N_EXPERTS), jnp.float32, -scale_in, scale_in), 'br': jax.random.uniform(ks[2], (N_EXPERTS,), jnp.float32, -scale_in, scale_in), 'W1': jax.random.uniform(ks[3], (N_EXPERTS, D_IN, D_HID), jnp.float32, -scale_in, scale_in), 'b1': jax.random.uniform(ks[4], (N_EXPERTS, D_HID), jnp.float32, -scale_in, scale_in), 'W2': jax.random.uniform(ks[5], (N_EXPERTS, D_HID, D_OUT), jnp.float32, -scale_hid, scale_hid), 'b2': jax.random.uniform(ks[6], (N_EXPERTS, D_OUT), jnp.float32, -scale_hid, scale_hid)}
    _L1_ffn_all = _L1_ffn_setup()
    _L1_ffn_in = {k: v for k, v in _L1_ffn_all.items() if k in ('Wr', 'br', 'W1', 'b1', 'W2', 'b2')}
    del _L1_ffn_all
    return {'x': x, 'L0_tok_base_embeddings': _L0_tok_in['base_embeddings'], 'L0_tok_rule_transform': _L0_tok_in['rule_transform'], 'L0_tok_token_rules': _L0_tok_in['token_rules'], 'L0_attn_ln1_g': _L0_attn_in['ln1_g'], 'L0_attn_ln1_b': _L0_attn_in['ln1_b'], 'L0_attn_qkv_w': _L0_attn_in['qkv_w'], 'L0_attn_qkv_b': _L0_attn_in['qkv_b'], 'L0_attn_bias_table': _L0_attn_in['bias_table'], 'L0_attn_scale': _L0_attn_in['scale'], 'L0_attn_proj_w': _L0_attn_in['proj_w'], 'L0_attn_proj_b': _L0_attn_in['proj_b'], 'L0_attn_ln2_g': _L0_attn_in['ln2_g'], 'L0_attn_ln2_b': _L0_attn_in['ln2_b'], 'L0_ffn_W_ih': _L0_ffn_in['W_ih'], 'L0_ffn_W_hh': _L0_ffn_in['W_hh'], 'L0_ffn_b_ih': _L0_ffn_in['b_ih'], 'L0_ffn_b_hh': _L0_ffn_in['b_hh'], 'L0_ffn_W_lin': _L0_ffn_in['W_lin'], 'L0_ffn_b_lin': _L0_ffn_in['b_lin'], 'L0_ffn_fw_att': _L0_ffn_in['fw_att'], 'L0_ffn_bw_att': _L0_ffn_in['bw_att'], 'L1_attn_W': _L1_attn_in['W'], 'L1_ffn_Wr': _L1_ffn_in['Wr'], 'L1_ffn_br': _L1_ffn_in['br'], 'L1_ffn_W1': _L1_ffn_in['W1'], 'L1_ffn_b1': _L1_ffn_in['b1'], 'L1_ffn_W2': _L1_ffn_in['W2'], 'L1_ffn_b2': _L1_ffn_in['b2']}

def reference(x, L0_tok_base_embeddings, L0_tok_rule_transform, L0_tok_token_rules, L0_attn_ln1_g, L0_attn_ln1_b, L0_attn_qkv_w, L0_attn_qkv_b, L0_attn_bias_table, L0_attn_scale, L0_attn_proj_w, L0_attn_proj_b, L0_attn_ln2_g, L0_attn_ln2_b, L0_ffn_W_ih, L0_ffn_W_hh, L0_ffn_b_ih, L0_ffn_b_hh, L0_ffn_W_lin, L0_ffn_b_lin, L0_ffn_fw_att, L0_ffn_bw_att, L1_attn_W, L1_ffn_Wr, L1_ffn_br, L1_ffn_W1, L1_ffn_b1, L1_ffn_W2, L1_ffn_b2):
    import jax
    import jax.numpy as jnp

    def _L0_tok_ref(token_ids, base_embeddings, rule_transform, token_rules):
        import jax, jax.numpy as jnp
        import numpy as np
        VOCAB = 8000
        EMBED_DIM = 64
        NUM_RULES = 100
        BATCH, SEQ = (4, 512)
        base_embeds = base_embeddings[token_ids]
        rule_indices = token_rules[token_ids]
        rule_matrices = rule_transform[rule_indices]
        return jnp.einsum('bsd,bsde->bse', base_embeds, rule_matrices)

    def _L0_attn_ref(x, ln1_g, ln1_b, qkv_w, qkv_b, bias_table, scale, proj_w, proj_b, ln2_g, ln2_b):
        import jax, jax.numpy as jnp
        import numpy as np
        SEQ_LEN = 512
        EMBED_DIM = 64
        BATCH = 8
        LN_EPS = 1e-05

        def _layernorm(x, g, b):
            mu = jnp.mean(x, axis=-1, keepdims=True)
            var = jnp.mean(jnp.square(x - mu), axis=-1, keepdims=True)
            return (x - mu) * jax.lax.rsqrt(var + LN_EPS) * g + b
        B, N, C = x.shape
        h = _layernorm(x, ln1_g, ln1_b)
        qkv = h @ qkv_w + qkv_b
        q, k, v = jnp.split(qkv, 3, axis=-1)
        coords = jnp.arange(N)
        rel_idx = coords[None, :] - coords[:, None] + (N - 1)
        rel_bias = bias_table[rel_idx]
        attn = jnp.einsum('bnc,bmc->bnm', q, k) + rel_bias
        attn = jax.nn.softmax(attn, axis=-1) * scale
        out = jnp.einsum('bnm,bmc->bnc', attn, v)
        out = out @ proj_w + proj_b
        out = _layernorm(out, ln2_g, ln2_b)
        return out

    def _L0_ffn_ref(x, W_ih, W_hh, b_ih, b_hh, W_lin, b_lin, fw_att, bw_att):
        import jax, jax.numpy as jnp
        import numpy as np
        B, T, D, H, L = (16, 1024, 64, 64, 2)

        def _lstm(x, W_ih, W_hh, b_ih, b_hh):
            x_proj = jnp.einsum('btd,gd->btg', x, W_ih) + b_ih + b_hh
            h0 = jnp.zeros((x.shape[0], W_hh.shape[1]), x.dtype)
            c0 = jnp.zeros_like(h0)

            def step(carry, xp):
                h, c = carry
                gates = xp + h @ W_hh.T
                i, f, g, o = jnp.split(gates, 4, axis=-1)
                c = jax.nn.sigmoid(f) * c + jax.nn.sigmoid(i) * jnp.tanh(g)
                h = jax.nn.sigmoid(o) * jnp.tanh(c)
                return ((h, c), h)
            _, hs = jax.lax.scan(step, (h0, c0), jnp.swapaxes(x_proj, 0, 1))
            return jnp.swapaxes(hs, 0, 1)
        lstm_out = _lstm(x, W_ih, W_hh, b_ih, b_hh)
        logits = jnp.einsum('bth,lh->btl', lstm_out, W_lin) + b_lin
        g = jax.lax.stop_gradient(jnp.argmax(logits, axis=-1).astype(lstm_out.dtype))[..., None]
        w = g * lstm_out
        inc = jnp.cumsum(w, axis=1)
        prefix = inc - w
        suffix = inc[:, -1:, :] - inc
        return 2.0 * lstm_out + prefix * fw_att + suffix * bw_att

    def _L1_attn_ref(nodes, W):
        import jax, jax.numpy as jnp
        import numpy as np
        F = nodes.shape[-1]
        norm_const = 1.0 / jnp.sqrt(jnp.asarray(F, dtype=nodes.dtype))
        x = jnp.einsum('bnf,fg->bng', nodes, W)
        prods = jnp.einsum('bnf,bmf->bnm', x, nodes)
        att_scores = jax.nn.softmax(prods * norm_const, axis=-1)
        messgs = jnp.einsum('bnm,bmf->bnf', att_scores, nodes)
        return messgs

    def _L1_ffn_ref(x, Wr, br, W1, b1, W2, b2):
        import jax, jax.numpy as jnp
        import numpy as np
        D_IN, D_HID, D_OUT = (64, 128, 64)
        N_EXPERTS, TOP_K = (64, 2)
        B, S = (8, 1024)
        Bx, Sx, D = x.shape
        xf = x.reshape(-1, D)
        T = xf.shape[0]
        E = Wr.shape[1]
        logits = xf @ Wr + br
        topk_logits, topk_idx = jax.lax.top_k(logits, TOP_K)
        gates = jax.nn.softmax(topk_logits, axis=1)
        combine = jnp.zeros((T, E), xf.dtype).at[jnp.arange(T)[:, None], topk_idx].add(gates)
        out = jnp.zeros((T, W2.shape[-1]), xf.dtype)
        for e in range(E):
            h = jax.nn.relu(xf @ W1[e] + b1[e])
            y = h @ W2[e] + b2[e]
            out = out + combine[:, e:e + 1] * y
        return out.reshape(Bx, Sx, -1)
    h = _L0_tok_ref(x, L0_tok_base_embeddings, L0_tok_rule_transform, L0_tok_token_rules)
    h = h + _L0_attn_ref(_layernorm(h, axis=-1), L0_attn_ln1_g, L0_attn_ln1_b, L0_attn_qkv_w, L0_attn_qkv_b, L0_attn_bias_table, L0_attn_scale, L0_attn_proj_w, L0_attn_proj_b, L0_attn_ln2_g, L0_attn_ln2_b)
    h = h + _L0_ffn_ref(_layernorm(h, axis=-1), L0_ffn_W_ih, L0_ffn_W_hh, L0_ffn_b_ih, L0_ffn_b_hh, L0_ffn_W_lin, L0_ffn_b_lin, L0_ffn_fw_att, L0_ffn_bw_att)
    h = h + _L1_attn_ref(_layernorm(h, axis=-1), L1_attn_W)
    h = h + _L1_ffn_ref(_layernorm(h, axis=-1), L1_ffn_Wr, L1_ffn_br, L1_ffn_W1, L1_ffn_b1, L1_ffn_W2, L1_ffn_b2)
    return h

_drawn_inputs = setup_inputs


def setup_inputs(seed=0):
    import zlib

    import numpy as np

    out = dict(_drawn_inputs(seed))
    spreads = {'L0_attn_ln1_g': (1.0, 0.6),
     'L0_attn_ln1_b': (0.0, 0.8),
     'L0_attn_qkv_b': (0.0, 0.8),
     'L0_attn_proj_b': (0.0, 0.1),
     'L0_attn_ln2_g': (1.0, 0.2),
     'L0_attn_ln2_b': (0.0, 0.418),
     'L0_ffn_fw_att': (0.0010000000474974513, 0.6),
     'L0_ffn_bw_att': (0.0010000000474974513, 0.6)}
    factors = {'L0_attn_qkv_w': 8.0,
     'L0_attn_bias_table': 64.0,
     'L0_attn_proj_w': 8.0,
     'L0_ffn_W_hh': 3.656,
     'L0_ffn_b_ih': 5.597,
     'L0_ffn_b_hh': 6.362,
     'L0_ffn_W_lin': 200.0,
     'L0_ffn_b_lin': 200.0,
     'L1_ffn_br': 8.0,
     'L1_ffn_W1': 2.686,
     'L1_ffn_b1': 8.0,
     'L1_ffn_b2': 8.0}
    for name, (base, spread) in spreads.items():
        noise = np.random.default_rng([zlib.crc32(name.encode()), seed]).standard_normal(out[name].shape)
        drawn = base * np.exp(spread * noise) if base else spread * noise
        out[name] = jnp.asarray(drawn.astype(out[name].dtype))
    for name, factor in factors.items():
        out[name] = (out[name] * factor).astype(out[name].dtype)
    return out
```

```python
from contextlib import ExitStack

import concourse.bass as bass
from concourse import mybir

P = 128
ALU = mybir.AluOpType
ACT = mybir.ActivationFunctionType
AX = mybir.AxisListType.X
F32 = mybir.dt.float32
BF16 = mybir.dt.bfloat16
I32 = mybir.dt.int32
U32 = mybir.dt.uint32

EPS = 1e-5
SLOTS = 4
STEPS = 16
HALF = STEPS // 2


def col(ap):
    return ap.rearrange("(c a) -> c a", a=1)


def row(ap):
    return ap.rearrange("(a c) -> a c", a=1)


def view(ap, offset, pattern):
    return bass.AP(tensor=ap.tensor, offset=ap.offset + offset, ap=pattern)


class Link:

    def __init__(self, engine, semaphore):
        self.engine, self.semaphore, self.count = engine, semaphore, 0

    def __call__(self, instruction):
        self.count += 1
        instruction.then_inc(self.semaphore, 1)
        self.engine.wait_ge(self.semaphore, self.count)


def wait_apart(engine, semaphore, value):
    engine.wait_ge(semaphore, value)
    engine.nop(nofuse=True)


class Shapes:
    def __init__(self, x, base, rules, rule_of, bias_table, w1, w2):
        self.B, self.L = x.shape
        self.T = self.B * self.L
        self.NT = self.T // P
        self.VOCAB, self.C = base.shape
        self.RULES = rules.shape[0]
        self.EXPERTS, _, self.HID = w1.shape
        assert self.C == 64 and self.L == 2 * P and self.HID == P and self.NT == 32
        self.RULE_ROWS = 64
        self.rule_blocks = (self.T + self.RULES * (self.RULE_ROWS - 1)) // self.RULE_ROWS
        self.rule_turns = -(-self.rule_blocks // (2 * SLOTS))
        self.RULE_BLOCKS = self.rule_turns * 2 * SLOTS
        self.expert_blocks = (2 * self.T + self.EXPERTS * (P - 1)) // P
        self.expert_turns = -(-self.expert_blocks // SLOTS)
        self.EXPERT_BLOCKS = self.expert_turns * SLOTS
        self.ROWS = max(self.RULE_BLOCKS * self.RULE_ROWS, self.EXPERT_BLOCKS * P)


def tower(nc, ins, out):
    s = Shapes(ins["x"], ins["L0_tok_base_embeddings"], ins["L0_tok_rule_transform"],
               ins["L0_tok_token_rules"], ins["L0_attn_bias_table"], ins["L1_ffn_W1"], ins["L1_ffn_W2"])
    with ExitStack() as ctx:
        m = Memory(nc, ctx, s)
        constants_and_ids(nc, m, s, ins)
        prepare_weights(nc, m, s, ins)
        gather_tokens(nc, m, s, ins)
        one_hot_rules(nc, m, s)
        route(nc, m, s, s.RULES, s.RULE_ROWS, s.RULE_BLOCKS, "rule")
        rule_positions(nc, m, s)
        rule_blocks(nc, m, s, ins)
        layer_norm(nc, m, s, m.h, m.xc, m.rstd, "ln_attn0", twice=True)
        attention(nc, m, s, 0)
        after_attention0(nc, m, s)
        layer_norm(nc, m, s, m.h, m.xc, m.rstd, "ln_lstm")
        lstm_inputs(nc, m, s)
        lstm(nc, m, s)
        lstm_output(nc, m, s)
        layer_norm(nc, m, s, m.h, m.xc, m.rstd, "ln_attn1")
        attention(nc, m, s, 1)
        add_messages(nc, m, s)
        layer_norm(nc, m, s, m.h, m.xc, m.rstd, "ln_moe")
        router(nc, m, s)
        route(nc, m, s, s.EXPERTS, P, s.EXPERT_BLOCKS, "expert")
        expert_positions(nc, m, s)
        expert_blocks(nc, m, s, ins)
        combine(nc, m, s, out)


class Memory:

    def __init__(self, nc, ctx, s):
        self.nc, self.ctx = nc, ctx

        def sb(name, shape, dt=F32):
            return ctx.enter_context(nc.sbuf_tensor(name, shape, dt))

        NT, C, T, B = s.NT, s.C, s.T, s.B
        self.rows_in = nc.dram_tensor("rows_in", [s.ROWS, C], F32)
        self.rows_out = nc.dram_tensor("rows_out", [s.ROWS, C], F32)
        self.bank = [ctx.enter_context(nc.psum_tensor(f"bank{i}", [P, 512], F32)) for i in range(8)]
        self.ident = sb("ident", [P, P])
        self.anti = sb("anti", [P, P])
        self.upto = sb("upto", [P, P])
        self.ones = sb("ones", [P, P])
        self.ones_b = sb("ones_b", [P, P], BF16)
        self.before_b = sb("before_b", [P, P], BF16)
        self.iota = sb("iota", [P, 256])
        self.zeros = sb("zeros", [P, s.ROWS * C // P // 4])
        self.ids = sb("ids", [NT, P], I32)
        self.ids_f = sb("ids_f", [NT, P])
        self.ids_neg = sb("ids_neg", [NT, P])
        self.id_col = sb("id_col", [P, NT], I32)
        self.rule_i = sb("rule_i", [P, NT], I32)
        self.rule_f = sb("rule_f", [P, NT])
        W = max(NT * s.RULES, T)
        self.mask = sb("mask", [P, NT * s.RULES], BF16)
        self.first = sb("first", [P, NT * 64], BF16)
        self.second = sb("second", [P, NT * 64], BF16)
        self.spread = sb("spread", [P, W])
        self.place = sb("place", [P, W])
        self.count = sb("count", [P, NT])
        self.prefix = sb("prefix", [P, NT])
        self.ones_nt = sb("ones_nt", [P, NT])
        self.blocks_f = sb("blocks_f", [P, 4])
        self.blocks_i = sb("blocks_i", [P, 2], I32)
        self.offset = sb("offset", [P, NT])
        self.ended = sb("ended", [P, 256])
        self.owner_f = sb("owner_f", [1, 256])
        self.owner_i = sb("owner_i", [1, 256], I32)
        self.pos_f = sb("pos_f", [P, 2, NT])
        self.pos_i = sb("pos_i", [P, 2, NT], I32)
        self.h = sb("h", [P, NT, C])
        self.xc = sb("xc", [P, NT, C])
        self.sq = sb("sq", [P, NT, C])
        self.msg = sb("msg", [P, NT, C])
        self.mean = sb("mean", [P, NT])
        self.var = sb("var", [P, NT])
        self.std = sb("std", [P, NT])
        self.rstd = sb("rstd", [P, NT])
        self.xb = [sb(f"xb{k}", [P, P]) for k in range(SLOTS)]
        self.xT = [sb(f"xT{k}", [C + 1, P]) for k in range(SLOTS)]
        self.wa = [sb(f"wa{k}", [C + 1, P]) for k in range(SLOTS)]
        self.wb = [sb(f"wb{k}", [P, C]) for k in range(SLOTS)]
        self.b2 = [sb(f"b2_{k}", [1, C]) for k in range(SLOTS)]
        self.hT = [sb(f"hT{k}", [P, P]) for k in range(SLOTS)]
        self.yb = [sb(f"yb{k}", [P, C]) for k in range(SLOTS)]
        self.qkv = sb("qkv", [C + 1, 3 * C])
        self.fold = sb("fold", [C + 1, C + 1])
        self.g1 = sb("g1", [C, 1])
        self.b1 = sb("b1", [C, 1])
        self.wp = sb("wp", [C, C])
        self.qkvT = [sb(f"qkvT{k}", [C, C + 1]) for k in range(3)]
        self.mqk = [sb("mqk0", [C + 1, C + 1]), sb("mqk1", [C, C])]
        self.wvp = sb("wvp", [C + 1, C])
        self.hankel = sb("hankel", [P, 3 * P])
        self.relbias = sb("relbias", [P, 3 * P])
        self.scale = sb("scale", [P, 1])
        self.pbias = sb("pbias", [P, C])
        self.g2 = sb("g2", [P, C])
        self.b2ln = sb("b2ln", [P, C])
        self.an = [sb(f"an{k}", [P, 2, C]) for k in range(2)]
        self.aT = [sb(f"aT{k}", [C + 1, 2 * P]) for k in range(2)]
        self.qT = [sb(f"qT{k}", [C + 1, 2 * P]) for k in range(2)]
        self.v = [sb(f"v{k}", [P, 2, C]) for k in range(2)]
        self.sc = [sb(f"sc{k}", [P, 2, 2 * P]) for k in range(2)]
        self.pr = [sb(f"pr{k}", [P, 2, 2 * P]) for k in range(2)]
        self.pT = [sb(f"pT{k}", [P, 2, 2 * P]) for k in range(2)]
        self.stat = [sb(f"stat{k}", [P, 8]) for k in range(2)]
        self.wraw = [sb(f"wraw{k}", [P, 2, C]) for k in range(2)]
        self.wi = sb("wi", [C + 1, 4 * C])
        self.wh = sb("wh", [C, 4 * C])
        self.bsum = sb("bsum", [C + 1, 2, 4 * C])
        self.wlin = sb("wlin", [C, 2])
        self.wlinb = sb("wlinb", [C, 2, C])
        self.blin = sb("blin", [C, 2])
        self.fwbw = sb("fwbw", [C, 4])
        self.xseq = sb("xseq", [C + 1, T + 2 * HALF * B])
        self.ring = sb("ring", [C, STEPS, B])
        self.gates = sb("gates", [C, 2, 5, B])
        self.prod = sb("prod", [C, 2, B])
        self.tanc = sb("tanc", [C, B])
        self.hist = sb("hist", [C, T])
        self.ta, self.tb = self.place[0:C, 0:T], self.spread[0:C, 0:T]
        self.lg0 = [sb(f"lg0_{k}", [C, 512]) for k in range(2)]
        self.gt = [sb(f"gt_{k}", [C, 512]) for k in range(2)]
        self.wr = sb("wr", [C + 1, s.EXPERTS])
        self.logits = sb("logits", [P, NT, s.EXPERTS])
        self.top = sb("top", [P, NT, 8])
        self.topi = sb("topi", [P, NT, 8], U32)
        self.topf = sb("topf", [P, NT, 2])
        self.gate = sb("gate", [P, 2, NT])
        self.gtmp = sb("gtmp", [P, 3, NT])
        self.zeroed = self.sem("zeroed")
        self.loaded_w = self.sem("loaded_w")

    def sem(self, name):
        return self.ctx.enter_context(self.nc.semaphore(name))


def constants_and_ids(nc, m, s, ins):
    loaded = m.sem("ids_loaded")
    made, built, filled = m.sem("const_made"), m.sem("const_built"), m.sem("const_filled")
    turned, step = m.sem("ids_turned"), m.sem("ids_step")
    with nc.Block() as block:

        @block.gpsimd
        def _(pool):
            nc.gpsimd.memset(m.ident[:], 0.0).then_inc(made, 1)
            nc.gpsimd.memset(m.anti[:], 0.0).then_inc(made, 1)
            nc.gpsimd.memset(m.upto[:], 1.0).then_inc(made, 1)
            nc.gpsimd.memset(m.before_b[:], 1.0).then_inc(made, 1)
            pool.wait_ge(made, 4)
            for mat, cmp, fill, base, mult, step_ in (
                    (m.ident, ALU.not_equal, 1.0, 0, 1, -1), (m.anti, ALU.not_equal, 1.0, -(P - 1), 1, 1),
                    (m.upto, ALU.is_ge, 0.0, 0, -1, 1), (m.before_b, ALU.is_gt, 0.0, 0, -1, 1)):
                nc.gpsimd.affine_select(out=mat[:], in_=mat[:], compare_op=cmp, fill=fill, base=base,
                                        pattern=[[step_, P]], channel_multiplier=mult).then_inc(built, 1)
            nc.gpsimd.iota(m.iota[:], pattern=[[1, 256]], base=0, channel_multiplier=0,
                           allow_small_or_imprecise_dtypes=True).then_inc(built, 1)

        @block.sync
        def _(sp):
            sp.dma_start(m.ids[:], ins["x"].rearrange("b (h p) -> (b h) p", p=P)).then_inc(loaded, 16)
            loads = [(m.qkv[0:s.C, :], ins["L0_attn_qkv_w"]), (m.qkv[s.C:s.C + 1, :], row(ins["L0_attn_qkv_b"])),
                     (m.wp[:], ins["L0_attn_proj_w"]), (m.mqk[1][:], ins["L1_attn_W"]),
                     (m.g1[:], col(ins["L0_attn_ln1_g"])), (m.b1[:], col(ins["L0_attn_ln1_b"])),
                     (m.hankel[:], view(ins["L0_attn_bias_table"], 0, [[1, P], [1, 3 * P]])),
                     (m.scale[:], view(ins["L0_attn_scale"], 0, [[0, P], [1, 1]])),
                     (m.pbias[:], view(ins["L0_attn_proj_b"], 0, [[0, P], [1, s.C]])),
                     (m.g2[:], view(ins["L0_attn_ln2_g"], 0, [[0, P], [1, s.C]])),
                     (m.b2ln[:], view(ins["L0_attn_ln2_b"], 0, [[0, P], [1, s.C]])),
                     (m.wraw[0][:], ins["L0_ffn_W_ih"].rearrange("(k p) c -> p k c", p=P)),
                     (m.wraw[1][:], ins["L0_ffn_W_hh"].rearrange("(k p) c -> p k c", p=P)),
                     (m.bsum[s.C:s.C + 1, 0, :], row(ins["L0_ffn_b_ih"])),
                     (m.bsum[s.C:s.C + 1, 1, :], row(ins["L0_ffn_b_hh"])),
                     (m.blin[:], view(ins["L0_ffn_b_lin"], 0, [[0, s.C], [1, 2]])),
                     (m.wlin[:, 0:1], view(ins["L0_ffn_W_lin"], 0, [[1, s.C], [1, 1]])),
                     (m.wlin[:, 1:2], view(ins["L0_ffn_W_lin"], s.C, [[1, s.C], [1, 1]])),
                     (m.fwbw[:, 0:1], view(ins["L0_ffn_fw_att"], 0, [[1, s.C], [1, 1]])),
                     (m.fwbw[:, 1:2], view(ins["L0_ffn_bw_att"], 0, [[1, s.C], [1, 1]])),
                     (m.wr[0:s.C, :], ins["L1_ffn_Wr"]), (m.wr[s.C:s.C + 1, :], row(ins["L1_ffn_br"]))]
            for dst, src in loads:
                sp.dma_start(dst, src).then_inc(m.loaded_w, 16)
            m.n_loads = len(loads)

        @block.vector
        def _(dve):
            nc.vector.memset(m.zeros[:], 0.0).then_inc(filled, 1)
            nc.vector.memset(m.ones[:], 1.0).then_inc(filled, 1)
            nc.vector.memset(m.ones_b[:], 1.0).then_inc(filled, 1)
            nc.vector.memset(m.ones_nt[:], 1.0).then_inc(filled, 1)
            for k in range(2):
                nc.vector.memset(m.aT[k][s.C:s.C + 1, :], 1.0).then_inc(filled, 1)
            for k in range(SLOTS):
                nc.vector.memset(m.xT[k][s.C:s.C + 1, :], 1.0).then_inc(filled, 1)
                nc.vector.memset(m.xb[k][:, s.C:P], 0.0).then_inc(filled, 1)
            nc.vector.memset(m.xseq[:], 1.0).then_inc(filled, 1)
            nc.vector.memset(m.gates[:, 0, 0, :], 0.0).then_inc(filled, 1)
            nc.vector.memset(m.ring[:], 0.0).then_inc(filled, 1)
            link = Link(dve, step)
            dve.wait_ge(loaded, 16)
            link(nc.vector.tensor_copy(m.ids_f[:], m.ids[:]))
            link(nc.vector.tensor_scalar(m.ids_neg[:], m.ids_f[:], 0.0, float(s.VOCAB), ALU.is_lt, ALU.mult))
            link(nc.vector.tensor_tensor(m.ids_f[:], m.ids_f[:], m.ids_neg[:], ALU.add))
            link(nc.vector.tensor_scalar(m.ids_f[:], m.ids_f[:], 0.0, float(s.VOCAB - 1), ALU.max, ALU.min))
            dve.wait_ge(turned, 1)
            nc.vector.tensor_copy(m.id_col[:], m.bank[0][:, 0:s.NT]).then_inc(turned, 1)

        @block.tensor
        def _(pe):
            pe.wait_ge(step, 4)
            pe.wait_ge(built, 5)
            nc.tensor.transpose(m.bank[0][:, 0:s.NT], m.ids_f[:], m.ident[0:s.NT, 0:s.NT]).then_inc(turned, 1)

        @block.scalar
        def _(act):
            act.wait_ge(filled, 1)
            quarters = m.rows_in.ap().rearrange("(q p r) c -> q p (r c)", p=P, q=4)
            for q in range(4):
                act.dma_start(quarters[q], m.zeros[:]).then_inc(m.zeroed, 16)


def prepare_weights(nc, m, s, ins):
    pe_done, cp = m.sem("prep_product"), m.sem("prep_copied")
    C = s.C
    bank = m.bank
    with nc.Block() as block:

        @block.tensor
        def _(pe):
            pe.wait_ge(m.loaded_w, 16 * m.n_loads)
            nc.tensor.matmul(bank[1][:, 0:3 * P], m.anti[:], m.hankel[:], start=True, stop=True).then_inc(pe_done, 1)
            for w in range(2):
                for k in range(2):
                    nc.tensor.transpose(bank[2 + w][0:C, k * P:(k + 1) * P], m.wraw[w][:, k, :], m.ident[:]).then_inc(pe_done, 1)
            pe.wait_ge(cp, 1)
            for k in range(3):
                nc.tensor.matmul(bank[4][0:C, k * 65:(k + 1) * 65], m.qkv[:, k * C:(k + 1) * C], m.fold[:],
                                 start=True, stop=True, skip_group_check=True).then_inc(pe_done, 1)
            pe.wait_ge(cp, 2)
            nc.tensor.matmul(bank[5][0:C + 1, 0:C + 1], m.qkvT[0][:], m.qkvT[1][:], start=True, stop=True).then_inc(pe_done, 1)
            nc.tensor.matmul(bank[6][0:C + 1, 0:C], m.qkvT[2][:], m.wp[:], start=True, stop=True).then_inc(pe_done, 1)

        @block.vector
        def _(dve):
            link = Link(dve, m.sem("prep_step"))
            dve.wait_ge(m.loaded_w, 16 * m.n_loads)
            link(nc.vector.tensor_copy(m.fold[C:C + 1, :], m.ident[C:C + 1, 0:C + 1]))
            link(nc.vector.tensor_scalar(m.fold[0:C, 0:C], m.ident[0:C, 0:C], m.g1[:, 0:1], None, ALU.mult))
            nc.vector.tensor_copy(m.fold[0:C, C:C + 1], m.b1[:]).then_inc(cp, 1)
            dve.wait_ge(pe_done, 1)
            link(nc.vector.tensor_copy(m.relbias[:], bank[1][:, 0:3 * P]))
            dve.wait_ge(pe_done, 8)
            for k in range(3):
                ins_ = nc.vector.tensor_copy(m.qkvT[k][:], bank[4][0:C, k * 65:(k + 1) * 65])
                if k < 2:
                    link(ins_)
            ins_.then_inc(cp, 1)
            for q, r in enumerate((2, 1, 0, 3)):
                f = 1.0 if r == 2 else 0.5
                link(nc.vector.tensor_scalar(m.wi[0:C, q * C:(q + 1) * C], bank[2][0:C, r * C:(r + 1) * C], f, None, ALU.mult))
                link(nc.vector.tensor_scalar(m.wh[:, q * C:(q + 1) * C], bank[3][0:C, r * C:(r + 1) * C], 0.5 * f, None, ALU.mult))
            link(nc.vector.tensor_tensor(m.bsum[C:C + 1, 0, :], m.bsum[C:C + 1, 0, :], m.bsum[C:C + 1, 1, :], ALU.add))
            for q, r in enumerate((2, 1, 0, 3)):
                f = 1.0 if r == 2 else 0.5
                link(nc.vector.tensor_scalar(m.wi[C:C + 1, q * C:(q + 1) * C], m.bsum[C:C + 1, 0, r * C:(r + 1) * C], f, None, ALU.mult))
            for l in range(2):
                link(nc.vector.tensor_scalar(m.wlinb[:, l, :], m.ones[0:C, 0:C], m.wlin[:, l:l + 1], 0.5, ALU.mult, ALU.mult))
            link(nc.vector.tensor_scalar(m.fwbw[:, 2:3], m.fwbw[:, 0:1], 0.5, None, ALU.mult))
            link(nc.vector.tensor_scalar(m.fwbw[:, 3:4], m.fwbw[:, 1:2], -0.5, None, ALU.mult))
            dve.wait_ge(pe_done, 10)
            link(nc.vector.tensor_copy(m.mqk[0][:], bank[5][0:C + 1, 0:C + 1]))
            link(nc.vector.tensor_copy(m.wvp[:], bank[6][0:C + 1, 0:C]))


def gather_tokens(nc, m, s, ins):
    got = m.sem("tokens_gathered")
    table = ins["L0_tok_base_embeddings"]
    rule_of = col(ins["L0_tok_token_rules"])
    with nc.Block() as block:

        @block.gpsimd
        def _(pool):
            for t in range(s.NT):
                index = bass.IndirectOffsetOnAxis(ap=m.id_col[:, t:t + 1], axis=0)
                pool.indirect_dma_start(m.rule_i[:, t:t + 1], None, rule_of, index).then_inc(got, 16)
            for t in range(s.NT):
                index = bass.IndirectOffsetOnAxis(ap=m.id_col[:, t:t + 1], axis=0)
                pool.indirect_dma_start(m.h[:, t, :], None, table, index).then_inc(got, 16)
            pool.wait_ge(got, 2 * 16 * s.NT)


def one_hot_rules(nc, m, s):
    with nc.Block() as block:

        @block.vector
        def _(dve):
            link = Link(dve, m.sem("one_hot_step"))
            link(nc.vector.tensor_copy(m.rule_f[:], m.rule_i[:]))
            shape = [P, s.NT, s.RULES]
            link(nc.vector.tensor_tensor(
                m.mask[:, 0:s.NT * s.RULES].rearrange("p (t r) -> p t r", t=s.NT),
                m.rule_f[:].unsqueeze(2).to_broadcast(shape),
                m.iota[:, 0:s.RULES].unsqueeze(1).to_broadcast(shape), ALU.is_equal))


def route(nc, m, s, E, rows, n_blocks, tag):
    NT = s.NT
    counted, laid, placed, done = (m.sem(f"{tag}_{x}") for x in ("counted", "laid", "placed", "placed_read"))
    group = 512 // E if 512 // E < 8 else 8
    while NT % group:
        group -= 1
    groups = NT // group
    W = group * E
    mask = m.mask[:, 0:NT * E]
    diag = m.spread[0:E, 0:NT * E].rearrange("e (t f) -> e t f", t=NT)
    shift = rows.bit_length() - 1
    with nc.Block() as block:

        @block.tensor
        def _(pe):
            for t in range(NT):
                ins = nc.tensor.matmul(m.bank[0][0:E, t:t + 1], mask[:, t * E:(t + 1) * E], m.ones_b[:, 0:1],
                                       start=True, stop=True, skip_group_check=True)
            ins.then_inc(counted, 1)
            pe.wait_ge(laid, 1)
            nc.tensor.matmul(m.bank[1][0:E, 0:1], m.upto[0:E, 0:E], m.blocks_f[0:E, 0:1], start=True, stop=True).then_inc(counted, 1)
            pe.wait_ge(laid, 2)
            nc.tensor.matmul(m.bank[2][0:1, 0:n_blocks], m.ones[0:E, 0:1], m.ended[0:E, 0:n_blocks], start=True, stop=True).then_inc(counted, 1)
            pe.wait_ge(laid, 3)
            for g in range(groups):
                if g >= 2:
                    pe.wait_ge(done, g - 1)
                b = m.bank[4 + g % 2]
                nc.tensor.matmul(b[:, 0:W], m.before_b[:], mask[:, g * W:(g + 1) * W], start=True, stop=False)
                nc.tensor.matmul(b[:, 0:W], m.ones[0:E, :], m.spread[0:E, g * W:(g + 1) * W], start=False, stop=True).then_inc(placed, 1)

        @block.vector
        def _(dve):
            link = Link(dve, m.sem(f"{tag}_step"))
            dve.wait_ge(counted, 1)
            link(nc.vector.tensor_copy(m.count[0:E, :], m.bank[0][0:E, 0:NT]))
            link(nc.vector.tensor_tensor_scan(m.prefix[0:E, :], m.ones_nt[0:E, :], m.count[0:E, :], 0.0, ALU.mult, ALU.add))
            link(nc.vector.tensor_scalar(m.blocks_i[0:E, 0:1], m.prefix[0:E, NT - 1:NT], float(rows - 1), None, ALU.add))
            link(nc.vector.tensor_scalar(m.blocks_i[0:E, 1:2], m.blocks_i[0:E, 0:1], shift, None, ALU.arith_shift_right))
            nc.vector.tensor_copy(m.blocks_f[0:E, 0:1], m.blocks_i[0:E, 1:2]).then_inc(laid, 1)
            dve.wait_ge(counted, 2)
            link(nc.vector.tensor_copy(m.blocks_f[0:E, 1:2], m.bank[1][0:E, 0:1]))
            nc.vector.tensor_scalar(m.ended[0:E, 0:n_blocks], m.iota[0:E, 0:n_blocks], m.blocks_f[0:E, 1:2], None, ALU.is_ge).then_inc(laid, 1)
            link(nc.vector.tensor_tensor(m.blocks_f[0:E, 2:3], m.blocks_f[0:E, 1:2], m.blocks_f[0:E, 0:1], ALU.subtract))
            link(nc.vector.tensor_scalar(m.blocks_f[0:E, 3:4], m.blocks_f[0:E, 2:3], float(rows), None, ALU.mult))
            link(nc.vector.tensor_tensor(m.offset[0:E, :], m.prefix[0:E, :], m.count[0:E, :], ALU.subtract))
            link(nc.vector.tensor_scalar(m.offset[0:E, :], m.offset[0:E, :], m.blocks_f[0:E, 3:4], None, ALU.add))
            nc.vector.tensor_tensor(diag, m.ident[0:E, 0:E].unsqueeze(1).to_broadcast([E, NT, E]),
                                    m.offset[0:E, :].unsqueeze(2).to_broadcast([E, NT, E]), ALU.mult).then_inc(laid, 1)
            dve.wait_ge(counted, 3)
            link(nc.vector.tensor_scalar(m.owner_f[:, 0:n_blocks], m.bank[2][0:1, 0:n_blocks], float(E - 1), None, ALU.min))
            link(nc.vector.tensor_copy(m.owner_i[:, 0:n_blocks], m.owner_f[:, 0:n_blocks]))
            for g in range(groups):
                dve.wait_ge(placed, g + 1)
                nc.vector.tensor_copy(m.place[:, g * W:(g + 1) * W], m.bank[4 + g % 2][:, 0:W]).then_inc(done, 1)
            dve.wait_ge(done, groups)


def pick_positions(nc, m, s, E, link, which, mask):
    NT = s.NT
    n = NT * E
    link(nc.vector.tensor_tensor(m.spread[:, 0:n], mask, m.place[:, 0:n], ALU.mult))
    link(nc.vector.tensor_reduce(m.pos_f[:, which, :], m.spread[:, 0:n].rearrange("p (t e) -> p t e", t=NT), AX, ALU.add))
    link(nc.vector.tensor_copy(m.pos_i[:, which, :], m.pos_f[:, which, :]))


def rule_positions(nc, m, s):
    with nc.Block() as block:

        @block.vector
        def _(dve):
            link = Link(dve, m.sem("rule_pos_step"))
            pick_positions(nc, m, s, s.RULES, link, 0, m.mask[:, 0:s.NT * s.RULES])


def rule_blocks(nc, m, s, ins):
    NT, C = s.NT, s.C
    scattered, gathered = m.sem("rule_scattered"), m.sem("rule_gathered")
    x_in = [m.sem(f"rule_x{k}") for k in range(SLOTS)]
    w_in = [m.sem(f"rule_w{k}") for k in range(SLOTS)]
    y_out = [m.sem(f"rule_y{k}") for k in range(SLOTS)]
    turned, copied, multiplied, kept = (m.sem(f"rule_{x}") for x in ("turned", "copied", "multiplied", "kept"))
    stored, halved = m.sem("rule_stored"), m.sem("rule_halved")
    rules = ins["L0_tok_rule_transform"]
    rows_in, rows_out = m.rows_in.ap(), m.rows_out.ap()
    with nc.Block() as block:

        @block.gpsimd
        def _(pool):
            pool.wait_ge(m.zeroed, 4 * 16)
            for t in range(NT):
                index = bass.IndirectOffsetOnAxis(ap=m.pos_i[:, 0, t:t + 1], axis=0)
                pool.indirect_dma_start(rows_in, index, m.h[:, t, :], None).then_inc(scattered, 16)
            pool.wait_ge(stored, 1)
            for t in range(NT):
                index = bass.IndirectOffsetOnAxis(ap=m.pos_i[:, 0, t:t + 1], axis=0)
                pool.indirect_dma_start(m.h[:, t, :], None, rows_out[0:s.RULE_BLOCKS * s.RULE_ROWS, :], index).then_inc(gathered, 16)
            pool.wait_ge(gathered, 16 * NT)

        @block.sync
        def _(sp):
            sp.wait_ge(scattered, 16 * NT)
            with sp.Fori(0, s.rule_turns) as i:
                for k in range(SLOTS):
                    sp.wait_ge(kept, i * SLOTS + k + 1)
                    sp.dma_start(m.xb[k][:, 0:C], rows_in[bass.ds(i * (SLOTS * P) + k * P, P), :]).then_inc(x_in[k], 16)
                    for half in range(2):
                        e = sp.value_load(m.owner_i[0:1, bass.ds(i * (2 * SLOTS) + 2 * k + half, 1)], min_val=0, max_val=s.RULES - 1)
                        sp.dma_start(m.wa[k][0:C, half * C:(half + 1) * C],
                                     rules[bass.ds(e, 1), :, :].rearrange("a d c -> (a d) c")).then_inc(w_in[k], 16)

        @block.tensor
        def _(pe):
            with pe.Fori(0, s.rule_turns) as i:
                for k in range(SLOTS):
                    pe.wait_ge(x_in[k], i * 16 + 16)
                    pe.wait_ge(kept, i * SLOTS + k + 1)
                    nc.tensor.transpose(m.bank[k][:, 0:P], m.xb[k][:], m.ident[:]).then_inc(turned, 1)
                for k in range(SLOTS):
                    pe.wait_ge(w_in[k], i * 32 + 32)
                    pe.wait_ge(copied, i * SLOTS + k + 1)
                    nc.tensor.matmul(m.bank[4 + k][:, 0:2 * C], m.xT[k][0:C, :], m.wa[k][0:C, :],
                                     start=True, stop=True).then_inc(multiplied, 1)

        @block.vector
        def _(dve):
            with dve.Fori(0, s.rule_turns) as i:
                for k in range(SLOTS):
                    dve.wait_ge(turned, i * SLOTS + k + 1)
                    nc.vector.tensor_copy(m.xT[k][0:C, :], m.bank[k][0:C, 0:P]).then_inc(copied, 1)

        @block.scalar
        def _(act):
            for k in range(SLOTS):
                act.sem_inc(kept, 1)
                act.sem_inc(y_out[k], 16)
            with act.Fori(0, s.rule_turns) as i:
                for k in range(SLOTS):
                    act.wait_ge(multiplied, i * SLOTS + k + 1)
                    act.wait_ge(y_out[k], i * 16 + 16)
                    nc.scalar.copy(m.yb[k][0:C, :], m.bank[4 + k][0:C, 0:C]).then_inc(halved, 1)
                    nc.scalar.copy(m.yb[k][C:P, :], m.bank[4 + k][C:P, C:2 * C]).then_inc(kept, 1)
                act.wait_ge(halved, i * SLOTS + SLOTS)
                for k in range(SLOTS):
                    act.wait_ge(kept, i * SLOTS + SLOTS + k + 1)
                    act.dma_start(rows_out[bass.ds(i * (SLOTS * P) + k * P, P), :], m.yb[k][:]).then_inc(y_out[k], 16)
            for k in range(SLOTS):
                act.wait_ge(y_out[k], 16 * (s.rule_turns + 1))
            act.sem_inc(stored, 1)


def layer_norm(nc, m, s, x, centred, rstd, tag, twice=False):
    NT, C = s.NT, s.C
    ready, rooted = m.sem(f"{tag}_var"), m.sem(f"{tag}_root")
    wide = [P, NT, C]
    with nc.Block() as block:

        @block.vector
        def _(dve):
            link = Link(dve, m.sem(f"{tag}_step"))
            link(nc.vector.tensor_reduce(m.mean[:], x[:], AX, ALU.add))
            link(nc.vector.tensor_scalar(m.mean[:], m.mean[:], 1.0 / C, None, ALU.mult))
            link(nc.vector.tensor_tensor(centred[:], x[:], m.mean[:].unsqueeze(2).to_broadcast(wide), ALU.subtract))
            link(nc.vector.tensor_tensor(m.sq[:], centred[:], centred[:], ALU.mult))
            link(nc.vector.tensor_reduce(m.mean[:], m.sq[:], AX, ALU.add))
            nc.vector.tensor_scalar(m.var[:], m.mean[:], 1.0 / C, EPS, ALU.mult, ALU.add).then_inc(ready, 1)
            dve.wait_ge(rooted, 1)
            link(nc.vector.reciprocal(rstd[:], m.std[:]))
            if twice:
                link(nc.vector.tensor_scalar(m.mean[:], m.mean[:], 1.0 / C, None, ALU.mult))
                link(nc.vector.tensor_tensor(m.mean[:], m.mean[:], rstd[:], ALU.mult))
                link(nc.vector.tensor_tensor(m.mean[:], m.mean[:], rstd[:], ALU.mult))
                nc.vector.tensor_scalar(m.var[:], m.mean[:], EPS, None, ALU.add).then_inc(ready, 1)
                dve.wait_ge(rooted, 2)
                link(nc.vector.reciprocal(m.mean[:], m.std[:]))
                link(nc.vector.tensor_tensor(rstd[:], rstd[:], m.mean[:], ALU.mult))

        @block.scalar
        def _(act):
            for n in range(2 if twice else 1):
                act.wait_ge(ready, n + 1)
                nc.scalar.activation(m.std[:], m.var[:], ACT.Sqrt).then_inc(rooted, 1)


def attention(nc, m, s, layer):
    C, NT = s.C, s.NT
    K = C + 1 if layer == 0 else C
    norm = 1.0 if layer == 0 else 1.0 / float(C) ** 0.5
    tag = f"att{layer}"
    scaled, tA, eA, mQ, eQ, mV, eV, mS, eM, xp, tP, eP, mO, rc, eO = (
        m.sem(f"{tag}_{x}") for x in ("scaled", "turned", "a_copied", "q_made", "q_copied", "v_made", "v_copied",
                                      "scored", "maxed", "exped", "p_turned", "p_copied", "mixed", "recip", "kept"))
    bank = m.bank
    mqk = m.mqk[layer]
    with nc.Block() as block:

        @block.tensor
        def _(pe):
            with pe.Fori(0, s.B // 2) as i:
                n = lambda k: i * 2 + (k + 1)
                for k in range(2):
                    pe.wait_ge(scaled, n(k))
                    pe.wait_ge(eO, n(k))
                    nc.tensor.transpose(bank[k][:, 0:P], m.an[k][:].rearrange("p j c -> p (j c)"), m.ident[:]).then_inc(tA, 1)
                for k in range(2):
                    wait_apart(pe, eA, i * 4 + (2 * k + 2))
                    nc.tensor.matmul(bank[k][0:K, 2 * P:4 * P], mqk[:], m.aT[k][0:K, :], start=True, stop=True).then_inc(mQ, 1)
                    if layer == 0:
                        for j in range(2):
                            ins = nc.tensor.matmul(bank[2 + k][:, j * C:(j + 1) * C], m.aT[k][:, j * P:(j + 1) * P], m.wvp[:],
                                                   start=True, stop=True)
                        ins.then_inc(mV, 1)
                for k in range(2):
                    wait_apart(pe, eQ, n(k))
                    for j in range(2):
                        ins = nc.tensor.matmul(bank[4 + k][:, j * 2 * P:(j + 1) * 2 * P], m.qT[k][0:K, j * P:(j + 1) * P],
                                               m.aT[k][0:K, :], start=True, stop=True)
                    ins.then_inc(mS, 1)
                for k in range(2):
                    pe.wait_ge(xp, n(k))
                    for j in range(2):
                        for c in range(2):
                            ins = nc.tensor.transpose(bank[6 + k][:, c * 2 * P + j * P:c * 2 * P + (j + 1) * P],
                                                      m.pr[k][:, j, c * P:(c + 1) * P], m.ident[:])
                    ins.then_inc(tP, 1)
                for k in range(2):
                    pe.wait_ge(eP, n(k))
                    if layer == 0:
                        pe.wait_ge(eV, n(k))
                    v = m.v[k] if layer == 0 else m.an[k]
                    for j in range(2):
                        for c in range(2):
                            ins = nc.tensor.matmul(bank[2 + k][:, (2 + j) * C:(3 + j) * C], m.pT[k][:, c, j * P:(j + 1) * P],
                                                   v[:, c, :], start=(c == 0), stop=(c == 1))
                    ins.then_inc(mO, 1)

        @block.vector
        def _(dve):
            for k in range(2):
                dve.sem_inc(eO, 1)
            with dve.Fori(0, s.B // 2) as i:
                n = lambda k: i * 2 + (k + 1)
                for k in range(2):
                    dve.wait_ge(eO, n(k))
                    tiles = bass.ds(i * 4 + 2 * k, 2)
                    nc.vector.tensor_tensor(m.an[k][:], m.xc[:, tiles, :], m.rstd[:, tiles].unsqueeze(2).to_broadcast([P, 2, C]),
                                            ALU.mult).then_inc(scaled, 1)
                for k in range(2):
                    dve.wait_ge(mQ, n(k))
                    nc.vector.tensor_copy(m.qT[k][0:K, :], bank[k][0:K, 2 * P:4 * P]).then_inc(eQ, 1)
                for k in range(2):
                    wait_apart(dve, mS, n(k))
                    st = m.stat[k]
                    if layer == 0:
                        for j in range(2):
                            ins = nc.vector.tensor_tensor_reduce(m.sc[k][:, j, :], bank[4 + k][:, j * 2 * P:(j + 1) * 2 * P],
                                                                 m.relbias[:, (1 - j) * P:(3 - j) * P], 1.0, -3.0e38,
                                                                 ALU.add, ALU.max, st[:, j:j + 1])
                        ins.then_inc(eM, 1)
                    else:
                        nc.vector.tensor_reduce(st[:, 0:2], bank[4 + k][:].rearrange("p (j n) -> p j n", j=2), AX, ALU.max).then_inc(eM, 1)
                    dve.wait_ge(eM, i * 4 + 2 * k + 1)
                    nc.vector.tensor_scalar(st[:, 2:4], st[:, 0:2], -norm, None, ALU.mult).then_inc(eM, 1)
                for k in range(2):
                    dve.wait_ge(xp, n(k))
                    nc.vector.reciprocal(m.stat[k][:, 6:8], m.stat[k][:, 4:6]).then_inc(rc, 1)
                    dve.wait_ge(tP, n(k))
                    nc.vector.tensor_copy(m.pT[k][:], bank[6 + k][:].rearrange("p (c n) -> p c n", c=2)).then_inc(eP, 1)
                for k in range(2):
                    dve.wait_ge(mO, n(k))
                    dve.wait_ge(rc, n(k))
                    nc.vector.tensor_tensor(m.msg[:, bass.ds(i * 4 + 2 * k, 2), :],
                                            bank[2 + k][:, 2 * C:4 * C].rearrange("p (j c) -> p j c", j=2),
                                            m.stat[k][:, 6:8].unsqueeze(2).to_broadcast([P, 2, C]), ALU.mult).then_inc(eO, 1)

        @block.scalar
        def _(act):
            with act.Fori(0, s.B // 2) as i:
                n = lambda k: i * 2 + (k + 1)
                for k in range(2):
                    act.wait_ge(tA, n(k))
                    nc.scalar.copy(m.aT[k][0:C, 0:P], bank[k][0:C, 0:P]).then_inc(eA, 1)
                    nc.scalar.copy(m.aT[k][0:C, P:2 * P], bank[k][C:2 * C, 0:P]).then_inc(eA, 1)
                if layer == 0:
                    for k in range(2):
                        act.wait_ge(mV, n(k))
                        nc.scalar.copy(m.v[k][:].rearrange("p j c -> p (j c)"), bank[2 + k][:, 0:2 * C]).then_inc(eV, 1)
                for k in range(2):
                    act.wait_ge(eM, i * 4 + 2 * k + 2)
                    for j in range(2):
                        src = m.sc[k][:, j, :] if layer == 0 else bank[4 + k][:, j * 2 * P:(j + 1) * 2 * P]
                        ins = nc.scalar.activation(m.pr[k][:, j, :], src, ACT.Exp, bias=m.stat[k][:, 2 + j:3 + j], scale=norm,
                                                   accum_out=m.stat[k][:, 4 + j:5 + j])
                    ins.then_inc(xp, 1)


def after_attention0(nc, m, s):
    NT, C = s.NT, s.C
    wide = [P, NT, C]
    with nc.Block() as block:

        @block.vector
        def _(dve):
            link = Link(dve, m.sem("after0_step"))
            link(nc.vector.scalar_tensor_tensor(out=m.msg[:], in0=m.msg[:], scalar=m.scale[:, 0:1],
                                                in1=m.pbias[:].unsqueeze(1).to_broadcast(wide), op0=ALU.mult, op1=ALU.add))
    layer_norm(nc, m, s, m.msg, m.xc, m.rstd, "ln2")
    with nc.Block() as block:

        @block.vector
        def _(dve):
            link = Link(dve, m.sem("after0_step2"))
            link(nc.vector.tensor_tensor(m.xc[:], m.xc[:], m.rstd[:].unsqueeze(2).to_broadcast(wide), ALU.mult))
            link(nc.vector.tensor_tensor(m.xc[:], m.xc[:], m.g2[:].unsqueeze(1).to_broadcast(wide), ALU.mult))
            link(nc.vector.tensor_tensor(m.xc[:], m.xc[:], m.b2ln[:].unsqueeze(1).to_broadcast(wide), ALU.add))
            link(nc.vector.tensor_tensor(m.h[:], m.h[:], m.xc[:], ALU.add))


def turn_tokens(nc, m, s, block, tag, scale_first, dest):
    NT, C = s.NT, s.C
    ready, turned, copied = (m.sem(f"{tag}_{x}") for x in ("ready", "turned", "copied"))

    @block.vector
    def _(dve):
        wide = [P, NT, C]
        nc.vector.tensor_tensor(m.xc[:], m.xc[:], m.rstd[:].unsqueeze(2).to_broadcast(wide), ALU.mult).then_inc(ready, 1)
        for g in range(0, NT // 4, 2):
            dve.wait_ge(turned, g + 1)
            dst, src = dest(g)
            nc.vector.tensor_copy(dst, src).then_inc(copied, 1)

    @block.scalar
    def _(act):
        for g in range(1, NT // 4, 2):
            act.wait_ge(turned, g + 1)
            dst, src = dest(g)
            nc.scalar.copy(dst, src).then_inc(copied, 1)

    @block.tensor
    def _(pe):
        pe.wait_ge(ready, 1)
        for g in range(NT // 4):
            for j in range(4):
                ins = nc.tensor.transpose(m.bank[g][0:C, j * P:(j + 1) * P], m.xc[:, 4 * g + j, :], m.ident[:])
            ins.then_inc(turned, 1)


def lstm_inputs(nc, m, s):
    C = s.C

    def dest(g):
        dst = m.xseq[0:C, 0:s.T].rearrange("c (t b) -> c b t", b=s.B)[:, 2 * g:2 * g + 2, :]
        return dst, m.bank[g][0:C, :].rearrange("c (b t) -> c b t", b=2)

    with nc.Block() as block:
        turn_tokens(nc, m, s, block, "lin", True, dest)


def lstm(nc, m, s):
    C, B, T = s.C, s.B, s.T
    summed, gated, prods, celled, tanned, hidden, saved = (
        m.sem(f"lstm_{x}") for x in ("summed", "gated", "products", "cell", "tanh", "hidden", "saved"))
    turns = s.L // STEPS
    W = 4 * B

    with nc.Block() as block:

        def project(bank, first):
            out = bank[0:C, :].rearrange("p (t q b) -> p t q b", q=4, b=B)
            for q in range(4):
                nc.tensor.matmul(out[:, :, q, :], m.wi[:, q * C:(q + 1) * C], m.xseq[:, first], start=(q == 0),
                                 stop=False, skip_group_check=True)

        @block.tensor
        def _(pe):
            project(m.bank[0], slice(0, HALF * B))
            with pe.Fori(0, turns) as i:
                for k in range(STEPS):
                    bank = m.bank[k // HALF]
                    wait_apart(pe, hidden, i * STEPS + (k + 1))
                    for q in range(4):
                        at = (k % HALF) * W + q * B
                        ins = nc.tensor.matmul(bank[0:C, at:at + B], m.wh[:, q * C:(q + 1) * C], m.ring[:, (k - 1) % STEPS, :],
                                               start=False, stop=True, skip_group_check=True)
                    ins.then_inc(summed, 1)
                    if k % HALF == HALF // 2:
                        nxt = (k // HALF + 1) * HALF * B
                        project(m.bank[1 - k // HALF], bass.ds(i * (STEPS * B) + nxt, HALF * B))

        @block.scalar
        def _(act):
            with act.Fori(0, turns) as i:
                for k in range(STEPS):
                    at = (k % HALF) * W
                    act.wait_ge(summed, i * STEPS + (k + 1))
                    nc.scalar.activation(m.gates[:, k % 2, 1:5, :], m.bank[k // HALF][0:C, at:at + W], ACT.Tanh).then_inc(gated, 1)
                    act.wait_ge(celled, i * STEPS + (k + 1))
                    nc.scalar.activation(m.tanc[:], m.gates[:, (k + 1) % 2, 0, :], ACT.Tanh, scale=0.5).then_inc(tanned, 1)

        @block.vector
        def _(dve):
            dve.sem_inc(hidden, 1)
            with dve.Fori(0, turns) as i:
                for k in range(STEPS):
                    dve.wait_ge(gated, i * STEPS + (k + 1))
                    nc.vector.scalar_tensor_tensor(out=m.prod[:], in0=m.gates[:, k % 2, 2:4, :], scalar=1.0,
                                                   in1=m.gates[:, k % 2, 0:2, :], op0=ALU.add, op1=ALU.mult).then_inc(prods, 1)
                    dve.wait_ge(prods, i * STEPS + (k + 1))
                    nc.vector.scalar_tensor_tensor(out=m.gates[:, (k + 1) % 2, 0, :], in0=m.prod[:, 0, :], scalar=0.5,
                                                   in1=m.prod[:, 1, :], op0=ALU.mult, op1=ALU.add).then_inc(celled, 1)
                    dve.wait_ge(tanned, i * STEPS + (k + 1))
                    if k % HALF == 0:
                        dve.wait_ge(saved, i * 2 + (k // HALF + 1))
                    nc.vector.scalar_tensor_tensor(out=m.ring[:, k, :], in0=m.gates[:, k % 2, 4, :], scalar=1.0,
                                                   in1=m.tanc[:], op0=ALU.add, op1=ALU.mult).then_inc(hidden, 1)

        @block.gpsimd
        def _(pool):
            hist = m.hist[:].rearrange("c (b t) -> c t b", b=B)
            pool.sem_inc(saved, 1)
            pool.sem_inc(saved, 1)
            with pool.Fori(0, turns) as i:
                for half in range(2):
                    pool.wait_ge(hidden, i * STEPS + ((half + 1) * HALF + 1))
                    nc.gpsimd.tensor_copy(hist[:, bass.ds(i * STEPS + half * HALF, HALF), :],
                                          m.ring[:, half * HALF:(half + 1) * HALF, :]).then_inc(saved, 1)


def lstm_output(nc, m, s):
    C, B, T, NT, L = s.C, s.B, s.T, s.NT, s.L
    lined, biased, gated, scanned = (m.sem(f"lout_{x}") for x in ("lined", "biased", "gated", "scanned"))
    turned, added = m.sem("lout_turned"), m.sem("lout_added")
    ready = m.sem("lout_ready")
    chunks = T // 512
    with nc.Block() as block:

        @block.tensor
        def _(pe):
            for i in range(chunks):
                k = i % 2
                if i >= 2:
                    pe.wait_ge(gated, 2 * (i - 1))
                for l in range(2):
                    ins = nc.tensor.matmul(m.bank[2 * k + l][0:C, :], m.wlinb[:, l, :], m.hist[:, i * 512:(i + 1) * 512],
                                           start=True, stop=True)
                ins.then_inc(lined, 1)
            pe.wait_ge(ready, 1)
            for g in range(NT // 8):
                for j in range(8):
                    ins = nc.tensor.transpose(m.bank[4 + g][:, j * C:(j + 1) * C], m.tb[:, (8 * g + j) * P:(8 * g + j + 1) * P],
                                              m.ident[0:C, 0:C])
                ins.then_inc(turned, 1)

        @block.scalar
        def _(act):
            for i in range(chunks):
                k = i % 2
                act.wait_ge(lined, i + 1)
                if i >= 2:
                    act.wait_ge(gated, 2 * (i - 1))
                nc.scalar.activation(m.lg0[k][:], m.bank[2 * k][0:C, :], ACT.Identity, bias=m.blin[:, 0:1]).then_inc(biased, 1)

        @block.vector
        def _(dve):
            link = Link(dve, m.sem("lout_step"))
            for i in range(chunks):
                for k in (i % 2,):
                    now = slice(i * 512, (i + 1) * 512)
                    dve.wait_ge(biased, i + 1)
                    nc.vector.scalar_tensor_tensor(out=m.gt[k][:], in0=m.bank[2 * k + 1][0:C, :], scalar=m.blin[:, 1:2],
                                                   in1=m.lg0[k][:], op0=ALU.add, op1=ALU.is_gt).then_inc(gated, 1)
                    dve.wait_ge(gated, 2 * i + 1)
                    nc.vector.tensor_tensor(m.ta[:, now], m.gt[k][:], m.hist[:, now], ALU.mult).then_inc(gated, 1)
            dve.wait_ge(gated, 2 * chunks)
            link(nc.vector.memset(m.lg0[0][:], 1.0))
            with dve.Fori(0, B) as b:
                nc.vector.tensor_tensor_scan(m.tb[:, bass.ds(b * L, L)], m.lg0[0][:, 0:L], m.ta[:, bass.ds(b * L, L)],
                                             0.0, ALU.mult, ALU.add).then_inc(scanned, 1)
            dve.wait_ge(scanned, B)
            tb3 = m.tb[:].rearrange("c (b t) -> c b t", b=B)
            ta3 = m.ta[:].rearrange("c (b t) -> c b t", b=B)
            link(nc.vector.tensor_tensor(m.ta[:], m.tb[:], m.ta[:], ALU.subtract))
            link(nc.vector.scalar_tensor_tensor(out=m.hist[:], in0=m.ta[:], scalar=m.fwbw[:, 2:3], in1=m.hist[:],
                                                op0=ALU.mult, op1=ALU.add))
            link(nc.vector.tensor_tensor(ta3, tb3, tb3[:, :, L - 1:L].to_broadcast([C, B, L]), ALU.subtract))
            nc.vector.scalar_tensor_tensor(out=m.tb[:], in0=m.ta[:], scalar=m.fwbw[:, 3:4], in1=m.hist[:],
                                           op0=ALU.mult, op1=ALU.add).then_inc(ready, 1)
            for g in range(NT // 8):
                dve.wait_ge(turned, g + 1)
                hg = m.h[:, 8 * g:8 * g + 8, :]
                nc.vector.tensor_tensor(hg, hg, m.bank[4 + g][:].rearrange("p (j c) -> p j c", j=8), ALU.add).then_inc(added, 1)
            dve.wait_ge(added, NT // 8)


def add_messages(nc, m, s):
    with nc.Block() as block:

        @block.vector
        def _(dve):
            link = Link(dve, m.sem("msg_step"))
            link(nc.vector.tensor_tensor(m.h[:], m.h[:], m.msg[:], ALU.add))


def router(nc, m, s):
    NT, C, E, T = s.NT, s.C, s.EXPERTS, s.T
    xT = m.xseq

    def dest(g):
        return xT[0:C, g * 512:(g + 1) * 512], m.bank[g][0:C, :]

    with nc.Block() as block:
        turn_tokens(nc, m, s, block, "rin", True, dest)
    lined, copied, topped, found = (m.sem(f"router_{x}") for x in ("lined", "copied", "topped", "found"))
    difference, exponent = m.sem("router_diff"), m.sem("router_exp")
    with nc.Block() as block:

        @block.tensor
        def _(pe):
            for g in range(NT // 8):
                for j in range(8):
                    t = 8 * g + j
                    ins = nc.tensor.matmul(m.bank[g][:, j * E:(j + 1) * E], xT[:, t * P:(t + 1) * P], m.wr[:], start=True, stop=True)
                ins.then_inc(lined, 1)

        @block.scalar
        def _(act):
            for g in range(NT // 8):
                act.wait_ge(lined, g + 1)
                nc.scalar.copy(m.logits[:, 8 * g:8 * g + 8, :], m.bank[g][:, 0:8 * E].rearrange("p (j e) -> p j e", j=8)).then_inc(copied, 1)
            act.wait_ge(difference, 1)
            nc.scalar.activation(m.gtmp[:, 1, :], m.gtmp[:, 0, :], ACT.Exp).then_inc(exponent, 1)

        @block.vector
        def _(dve):
            link = Link(dve, m.sem("router_step"))
            dve.wait_ge(copied, NT // 8)
            for t in range(NT):
                nc.vector.max(m.top[:, t, :], m.logits[:, t, :]).then_inc(topped, 1)
            for t in range(NT):
                dve.wait_ge(topped, t + 1)
                nc.vector.max_index(m.topi[:, t, :], m.top[:, t, :], m.logits[:, t, :]).then_inc(found, 1)
            dve.wait_ge(found, NT)
            nc.vector.tensor_tensor(m.gtmp[:, 0, :], m.top[:, :, 1], m.top[:, :, 0], ALU.subtract).then_inc(difference, 1)
            link(nc.vector.tensor_copy(m.topf[:], m.topi[:, :, 0:2]))
            shape = [P, NT, E]
            n = NT * E
            for which, dst in ((0, m.first), (1, m.second)):
                link(nc.vector.tensor_tensor(dst[:].rearrange("p (t e) -> p t e", t=NT),
                                             m.topf[:, :, which:which + 1].to_broadcast(shape),
                                             m.iota[:, 0:E].unsqueeze(1).to_broadcast(shape), ALU.is_equal))
            link(nc.vector.tensor_tensor(m.mask[:, 0:n], m.first[:], m.second[:], ALU.add))
            dve.wait_ge(exponent, 1)
            link(nc.vector.tensor_scalar(m.gtmp[:, 2, :], m.gtmp[:, 1, :], 1.0, None, ALU.add))
            link(nc.vector.reciprocal(m.gate[:, 0, :], m.gtmp[:, 2, :]))
            link(nc.vector.tensor_tensor(m.gate[:, 1, :], m.gate[:, 0, :], m.gtmp[:, 1, :], ALU.mult))


def expert_positions(nc, m, s):
    with nc.Block() as block:

        @block.vector
        def _(dve):
            link = Link(dve, m.sem("expert_pos_step"))
            pick_positions(nc, m, s, s.EXPERTS, link, 0, m.first[:])
            pick_positions(nc, m, s, s.EXPERTS, link, 1, m.second[:])


def expert_blocks(nc, m, s, ins):
    NT, C, H = s.NT, s.C, s.HID
    scattered = m.sem("exp_scattered")
    x_in = [m.sem(f"exp_x{k}") for k in range(SLOTS)]
    w_in = [m.sem(f"exp_w{k}") for k in range(SLOTS)]
    y_out = [m.sem(f"exp_y{k}") for k in range(SLOTS)]
    turned, copied, up, active, down, kept = (m.sem(f"exp_{x}") for x in ("turned", "copied", "up", "active", "down", "kept"))
    w1, b1, w2, b2 = (ins[f"L1_ffn_{x}"] for x in ("W1", "b1", "W2", "b2"))
    rows_in, rows_out = m.rows_in.ap(), m.rows_out.ap()
    with nc.Block() as block:

        @block.gpsimd
        def _(pool):
            for which in range(2):
                for t in range(NT):
                    index = bass.IndirectOffsetOnAxis(ap=m.pos_i[:, which, t:t + 1], axis=0)
                    pool.indirect_dma_start(rows_in, index, m.xc[:, t, :], None).then_inc(scattered, 16)

        @block.sync
        def _(sp):
            sp.wait_ge(scattered, 2 * 16 * NT)
            with sp.Fori(0, s.expert_turns) as i:
                for k in range(SLOTS):
                    sp.wait_ge(kept, i * SLOTS + k + 1)
                    sp.dma_start(m.xb[k][:, 0:C], rows_in[bass.ds(i * (SLOTS * P) + k * P, P), :]).then_inc(x_in[k], 16)
                    e = sp.value_load(m.owner_i[0:1, bass.ds(i * SLOTS + k, 1)], min_val=0, max_val=s.EXPERTS - 1)
                    sp.dma_start(m.wa[k][0:C, :], w1[bass.ds(e, 1), :, :].rearrange("a d c -> (a d) c")).then_inc(w_in[k], 16)
                    sp.dma_start(m.wa[k][C:C + 1, :], b1[bass.ds(e, 1), :]).then_inc(w_in[k], 16)
                    sp.dma_start(m.wb[k][:], w2[bass.ds(e, 1), :, :].rearrange("a d c -> (a d) c")).then_inc(w_in[k], 16)
                    sp.dma_start(m.b2[k][:], b2[bass.ds(e, 1), :]).then_inc(w_in[k], 16)

        @block.tensor
        def _(pe):
            with pe.Fori(0, s.expert_turns) as i:
                n = lambda k: i * SLOTS + (k + 1)
                for k in range(SLOTS):
                    pe.wait_ge(x_in[k], i * 16 + 16)
                    pe.wait_ge(kept, n(k))
                    nc.tensor.transpose(m.bank[k][:, 0:P], m.xb[k][:], m.ident[:]).then_inc(turned, 1)
                for k in range(SLOTS):
                    pe.wait_ge(w_in[k], i * 64 + 64)
                    pe.wait_ge(copied, n(k))
                    nc.tensor.matmul(m.bank[k][:, P:2 * P], m.wa[k][:], m.xT[k][:], start=True, stop=True).then_inc(up, 1)
                for k in range(SLOTS):
                    pe.wait_ge(active, n(k))
                    nc.tensor.matmul(m.bank[4 + k][:, 0:C], m.hT[k][:], m.wb[k][:], start=True, stop=False)
                    nc.tensor.matmul(m.bank[4 + k][:, 0:C], m.ones[0:1, :], m.b2[k][:], start=False, stop=True).then_inc(down, 1)

        @block.vector
        def _(dve):
            with dve.Fori(0, s.expert_turns) as i:
                n = lambda k: i * SLOTS + (k + 1)
                for k in range(SLOTS):
                    dve.wait_ge(turned, n(k))
                    nc.vector.tensor_copy(m.xT[k][0:C, :], m.bank[k][0:C, 0:P]).then_inc(copied, 1)
                for k in range(SLOTS):
                    dve.wait_ge(up, n(k))
                    nc.vector.tensor_scalar(m.hT[k][:], m.bank[k][:, P:2 * P], 0.0, None, ALU.max).then_inc(active, 1)

        @block.scalar
        def _(act):
            for k in range(SLOTS):
                act.sem_inc(kept, 1)
                act.sem_inc(y_out[k], 16)
            with act.Fori(0, s.expert_turns) as i:
                for k in range(SLOTS):
                    act.wait_ge(down, i * SLOTS + (k + 1))
                    act.wait_ge(y_out[k], i * 16 + 16)
                    nc.scalar.copy(m.yb[k][:], m.bank[4 + k][:, 0:C]).then_inc(kept, 1)
                for k in range(SLOTS):
                    act.wait_ge(kept, i * SLOTS + (SLOTS + k + 1))
                    act.dma_start(rows_out[bass.ds(i * (SLOTS * P) + k * P, P), :], m.yb[k][:]).then_inc(y_out[k], 16)
            for k in range(SLOTS):
                act.wait_ge(y_out[k], 16 * (s.expert_turns + 1))


def combine(nc, m, s, out):
    NT, C = s.NT, s.C
    gathered, summed, stored = m.sem("comb_gathered"), m.sem("comb_summed"), m.sem("comb_stored")
    wide = [P, NT, C]
    ys = (m.msg, m.sq)
    with nc.Block() as block:

        @block.gpsimd
        def _(pool):
            for which in range(2):
                for t in range(NT):
                    index = bass.IndirectOffsetOnAxis(ap=m.pos_i[:, which, t:t + 1], axis=0)
                    pool.indirect_dma_start(ys[which][:, t, :], None, m.rows_out.ap()[0:s.EXPERT_BLOCKS * P, :], index).then_inc(gathered, 16)

        @block.vector
        def _(dve):
            link = Link(dve, m.sem("comb_step"))
            dve.wait_ge(gathered, 2 * 16 * NT)
            for which in range(2):
                y = ys[which]
                link(nc.vector.tensor_tensor(y[:], y[:], m.gate[:, which, :].unsqueeze(2).to_broadcast(wide), ALU.mult))
                ins = nc.vector.tensor_tensor(m.h[:], m.h[:], y[:], ALU.add)
                if which == 0:
                    link(ins)
            ins.then_inc(summed, 1)

        @block.sync
        def _(sp):
            sp.wait_ge(summed, 1)
            sp.dma_start(out.rearrange("b (h p) c -> p (b h) c", p=P), m.h[:]).then_inc(stored, 16)
            sp.wait_ge(stored, 16)


_INS = ["x", "L0_tok_base_embeddings", "L0_tok_rule_transform", "L0_tok_token_rules", "L0_attn_ln1_g", "L0_attn_ln1_b",
        "L0_attn_qkv_w", "L0_attn_qkv_b", "L0_attn_bias_table", "L0_attn_scale", "L0_attn_proj_w", "L0_attn_proj_b",
        "L0_attn_ln2_g", "L0_attn_ln2_b", "L0_ffn_W_ih", "L0_ffn_W_hh", "L0_ffn_b_ih", "L0_ffn_b_hh", "L0_ffn_W_lin",
        "L0_ffn_b_lin", "L0_ffn_fw_att", "L0_ffn_bw_att", "L1_attn_W", "L1_ffn_Wr", "L1_ffn_br", "L1_ffn_W1", "L1_ffn_b1",
        "L1_ffn_W2", "L1_ffn_b2"]


def kernel(**inputs):
    import numpy as _np
    import concourse.bacc as _bacc
    from concourse.bass_utils import run_bass_kernel_spmd as _run

    nc = _bacc.Bacc("TRN2", target_bir_lowering=False, num_devices=1)
    arrays, args = {}, {}
    for name in _INS:
        a = _np.ascontiguousarray(inputs[name])
        if a.ndim == 0:
            a = a.reshape(1)
        arrays[f"in_{name}"] = a
        args[name] = nc.dram_tensor(f"in_{name}", a.shape, mybir.dt.from_np(a.dtype), kind="ExternalInput").ap()
    shape = tuple(inputs["x"].shape) + (inputs["L0_tok_base_embeddings"].shape[1],)
    result = nc.dram_tensor("result", shape, F32, kind="ExternalOutput").ap()
    tower(nc, args, result)
    r = _run(nc, [arrays], core_ids=[0])
    return r.results[0]["result"]
```

```python
from contextlib import ExitStack

import concourse.bass as bass
from concourse import mybir

P = 128
ALU = mybir.AluOpType
ACT = mybir.ActivationFunctionType
AX = mybir.AxisListType.X
F32 = mybir.dt.float32
BF16 = mybir.dt.bfloat16
I32 = mybir.dt.int32
U32 = mybir.dt.uint32

EPS = 1e-5
TURN = 4
STEPS = 32
AHEAD = 8
RING = 2 * AHEAD
WARMERS = 4


def col(ap):
    return ap.rearrange("(c a) -> c a", a=1)


def row(ap):
    return ap.rearrange("(a c) -> a c", a=1)


def view(ap, offset, pattern):
    return bass.AP(tensor=ap.tensor, offset=ap.offset + offset, ap=pattern)


class Link:

    def __init__(self, engine, semaphore):
        self.engine, self.semaphore, self.count = engine, semaphore, 0

    def __call__(self, instruction):
        self.count += 1
        instruction.then_inc(self.semaphore, 1)
        self.engine.wait_ge(self.semaphore, self.count)


def wait_apart(engine, semaphore, value):
    engine.wait_ge(semaphore, value)
    engine.nop(nofuse=True)


def load_owners(nc, engine, m, first, count, choices):
    _, owners = nc.values_load_multi_w_load_instructions(
        m.owner_i[0:1, bass.ds(first, count)], engines=(engine,), min_val=0, max_val=choices - 1,
        skip_runtime_bounds_check_because="route() clamps the owners to the last choice")
    return owners


class Shapes:
    def __init__(self, x, base, rules, rule_of, bias_table, w1, w2):
        self.B, self.L = x.shape
        self.T = self.B * self.L
        self.NT = self.T // P
        self.VOCAB, self.C = base.shape
        self.RULES = rules.shape[0]
        self.EXPERTS, _, self.HID = w1.shape
        assert self.C == 64 and self.L == 2 * P and self.HID == P and self.NT == 32
        self.RULE_ROWS = 64
        rule_blocks = (self.T + self.RULES * (self.RULE_ROWS - 1)) // self.RULE_ROWS
        expert_blocks = (2 * self.T + self.EXPERTS * (P - 1)) // P
        self.rule_turns = even_turns(rule_blocks * self.RULE_ROWS)
        self.expert_turns = even_turns(expert_blocks * P)
        self.TURN_ROWS = TURN * P
        self.ROWS = (max(self.rule_turns, self.expert_turns) + 2) * self.TURN_ROWS
        self.RULE_BLOCKS = self.rule_turns * self.TURN_ROWS // self.RULE_ROWS
        self.EXPERT_BLOCKS = (self.expert_turns + 2) * TURN


def even_turns(rows):
    return 2 * -(-rows // (2 * TURN * P))


def tower(nc, ins, out):
    s = Shapes(ins["x"], ins["L0_tok_base_embeddings"], ins["L0_tok_rule_transform"],
               ins["L0_tok_token_rules"], ins["L0_attn_bias_table"], ins["L1_ffn_W1"], ins["L1_ffn_W2"])
    with ExitStack() as ctx:
        m = Memory(nc, ctx, s)
        constants_and_ids(nc, m, s, ins)
        prepare_weights(nc, m, s, ins)
        gather_tokens(nc, m, s, ins)
        one_hot_rules(nc, m, s)
        route(nc, m, s, s.RULES, s.RULE_ROWS, s.RULE_BLOCKS, "rule")
        rule_positions(nc, m, s)
        rule_blocks(nc, m, s, ins)
        layer_norm(nc, m, s, m.h, m.xc, m.rstd, "ln_attn0", twice=True)
        attention(nc, m, s, ins, 0)
        after_attention0(nc, m, s)
        layer_norm(nc, m, s, m.h, m.xc, m.rstd, "ln_lstm")
        lstm_inputs(nc, m, s)
        lstm(nc, m, s)
        lstm_output(nc, m, s)
        layer_norm(nc, m, s, m.h, m.xc, m.rstd, "ln_attn1")
        attention(nc, m, s, ins, 1)
        add_messages(nc, m, s)
        layer_norm(nc, m, s, m.h, m.xc, m.rstd, "ln_moe")
        router(nc, m, s)
        route(nc, m, s, s.EXPERTS, P, s.EXPERT_BLOCKS, "expert")
        expert_positions(nc, m, s)
        expert_blocks(nc, m, s, ins)
        combine(nc, m, s, out)


class Memory:

    def __init__(self, nc, ctx, s):
        self.nc, self.ctx = nc, ctx

        def sb(name, shape, dt=F32):
            return ctx.enter_context(nc.sbuf_tensor(name, shape, dt))

        NT, C, T, B = s.NT, s.C, s.T, s.B
        self.rows_in = nc.dram_tensor("rows_in", [s.ROWS, C], F32)
        self.rows_out = nc.dram_tensor("rows_out", [s.ROWS, C], F32)
        self.bank = [ctx.enter_context(nc.psum_tensor(f"bank{i}", [P, 512], F32)) for i in range(8)]
        self.ident = sb("ident", [P, P])
        self.anti = sb("anti", [P, P])
        self.upto = sb("upto", [P, P])
        self.ones = sb("ones", [P, P])
        self.ones_b = sb("ones_b", [P, P], BF16)
        self.before_b = sb("before_b", [P, P], BF16)
        self.iota = sb("iota", [P, 256])
        self.ids = sb("ids", [NT, P], I32)
        self.ids_f = sb("ids_f", [NT, P])
        self.ids_neg = sb("ids_neg", [NT, P])
        self.id_col = sb("id_col", [P, NT], I32)
        self.rule_i = sb("rule_i", [P, NT], I32)
        self.rule_f = sb("rule_f", [P, NT])
        W = max(NT * s.RULES, T)
        self.mask = sb("mask", [P, NT * s.RULES], BF16)
        self.first = sb("first", [P, NT * 64], BF16)
        self.second = sb("second", [P, NT * 64], BF16)
        self.spread = sb("spread", [P, W])
        self.place = sb("place", [P, W])
        self.count = sb("count", [P, NT])
        self.prefix = sb("prefix", [P, NT])
        self.ones_nt = sb("ones_nt", [P, NT])
        self.blocks_f = sb("blocks_f", [P, 4])
        self.blocks_i = sb("blocks_i", [P, 2], I32)
        self.offset = sb("offset", [P, NT])
        self.ended = sb("ended", [P, 256])
        self.owner_f = sb("owner_f", [1, 256])
        self.owner_i = sb("owner_i", [1, 256], I32)
        self.pos_f = sb("pos_f", [P, 2, NT])
        self.pos_i = sb("pos_i", [P, 2, NT], I32)
        self.h = sb("h", [P, NT, C])
        self.xc = sb("xc", [P, NT, C])
        self.sq = sb("sq", [P, NT, C])
        self.msg = sb("msg", [P, NT, C])
        self.mean = sb("mean", [P, NT])
        self.var = sb("var", [P, NT])
        self.std = sb("std", [P, NT])
        self.rstd = sb("rstd", [P, NT])
        self.xb = [sb(f"xb{k}", [P, TURN, C]) for k in range(2)]
        self.xT = [sb(f"xT{k}", [C + 1, TURN, P]) for k in range(2)]
        self.w1 = [sb(f"w1_{k}", [C + 1, TURN, P]) for k in range(2)]
        self.hT = [sb(f"hT{k}", [P, TURN, P]) for k in range(2)]
        self.yb = [sb(f"yb{k}", [P, TURN, C]) for k in range(2)]
        late = sb("late", [P, s.EXPERTS * s.HID])
        self.rules = late[0:C, 0:s.RULES * C].rearrange("d (r c) -> d r c", c=C)
        self.hist = late[0:C, 0:T]
        self.lg0 = [late[0:C, T + 512 * k:T + 512 * (k + 1)] for k in range(2)]
        self.gt = [late[0:C, T + 512 * (2 + k):T + 512 * (3 + k)] for k in range(2)]
        self.w1_all = late[0:C + 1, :].rearrange("d (e h) -> d e h", h=s.HID)
        self.w2_all = sb("w2_all", [P, s.EXPERTS, C])
        self.b2_all = sb("b2_all", [s.EXPERTS, C])
        self.gT = [sb(f"gT{k}", [s.EXPERTS, 4 * P]) for k in range(2)]
        self.qkv = sb("qkv", [C + 1, 3 * C])
        self.fold = sb("fold", [C + 1, C + 1])
        self.g1 = sb("g1", [C, 1])
        self.b1 = sb("b1", [C, 1])
        self.wp = sb("wp", [C, C])
        self.qkvT = [sb(f"qkvT{k}", [C, C + 1]) for k in range(3)]
        self.mqk = [sb("mqk0", [C + 1, C + 1]), sb("mqk1", [C, C])]
        self.wvp = sb("wvp", [C + 1, C])
        self.hankel = sb("hankel", [P, 3 * P])
        self.relbias = sb("relbias", [P, 3 * P])
        self.scale = sb("scale", [P, 1])
        self.pbias = sb("pbias", [P, C])
        self.g2 = sb("g2", [P, C])
        self.b2ln = sb("b2ln", [P, C])
        self.an = [sb(f"an{k}", [P, 2, C]) for k in range(2)]
        self.aT = [sb(f"aT{k}", [C + 1, 2 * P]) for k in range(2)]
        self.qT = [sb(f"qT{k}", [C + 1, 2 * P]) for k in range(2)]
        self.v = [sb(f"v{k}", [P, 2, C]) for k in range(2)]
        self.pr = [sb(f"pr{k}", [P, 2, 2 * P]) for k in range(2)]
        self.pT = [sb(f"pT{k}", [P, 2, 2 * P]) for k in range(2)]
        self.stat = [sb(f"stat{k}", [P, 8]) for k in range(2)]
        self.wraw = [sb(f"wraw{k}", [P, 2, C]) for k in range(2)]
        self.wi = sb("wi", [C + 1, 4 * C])
        self.wh = sb("wh", [P, 4 * C])
        self.bsum = sb("bsum", [C + 1, 2, 4 * C])
        self.wlin = sb("wlin", [C, 2])
        self.wlinb = sb("wlinb", [C, 2, C])
        self.blin = sb("blin", [C, 2])
        self.fwbw = sb("fwbw", [C, 4])
        self.xseq = sb("xseq", [C + 1, T + AHEAD * B])
        self.ring = sb("ring", [P, RING, B])
        self.forget = sb("forget", [C, B])
        self.emit = sb("emit", [C, B])
        self.factors = sb("factors", [C, B, 2])
        self.terms = sb("terms", [C, B, 2])
        self.cells = sb("cells", [C, B, 2])
        self.tanc = sb("tanc", [C, B])
        self.ta, self.tb = self.place[0:C, 0:T], self.spread[0:C, 0:T]
        self.wr = sb("wr", [C + 1, s.EXPERTS])
        self.logits = self.place[:, 0:NT * s.EXPERTS].rearrange("p (t e) -> p t e", t=NT)
        self.top = sb("top", [P, NT, 8])
        self.topi = sb("topi", [P, NT, 8], U32)
        self.topf = sb("topf", [P, NT, 2])
        self.gate = sb("gate", [P, 2, NT])
        self.gtmp = sb("gtmp", [P, 3, NT])
        self.zeroed = self.sem("zeroed")
        self.loaded_rules = self.sem("loaded_rules")
        self.loaded_experts = self.sem("loaded_experts")
        self.loaded_w = self.sem("loaded_w")

    def sem(self, name):
        return self.ctx.enter_context(self.nc.semaphore(name))


def constants_and_ids(nc, m, s, ins):
    loaded = m.sem("ids_loaded")
    made, built, filled = m.sem("const_made"), m.sem("const_built"), m.sem("const_filled")
    turned, step = m.sem("ids_turned"), m.sem("ids_step")
    with nc.Block() as block:

        @block.gpsimd
        def _(pool):
            nc.gpsimd.memset(m.ident[:], 0.0).then_inc(made, 1)
            nc.gpsimd.memset(m.anti[:], 0.0).then_inc(made, 1)
            nc.gpsimd.memset(m.upto[:], 1.0).then_inc(made, 1)
            nc.gpsimd.memset(m.before_b[:], 1.0).then_inc(made, 1)
            pool.wait_ge(made, 4)
            for mat, cmp, fill, base, mult, step_ in (
                    (m.ident, ALU.not_equal, 1.0, 0, 1, -1), (m.anti, ALU.not_equal, 1.0, -(P - 1), 1, 1),
                    (m.upto, ALU.is_ge, 0.0, 0, -1, 1), (m.before_b, ALU.is_gt, 0.0, 0, -1, 1)):
                nc.gpsimd.affine_select(out=mat[:], in_=mat[:], compare_op=cmp, fill=fill, base=base,
                                        pattern=[[step_, P]], channel_multiplier=mult).then_inc(built, 1)
            nc.gpsimd.iota(m.iota[:], pattern=[[1, 256]], base=0, channel_multiplier=0,
                           allow_small_or_imprecise_dtypes=True).then_inc(built, 1)

        @block.sync
        def _(sp):
            sp.dma_start(m.ids[:], ins["x"].rearrange("b (h p) -> (b h) p", p=P)).then_inc(loaded, 16)
            loads = [(m.qkv[0:s.C, :], ins["L0_attn_qkv_w"]), (m.qkv[s.C:s.C + 1, :], row(ins["L0_attn_qkv_b"])),
                     (m.wp[:], ins["L0_attn_proj_w"]), (m.mqk[1][:], ins["L1_attn_W"]),
                     (m.g1[:], col(ins["L0_attn_ln1_g"])), (m.b1[:], col(ins["L0_attn_ln1_b"])),
                     (m.hankel[:], view(ins["L0_attn_bias_table"], 0, [[1, P], [1, 3 * P]])),
                     (m.scale[:], view(ins["L0_attn_scale"], 0, [[0, P], [1, 1]])),
                     (m.pbias[:], view(ins["L0_attn_proj_b"], 0, [[0, P], [1, s.C]])),
                     (m.g2[:], view(ins["L0_attn_ln2_g"], 0, [[0, P], [1, s.C]])),
                     (m.b2ln[:], view(ins["L0_attn_ln2_b"], 0, [[0, P], [1, s.C]])),
                     (m.wraw[0][:], ins["L0_ffn_W_ih"].rearrange("(k p) c -> p k c", p=P)),
                     (m.wraw[1][:], ins["L0_ffn_W_hh"].rearrange("(k p) c -> p k c", p=P)),
                     (m.bsum[s.C:s.C + 1, 0, :], row(ins["L0_ffn_b_ih"])),
                     (m.bsum[s.C:s.C + 1, 1, :], row(ins["L0_ffn_b_hh"])),
                     (m.blin[:], view(ins["L0_ffn_b_lin"], 0, [[0, s.C], [1, 2]])),
                     (m.wlin[:, 0:1], view(ins["L0_ffn_W_lin"], 0, [[1, s.C], [1, 1]])),
                     (m.wlin[:, 1:2], view(ins["L0_ffn_W_lin"], s.C, [[1, s.C], [1, 1]])),
                     (m.fwbw[:, 0:1], view(ins["L0_ffn_fw_att"], 0, [[1, s.C], [1, 1]])),
                     (m.fwbw[:, 1:2], view(ins["L0_ffn_bw_att"], 0, [[1, s.C], [1, 1]])),
                     (m.wr[0:s.C, :], ins["L1_ffn_Wr"]), (m.wr[s.C:s.C + 1, :], row(ins["L1_ffn_br"]))]
            for dst, src in loads:
                sp.dma_start(dst, src).then_inc(m.loaded_w, 16)
            m.n_loads = len(loads)
            sp.dma_start(m.rules[:], ins["L0_tok_rule_transform"].rearrange("r d c -> d r c")).then_inc(m.loaded_rules, 16)
            sp.dma_start(m.w2_all[:], ins["L1_ffn_W2"].rearrange("e h c -> h e c")).then_inc(m.loaded_experts, 16)
            sp.dma_start(m.b2_all[:], ins["L1_ffn_b2"]).then_inc(m.loaded_experts, 16)

        @block.vector
        def _(dve):
            nc.vector.memset(m.place[:], 0.0).then_inc(filled, 1)
            nc.vector.memset(m.ones[:], 1.0).then_inc(filled, 1)
            nc.vector.memset(m.ones_b[:], 1.0).then_inc(filled, 1)
            nc.vector.memset(m.ones_nt[:], 1.0).then_inc(filled, 1)
            for k in range(2):
                nc.vector.memset(m.aT[k][s.C:s.C + 1, :], 1.0).then_inc(filled, 1)
            for k in range(2):
                nc.vector.memset(m.xT[k][s.C:s.C + 1, :, :], 1.0).then_inc(filled, 1)
            nc.vector.memset(m.xseq[:], 1.0).then_inc(filled, 1)
            nc.vector.memset(m.factors[:], 0.0).then_inc(filled, 1)
            nc.vector.memset(m.cells[:], 0.0).then_inc(filled, 1)
            nc.vector.memset(m.wh[s.C:P, :], 0.0).then_inc(filled, 1)
            nc.vector.memset(m.ring[:], 0.0).then_inc(filled, 1)
            link = Link(dve, step)
            dve.wait_ge(loaded, 16)
            link(nc.vector.tensor_copy(m.ids_f[:], m.ids[:]))
            link(nc.vector.tensor_scalar(m.ids_neg[:], m.ids_f[:], 0.0, float(s.VOCAB), ALU.is_lt, ALU.mult))
            link(nc.vector.tensor_tensor(m.ids_f[:], m.ids_f[:], m.ids_neg[:], ALU.add))
            link(nc.vector.tensor_scalar(m.ids_f[:], m.ids_f[:], 0.0, float(s.VOCAB - 1), ALU.max, ALU.min))
            dve.wait_ge(turned, 1)
            nc.vector.tensor_copy(m.id_col[:], m.bank[0][:, 0:s.NT]).then_inc(turned, 1)

        @block.tensor
        def _(pe):
            pe.wait_ge(step, 4)
            pe.wait_ge(built, 5)
            nc.tensor.transpose(m.bank[0][:, 0:s.NT], m.ids_f[:], m.ident[0:s.NT, 0:s.NT]).then_inc(turned, 1)

        @block.scalar
        def _(act):
            act.wait_ge(filled, 1)
            quarters = m.rows_in.ap().rearrange("(q p r) c -> q p (r c)", p=P, q=4)
            for q in range(4):
                act.dma_start(quarters[q], m.place[:, 0:s.ROWS * s.C // P // 4]).then_inc(m.zeroed, 16)


def prepare_weights(nc, m, s, ins):
    pe_done, cp = m.sem("prep_product"), m.sem("prep_copied")
    C = s.C
    bank = m.bank
    with nc.Block() as block:

        @block.tensor
        def _(pe):
            pe.wait_ge(m.loaded_w, 16 * m.n_loads)
            nc.tensor.matmul(bank[1][:, 0:3 * P], m.anti[:], m.hankel[:], start=True, stop=True).then_inc(pe_done, 1)
            for w in range(2):
                for k in range(2):
                    nc.tensor.transpose(bank[2 + w][0:C, k * P:(k + 1) * P], m.wraw[w][:, k, :], m.ident[:]).then_inc(pe_done, 1)
            pe.wait_ge(cp, 1)
            for k in range(3):
                nc.tensor.matmul(bank[4][0:C, k * 65:(k + 1) * 65], m.qkv[:, k * C:(k + 1) * C], m.fold[:],
                                 start=True, stop=True, skip_group_check=True).then_inc(pe_done, 1)
            pe.wait_ge(cp, 2)
            nc.tensor.matmul(bank[5][0:C + 1, 0:C + 1], m.qkvT[0][:], m.qkvT[1][:], start=True, stop=True).then_inc(pe_done, 1)
            nc.tensor.matmul(bank[6][0:C + 1, 0:C], m.qkvT[2][:], m.wp[:], start=True, stop=True).then_inc(pe_done, 1)

        @block.vector
        def _(dve):
            link = Link(dve, m.sem("prep_step"))
            dve.wait_ge(m.loaded_w, 16 * m.n_loads)
            link(nc.vector.tensor_copy(m.fold[C:C + 1, :], m.ident[C:C + 1, 0:C + 1]))
            link(nc.vector.tensor_scalar(m.fold[0:C, 0:C], m.ident[0:C, 0:C], m.g1[:, 0:1], None, ALU.mult))
            nc.vector.tensor_copy(m.fold[0:C, C:C + 1], m.b1[:]).then_inc(cp, 1)
            dve.wait_ge(pe_done, 1)
            link(nc.vector.tensor_copy(m.relbias[:], bank[1][:, 0:3 * P]))
            dve.wait_ge(pe_done, 8)
            for k in range(3):
                ins_ = nc.vector.tensor_copy(m.qkvT[k][:], bank[4][0:C, k * 65:(k + 1) * 65])
                if k < 2:
                    link(ins_)
            ins_.then_inc(cp, 1)
            link(nc.vector.tensor_tensor(m.bsum[C:C + 1, 0, :], m.bsum[C:C + 1, 0, :], m.bsum[C:C + 1, 1, :], ALU.add))
            for q, r in enumerate((1, 0, 2, 3)):
                link(nc.vector.tensor_copy(m.wi[0:C, q * C:(q + 1) * C], bank[2][0:C, r * C:(r + 1) * C]))
                link(nc.vector.tensor_copy(m.wh[0:C, q * C:(q + 1) * C], bank[3][0:C, r * C:(r + 1) * C]))
                link(nc.vector.tensor_copy(m.wi[C:C + 1, q * C:(q + 1) * C], m.bsum[C:C + 1, 0, r * C:(r + 1) * C]))
            for l in range(2):
                link(nc.vector.tensor_scalar(m.wlinb[:, l, :], m.ones[0:C, 0:C], m.wlin[:, l:l + 1], 0.5, ALU.mult, ALU.mult))
            link(nc.vector.tensor_scalar(m.fwbw[:, 2:3], m.fwbw[:, 0:1], 0.5, None, ALU.mult))
            link(nc.vector.tensor_scalar(m.fwbw[:, 3:4], m.fwbw[:, 1:2], -0.5, None, ALU.mult))
            dve.wait_ge(pe_done, 10)
            link(nc.vector.tensor_copy(m.mqk[0][:], bank[5][0:C + 1, 0:C + 1]))
            link(nc.vector.tensor_copy(m.wvp[:], bank[6][0:C + 1, 0:C]))


def gather_tokens(nc, m, s, ins):
    got = m.sem("tokens_gathered")
    table = ins["L0_tok_base_embeddings"]
    rule_of = col(ins["L0_tok_token_rules"])
    with nc.Block() as block:

        @block.gpsimd
        def _(pool):
            for t in range(s.NT):
                index = bass.IndirectOffsetOnAxis(ap=m.id_col[:, t:t + 1], axis=0)
                pool.indirect_dma_start(m.rule_i[:, t:t + 1], None, rule_of, index).then_inc(got, 16)
            for t in range(s.NT):
                index = bass.IndirectOffsetOnAxis(ap=m.id_col[:, t:t + 1], axis=0)
                pool.indirect_dma_start(m.h[:, t, :], None, table, index).then_inc(got, 16)
            pool.wait_ge(got, 2 * 16 * s.NT)


def one_hot_rules(nc, m, s):
    with nc.Block() as block:

        @block.vector
        def _(dve):
            link = Link(dve, m.sem("one_hot_step"))
            link(nc.vector.tensor_copy(m.rule_f[:], m.rule_i[:]))
            shape = [P, s.NT, s.RULES]
            link(nc.vector.tensor_tensor(
                m.mask[:, 0:s.NT * s.RULES].rearrange("p (t r) -> p t r", t=s.NT),
                m.rule_f[:].unsqueeze(2).to_broadcast(shape),
                m.iota[:, 0:s.RULES].unsqueeze(1).to_broadcast(shape), ALU.is_equal))


def route(nc, m, s, E, rows, n_blocks, tag):
    NT = s.NT
    counted, laid, placed, done = (m.sem(f"{tag}_{x}") for x in ("counted", "laid", "placed", "placed_read"))
    group = 512 // E if 512 // E < 8 else 8
    while NT % group:
        group -= 1
    groups = NT // group
    W = group * E
    mask = m.mask[:, 0:NT * E]
    diag = m.spread[0:E, 0:NT * E].rearrange("e (t f) -> e t f", t=NT)
    shift = rows.bit_length() - 1
    with nc.Block() as block:

        @block.tensor
        def _(pe):
            for t in range(NT):
                ins = nc.tensor.matmul(m.bank[0][0:E, t:t + 1], mask[:, t * E:(t + 1) * E], m.ones_b[:, 0:1],
                                       start=True, stop=True, skip_group_check=True)
            ins.then_inc(counted, 1)
            pe.wait_ge(laid, 1)
            nc.tensor.matmul(m.bank[1][0:E, 0:1], m.upto[0:E, 0:E], m.blocks_f[0:E, 0:1], start=True, stop=True).then_inc(counted, 1)
            pe.wait_ge(laid, 2)
            nc.tensor.matmul(m.bank[2][0:1, 0:n_blocks], m.ones[0:E, 0:1], m.ended[0:E, 0:n_blocks], start=True, stop=True).then_inc(counted, 1)
            pe.wait_ge(laid, 3)
            for g in range(groups):
                if g >= 2:
                    pe.wait_ge(done, g - 1)
                b = m.bank[4 + g % 2]
                nc.tensor.matmul(b[:, 0:W], m.before_b[:], mask[:, g * W:(g + 1) * W], start=True, stop=False)
                nc.tensor.matmul(b[:, 0:W], m.ones[0:E, :], m.spread[0:E, g * W:(g + 1) * W], start=False, stop=True).then_inc(placed, 1)

        @block.vector
        def _(dve):
            link = Link(dve, m.sem(f"{tag}_step"))
            dve.wait_ge(counted, 1)
            link(nc.vector.tensor_copy(m.count[0:E, :], m.bank[0][0:E, 0:NT]))
            link(nc.vector.tensor_tensor_scan(m.prefix[0:E, :], m.ones_nt[0:E, :], m.count[0:E, :], 0.0, ALU.mult, ALU.add))
            link(nc.vector.tensor_scalar(m.blocks_i[0:E, 0:1], m.prefix[0:E, NT - 1:NT], float(rows - 1), None, ALU.add))
            link(nc.vector.tensor_scalar(m.blocks_i[0:E, 1:2], m.blocks_i[0:E, 0:1], shift, None, ALU.arith_shift_right))
            nc.vector.tensor_copy(m.blocks_f[0:E, 0:1], m.blocks_i[0:E, 1:2]).then_inc(laid, 1)
            dve.wait_ge(counted, 2)
            link(nc.vector.tensor_copy(m.blocks_f[0:E, 1:2], m.bank[1][0:E, 0:1]))
            nc.vector.tensor_scalar(m.ended[0:E, 0:n_blocks], m.iota[0:E, 0:n_blocks], m.blocks_f[0:E, 1:2], None, ALU.is_ge).then_inc(laid, 1)
            link(nc.vector.tensor_tensor(m.blocks_f[0:E, 2:3], m.blocks_f[0:E, 1:2], m.blocks_f[0:E, 0:1], ALU.subtract))
            link(nc.vector.tensor_scalar(m.blocks_f[0:E, 3:4], m.blocks_f[0:E, 2:3], float(rows), None, ALU.mult))
            link(nc.vector.tensor_tensor(m.offset[0:E, :], m.prefix[0:E, :], m.count[0:E, :], ALU.subtract))
            link(nc.vector.tensor_scalar(m.offset[0:E, :], m.offset[0:E, :], m.blocks_f[0:E, 3:4], None, ALU.add))
            nc.vector.tensor_tensor(diag, m.ident[0:E, 0:E].unsqueeze(1).to_broadcast([E, NT, E]),
                                    m.offset[0:E, :].unsqueeze(2).to_broadcast([E, NT, E]), ALU.mult).then_inc(laid, 1)
            dve.wait_ge(counted, 3)
            link(nc.vector.tensor_scalar(m.owner_f[:, 0:n_blocks], m.bank[2][0:1, 0:n_blocks], float(E - 1), None, ALU.min))
            link(nc.vector.tensor_copy(m.owner_i[:, 0:n_blocks], m.owner_f[:, 0:n_blocks]))
            dve.wait_ge(m.zeroed, 4 * 16)
            for g in range(groups):
                dve.wait_ge(placed, g + 1)
                nc.vector.tensor_copy(m.place[:, g * W:(g + 1) * W], m.bank[4 + g % 2][:, 0:W]).then_inc(done, 1)
            dve.wait_ge(done, groups)


def pick_positions(nc, m, s, E, link, which, mask):
    NT = s.NT
    n = NT * E
    link(nc.vector.tensor_tensor(m.spread[:, 0:n], mask, m.place[:, 0:n], ALU.mult))
    link(nc.vector.tensor_reduce(m.pos_f[:, which, :], m.spread[:, 0:n].rearrange("p (t e) -> p t e", t=NT), AX, ALU.add))
    link(nc.vector.tensor_copy(m.pos_i[:, which, :], m.pos_f[:, which, :]))


def rule_positions(nc, m, s):
    with nc.Block() as block:

        @block.vector
        def _(dve):
            link = Link(dve, m.sem("rule_pos_step"))
            pick_positions(nc, m, s, s.RULES, link, 0, m.mask[:, 0:s.NT * s.RULES])


def turn_rows(rows, turn):
    return rows[bass.ds(turn * (TURN * P), TURN * P), :].rearrange("(k p) c -> p k c", p=P)


def load_turns(sp, m, turns, x_in, turned):
    rows_in = m.rows_in.ap()
    for j in range(2):
        sp.dma_start(m.xb[j][:], turn_rows(rows_in, j)).then_inc(x_in[j], 16)
    with sp.Fori(0, turns // 2) as i:
        for j in range(2):
            sp.wait_ge(turned, i * 2 + (j + 1))
            sp.dma_start(m.xb[j][:], turn_rows(rows_in, i * 2 + (j + 2))).then_inc(x_in[j], 16)


def transpose_turn(nc, m, j, turned):
    for a in range(TURN // 2):
        ins = nc.tensor.transpose(m.bank[j][:, a * P:(a + 1) * P], m.xb[j][:, 2 * a:2 * a + 2, :].rearrange("p k c -> p (k c)"),
                                  m.ident[:])
    ins.then_inc(turned, 1)


def copy_turn(nc, m, s, j, copied):
    for odd in range(2):
        src = m.bank[j][odd * s.C:(odd + 1) * s.C, 0:2 * P].rearrange("c (a p) -> c a p", a=2)
        nc.scalar.copy(m.xT[j][0:s.C, odd:TURN:2, :], src).then_inc(copied, 1)


def rule_blocks(nc, m, s, ins):
    NT, C = s.NT, s.C
    turns = s.rule_turns
    scattered, gathered = m.sem("rule_scattered"), m.sem("rule_gathered")
    x_in = [m.sem(f"rule_x{k}") for k in range(2)]
    y_out = [m.sem(f"rule_y{k}") for k in range(2)]
    turned, copied, multiplied, kept = (m.sem(f"rule_{x}") for x in ("turned", "copied", "multiplied", "kept"))
    stored = m.sem("rule_stored")
    rows_in, rows_out = m.rows_in.ap(), m.rows_out.ap()
    with nc.Block() as block:

        @block.gpsimd
        def _(pool):
            pool.wait_ge(m.zeroed, 4 * 16)
            for t in range(NT):
                index = bass.IndirectOffsetOnAxis(ap=m.pos_i[:, 0, t:t + 1], axis=0)
                pool.indirect_dma_start(rows_in, index, m.h[:, t, :], None).then_inc(scattered, 16)
            pool.wait_ge(stored, 1)
            for t in range(NT):
                index = bass.IndirectOffsetOnAxis(ap=m.pos_i[:, 0, t:t + 1], axis=0)
                pool.indirect_dma_start(m.h[:, t, :], None, rows_out[0:turns * s.TURN_ROWS, :], index).then_inc(gathered, 16)
            pool.wait_ge(gathered, 16 * NT)

        @block.sync
        def _(sp):
            sp.wait_ge(scattered, 16 * NT)
            load_turns(sp, m, turns, x_in, turned)
            for j in range(2):
                sp.wait_ge(x_in[j], 16 * (turns // 2 + 1))

        @block.tensor
        def _(pe):
            pe.wait_ge(m.loaded_rules, 16)
            for j in range(2):
                pe.wait_ge(x_in[j], 16)
                transpose_turn(nc, m, j, turned)
            with pe.Fori(0, turns // 2) as i:
                for j in range(2):
                    owners = load_owners(nc, mybir.EngineType.PE, m, i * (4 * TURN) + 2 * TURN * j, 2 * TURN, s.RULES)
                    pe.wait_ge(copied, i * 4 + (2 * j + 2))
                    pe.wait_ge(kept, i * 4 + (2 * j + 2))
                    for k in range(TURN):
                        for half in range(2):
                            e = owners[2 * k + half]
                            ins_ = nc.tensor.matmul(m.bank[2 + j][:, (2 * k + half) * C:(2 * k + half + 1) * C], m.xT[j][0:C, k, :],
                                                    m.rules[:, bass.ds(e, 1), :].rearrange("d a c -> d (a c)"), start=True, stop=True)
                    ins_.then_inc(multiplied, 1)
                    pe.wait_ge(x_in[j], i * 16 + 32)
                    transpose_turn(nc, m, j, turned)

        @block.scalar
        def _(act):
            for j in range(2):
                act.wait_ge(turned, j + 1)
                copy_turn(nc, m, s, j, copied)
            with act.Fori(0, turns // 2) as i:
                for j in range(2):
                    act.wait_ge(multiplied, i * 2 + (j + 1))
                    act.wait_ge(turned, i * 2 + (j + 3))
                    copy_turn(nc, m, s, j, copied)
                    act.wait_ge(kept, i * 4 + (2 * j + 6))
                    act.dma_start(turn_rows(rows_out, i * 2 + j), m.yb[j][:]).then_inc(y_out[j], 16)
            for j in range(2):
                act.wait_ge(y_out[j], 16 * (turns // 2 + 1))
            act.sem_inc(stored, 1)

        @block.vector
        def _(dve):
            dve.sem_inc(kept, 4)
            for j in range(2):
                dve.sem_inc(y_out[j], 16)
            with dve.Fori(0, turns // 2) as i:
                for j in range(2):
                    dve.wait_ge(multiplied, i * 2 + (j + 1))
                    dve.wait_ge(y_out[j], i * 16 + 16)
                    for half in range(2):
                        rows = slice(half * C, (half + 1) * C)
                        src = m.bank[2 + j][rows, :].rearrange("p (k f c) -> p k f c", k=TURN, f=2)[:, :, half, :]
                        nc.vector.tensor_copy(m.yb[j][rows, :, :], src).then_inc(kept, 1)


def layer_norm(nc, m, s, x, centred, rstd, tag, twice=False):
    NT, C = s.NT, s.C
    ready, rooted = m.sem(f"{tag}_var"), m.sem(f"{tag}_root")
    wide = [P, NT, C]
    with nc.Block() as block:

        @block.vector
        def _(dve):
            link = Link(dve, m.sem(f"{tag}_step"))
            link(nc.vector.tensor_reduce(m.mean[:], x[:], AX, ALU.add))
            link(nc.vector.tensor_scalar(m.mean[:], m.mean[:], 1.0 / C, None, ALU.mult))
            link(nc.vector.tensor_tensor(centred[:], x[:], m.mean[:].unsqueeze(2).to_broadcast(wide), ALU.subtract))
            link(nc.vector.tensor_tensor(m.sq[:], centred[:], centred[:], ALU.mult))
            link(nc.vector.tensor_reduce(m.mean[:], m.sq[:], AX, ALU.add))
            nc.vector.tensor_scalar(m.var[:], m.mean[:], 1.0 / C, EPS, ALU.mult, ALU.add).then_inc(ready, 1)
            dve.wait_ge(rooted, 1)
            link(nc.vector.reciprocal(rstd[:], m.std[:]))
            if twice:
                link(nc.vector.tensor_scalar(m.mean[:], m.mean[:], 1.0 / C, None, ALU.mult))
                link(nc.vector.tensor_tensor(m.mean[:], m.mean[:], rstd[:], ALU.mult))
                link(nc.vector.tensor_tensor(m.mean[:], m.mean[:], rstd[:], ALU.mult))
                nc.vector.tensor_scalar(m.var[:], m.mean[:], EPS, None, ALU.add).then_inc(ready, 1)
                dve.wait_ge(rooted, 2)
                link(nc.vector.reciprocal(m.mean[:], m.std[:]))
                link(nc.vector.tensor_tensor(rstd[:], rstd[:], m.mean[:], ALU.mult))

        @block.scalar
        def _(act):
            for n in range(2 if twice else 1):
                act.wait_ge(ready, n + 1)
                nc.scalar.activation(m.std[:], m.var[:], ACT.Sqrt).then_inc(rooted, 1)


def attention(nc, m, s, ins, layer):
    C, NT = s.C, s.NT
    K = C + 1 if layer == 0 else C
    norm = 1.0 if layer == 0 else 1.0 / float(C) ** 0.5
    tag = f"att{layer}"
    scaled, tA, eA, mQ, eQ, mV, eV, mS, eM, xp, tP, eP, mO, rc, eO = (
        m.sem(f"{tag}_{x}") for x in ("scaled", "turned", "a_copied", "q_made", "q_copied", "v_made", "v_copied",
                                      "scored", "maxed", "exped", "p_turned", "p_copied", "mixed", "recip", "kept"))
    bank = m.bank
    mqk = m.mqk[layer]
    with nc.Block() as block:

        @block.sync
        def _(sp):
            if layer == 1:
                sp.dma_start(m.w1_all[0:C, :, :], ins["L1_ffn_W1"].rearrange("e d h -> d e h")).then_inc(m.loaded_experts, 16)
                sp.dma_start(m.w1_all[C:C + 1, :, :], ins["L1_ffn_b1"].rearrange("(a e) h -> a e h", a=1)).then_inc(m.loaded_experts, 16)

        @block.tensor
        def _(pe):
            with pe.Fori(0, s.B // 2) as i:
                n = lambda k: i * 2 + (k + 1)
                for k in range(2):
                    pe.wait_ge(scaled, n(k))
                    pe.wait_ge(eO, n(k))
                    nc.tensor.transpose(bank[k][:, 0:P], m.an[k][:].rearrange("p j c -> p (j c)"), m.ident[:]).then_inc(tA, 1)
                for k in range(2):
                    wait_apart(pe, eA, i * 4 + (2 * k + 2))
                    nc.tensor.matmul(bank[k][0:K, 2 * P:4 * P], mqk[:], m.aT[k][0:K, :], start=True, stop=True).then_inc(mQ, 1)
                    if layer == 0:
                        for j in range(2):
                            ins = nc.tensor.matmul(bank[2 + k][:, j * C:(j + 1) * C], m.aT[k][:, j * P:(j + 1) * P], m.wvp[:],
                                                   start=True, stop=True)
                        ins.then_inc(mV, 1)
                for k in range(2):
                    wait_apart(pe, eQ, n(k))
                    for j in range(2):
                        ins = nc.tensor.matmul(bank[4 + k][:, j * 2 * P:(j + 1) * 2 * P], m.qT[k][0:K, j * P:(j + 1) * P],
                                               m.aT[k][0:K, :], start=True, stop=True)
                    ins.then_inc(mS, 1)
                for k in range(2):
                    pe.wait_ge(xp, n(k))
                    for j in range(2):
                        for c in range(2):
                            ins = nc.tensor.transpose(bank[6 + k][:, c * 2 * P + j * P:c * 2 * P + (j + 1) * P],
                                                      m.pr[k][:, j, c * P:(c + 1) * P], m.ident[:])
                    ins.then_inc(tP, 1)
                for k in range(2):
                    pe.wait_ge(eP, n(k))
                    if layer == 0:
                        pe.wait_ge(eV, n(k))
                    v = m.v[k] if layer == 0 else m.an[k]
                    for j in range(2):
                        for c in range(2):
                            ins = nc.tensor.matmul(bank[2 + k][:, (2 + j) * C:(3 + j) * C], m.pT[k][:, c, j * P:(j + 1) * P],
                                                   v[:, c, :], start=(c == 0), stop=(c == 1))
                    ins.then_inc(mO, 1)

        @block.vector
        def _(dve):
            for k in range(2):
                dve.sem_inc(eO, 1)
            with dve.Fori(0, s.B // 2) as i:
                n = lambda k: i * 2 + (k + 1)
                for k in range(2):
                    dve.wait_ge(eO, n(k))
                    tiles = bass.ds(i * 4 + 2 * k, 2)
                    nc.vector.tensor_tensor(m.an[k][:], m.xc[:, tiles, :], m.rstd[:, tiles].unsqueeze(2).to_broadcast([P, 2, C]),
                                            ALU.mult).then_inc(scaled, 1)
                for k in range(2):
                    dve.wait_ge(mQ, n(k))
                    nc.vector.tensor_copy(m.qT[k][0:K, :], bank[k][0:K, 2 * P:4 * P]).then_inc(eQ, 1)
                for k in range(2):
                    wait_apart(dve, mS, n(k))
                    st = m.stat[k]
                    if layer == 0:
                        for j in range(2):
                            ins = nc.vector.tensor_tensor_reduce(m.pr[k][:, j, :], bank[4 + k][:, j * 2 * P:(j + 1) * 2 * P],
                                                                 m.relbias[:, (1 - j) * P:(3 - j) * P], 1.0, -3.0e38,
                                                                 ALU.add, ALU.max, st[:, j:j + 1])
                        ins.then_inc(eM, 1)
                    else:
                        nc.vector.tensor_reduce(st[:, 0:2], bank[4 + k][:].rearrange("p (j n) -> p j n", j=2), AX, ALU.max).then_inc(eM, 1)
                    dve.wait_ge(eM, i * 4 + 2 * k + 1)
                    nc.vector.tensor_scalar(st[:, 2:4], st[:, 0:2], -norm, None, ALU.mult).then_inc(eM, 1)
                for k in range(2):
                    dve.wait_ge(xp, n(k))
                    nc.vector.reciprocal(m.stat[k][:, 6:8], m.stat[k][:, 4:6]).then_inc(rc, 1)
                    dve.wait_ge(tP, n(k))
                    nc.vector.tensor_copy(m.pT[k][:], bank[6 + k][:].rearrange("p (c n) -> p c n", c=2)).then_inc(eP, 1)
                for k in range(2):
                    dve.wait_ge(mO, n(k))
                    dve.wait_ge(rc, n(k))
                    nc.vector.tensor_tensor(m.msg[:, bass.ds(i * 4 + 2 * k, 2), :],
                                            bank[2 + k][:, 2 * C:4 * C].rearrange("p (j c) -> p j c", j=2),
                                            m.stat[k][:, 6:8].unsqueeze(2).to_broadcast([P, 2, C]), ALU.mult).then_inc(eO, 1)

        @block.scalar
        def _(act):
            with act.Fori(0, s.B // 2) as i:
                n = lambda k: i * 2 + (k + 1)
                for k in range(2):
                    act.wait_ge(tA, n(k))
                    nc.scalar.copy(m.aT[k][0:C, 0:P], bank[k][0:C, 0:P]).then_inc(eA, 1)
                    nc.scalar.copy(m.aT[k][0:C, P:2 * P], bank[k][C:2 * C, 0:P]).then_inc(eA, 1)
                if layer == 0:
                    for k in range(2):
                        act.wait_ge(mV, n(k))
                        nc.scalar.copy(m.v[k][:].rearrange("p j c -> p (j c)"), bank[2 + k][:, 0:2 * C]).then_inc(eV, 1)
                for k in range(2):
                    act.wait_ge(eM, i * 4 + 2 * k + 2)
                    for j in range(2):
                        src = m.pr[k][:, j, :] if layer == 0 else bank[4 + k][:, j * 2 * P:(j + 1) * 2 * P]
                        ins = nc.scalar.activation(m.pr[k][:, j, :], src, ACT.Exp, bias=m.stat[k][:, 2 + j:3 + j], scale=norm,
                                                   accum_out=m.stat[k][:, 4 + j:5 + j])
                    ins.then_inc(xp, 1)


def after_attention0(nc, m, s):
    NT, C = s.NT, s.C
    wide = [P, NT, C]
    with nc.Block() as block:

        @block.vector
        def _(dve):
            link = Link(dve, m.sem("after0_step"))
            link(nc.vector.scalar_tensor_tensor(out=m.msg[:], in0=m.msg[:], scalar=m.scale[:, 0:1],
                                                in1=m.pbias[:].unsqueeze(1).to_broadcast(wide), op0=ALU.mult, op1=ALU.add))
    layer_norm(nc, m, s, m.msg, m.xc, m.rstd, "ln2")
    with nc.Block() as block:

        @block.vector
        def _(dve):
            link = Link(dve, m.sem("after0_step2"))
            link(nc.vector.tensor_tensor(m.xc[:], m.xc[:], m.rstd[:].unsqueeze(2).to_broadcast(wide), ALU.mult))
            link(nc.vector.tensor_tensor(m.xc[:], m.xc[:], m.g2[:].unsqueeze(1).to_broadcast(wide), ALU.mult))
            link(nc.vector.tensor_tensor(m.xc[:], m.xc[:], m.b2ln[:].unsqueeze(1).to_broadcast(wide), ALU.add))
            link(nc.vector.tensor_tensor(m.h[:], m.h[:], m.xc[:], ALU.add))


def turn_tokens(nc, m, s, block, tag, scale_first, dest):
    NT, C = s.NT, s.C
    ready, turned, copied = (m.sem(f"{tag}_{x}") for x in ("ready", "turned", "copied"))

    @block.vector
    def _(dve):
        wide = [P, NT, C]
        nc.vector.tensor_tensor(m.xc[:], m.xc[:], m.rstd[:].unsqueeze(2).to_broadcast(wide), ALU.mult).then_inc(ready, 1)
        for g in range(0, NT // 4, 2):
            dve.wait_ge(turned, g + 1)
            dst, src = dest(g)
            nc.vector.tensor_copy(dst, src).then_inc(copied, 1)

    @block.scalar
    def _(act):
        for g in range(1, NT // 4, 2):
            act.wait_ge(turned, g + 1)
            dst, src = dest(g)
            nc.scalar.copy(dst, src).then_inc(copied, 1)

    @block.tensor
    def _(pe):
        pe.wait_ge(ready, 1)
        for g in range(NT // 4):
            for j in range(4):
                ins = nc.tensor.transpose(m.bank[g][0:C, j * P:(j + 1) * P], m.xc[:, 4 * g + j, :], m.ident[:])
            ins.then_inc(turned, 1)


def lstm_inputs(nc, m, s):
    C = s.C

    def dest(g):
        dst = m.xseq[0:C, 0:s.T].rearrange("c (t b) -> c b t", b=s.B)[:, 2 * g:2 * g + 2, :]
        return dst, m.bank[g][0:C, :].rearrange("c (b t) -> c b t", b=2)

    with nc.Block() as block:
        turn_tokens(nc, m, s, block, "lin", True, dest)


def lstm(nc, m, s):
    C, B = s.C, s.B
    summed, forgot, entered, celled, tanned, hidden, saved = (
        m.sem(f"lstm_{x}") for x in ("summed", "forgot", "entered", "cell", "tanh", "hidden", "saved"))
    turns = s.L // STEPS
    groups = STEPS // AHEAD

    def gate_bank(q, k):
        return m.bank[2 * q + k // AHEAD % 2]

    def gate_sums(q, k):
        at = k % AHEAD * B
        return gate_bank(q, k)[0:C, at:at + B]

    with nc.Block() as block:

        def project(k, first):
            for q in range(4):
                nc.tensor.matmul(gate_bank(q, k)[0:C, 0:AHEAD * B], m.wi[:, q * C:(q + 1) * C], m.xseq[:, first],
                                 start=True, stop=False, skip_group_check=True)

        @block.tensor
        def _(pe):
            project(0, slice(0, AHEAD * B))
            with pe.Fori(0, turns) as i:
                for k in range(STEPS):
                    pe.wait_ge(hidden, i * STEPS + (k + 1))
                    for q in range(4):
                        nc.tensor.matmul(gate_sums(q, k), m.wh[:, q * C:(q + 1) * C], m.ring[:, (k - 1) % RING, :],
                                         start=False, stop=True, skip_group_check=True).then_inc(summed, 1)
                    if k % AHEAD == AHEAD - 1:
                        project(k + 1, bass.ds(i * (STEPS * B) + (k + 1) * B, AHEAD * B))
                    else:
                        for w in range(WARMERS):
                            nc.tensor.matmul(gate_bank(w % 4, k + AHEAD)[0:C, :], m.ones_b[:, 0:C], m.mask[:, 0:512],
                                             start=True, stop=True, skip_group_check=True)

        @block.scalar
        def _(act):
            with act.Fori(0, turns) as i:
                for k in range(STEPS):
                    n = lambda q: i * (4 * STEPS) + (4 * k + q + 1)
                    act.wait_ge(summed, n(0))
                    nc.scalar.activation(m.forget[:], gate_sums(0, k), ACT.Sigmoid).then_inc(forgot, 1)
                    act.wait_ge(summed, n(1))
                    nc.scalar.activation(m.factors[:, :, 1], gate_sums(1, k), ACT.Sigmoid).then_inc(entered, 1)
                    act.wait_ge(summed, n(2))
                    nc.scalar.activation(m.terms[:, :, 0], gate_sums(2, k), ACT.Tanh).then_inc(entered, 1)
                    act.wait_ge(summed, n(3))
                    nc.scalar.activation(m.emit[:], gate_sums(3, k), ACT.Sigmoid)
                    act.wait_ge(celled, i * STEPS + (k + 1))
                    nc.scalar.activation(m.tanc[:], m.cells[:, :, 1], ACT.Tanh).then_inc(tanned, 1)

        @block.vector
        def _(dve):
            dve.sem_inc(hidden, 1)
            with dve.Fori(0, turns) as i:
                for k in range(STEPS):
                    if k % AHEAD == 0:
                        dve.wait_ge(saved, i * groups + (k // AHEAD + 1))
                    dve.wait_ge(forgot, i * STEPS + (k + 1))
                    nc.vector.tensor_tensor(m.terms[:, :, 1], m.forget[:], m.cells[:, :, 1], ALU.mult).then_inc(entered, 1)
                    dve.wait_ge(entered, i * (3 * STEPS) + (3 * k + 3))
                    nc.vector.tensor_tensor_scan(m.cells[:].rearrange("c b t -> c (b t)"), m.factors[:].rearrange("c b t -> c (b t)"),
                                                 m.terms[:].rearrange("c b t -> c (b t)"), 0.0, ALU.mult, ALU.add).then_inc(celled, 1)
                    dve.wait_ge(tanned, i * STEPS + (k + 1))
                    nc.vector.tensor_tensor(m.ring[0:C, k % RING, :], m.emit[:], m.tanc[:], ALU.mult).then_inc(hidden, 1)

        @block.gpsimd
        def _(pool):
            hist = m.hist[:].rearrange("c (b t) -> c t b", b=B)
            pool.sem_inc(saved, 1)
            pool.sem_inc(saved, 1)
            with pool.Fori(0, turns) as i:
                for g in range(groups):
                    half = g % 2 * AHEAD
                    pool.wait_ge(hidden, i * STEPS + ((g + 1) * AHEAD + 1))
                    h = m.ring[0:C, half:half + AHEAD, :]
                    nc.gpsimd.tensor_tensor(hist[:, bass.ds(i * STEPS + g * AHEAD, AHEAD), :], h, h, ALU.add).then_inc(saved, 1)


def lstm_output(nc, m, s):
    C, B, T, NT, L = s.C, s.B, s.T, s.NT, s.L
    lined, biased, gated, scanned = (m.sem(f"lout_{x}") for x in ("lined", "biased", "gated", "scanned"))
    turned, added = m.sem("lout_turned"), m.sem("lout_added")
    ready = m.sem("lout_ready")
    chunks = T // 512
    with nc.Block() as block:

        @block.tensor
        def _(pe):
            for i in range(chunks):
                k = i % 2
                if i >= 2:
                    pe.wait_ge(gated, 2 * (i - 1))
                for l in range(2):
                    ins = nc.tensor.matmul(m.bank[2 * k + l][0:C, :], m.wlinb[:, l, :], m.hist[:, i * 512:(i + 1) * 512],
                                           start=True, stop=True)
                ins.then_inc(lined, 1)
            pe.wait_ge(ready, 1)
            for g in range(NT // 8):
                for j in range(8):
                    ins = nc.tensor.transpose(m.bank[4 + g][:, j * C:(j + 1) * C], m.tb[:, (8 * g + j) * P:(8 * g + j + 1) * P],
                                              m.ident[0:C, 0:C])
                ins.then_inc(turned, 1)

        @block.scalar
        def _(act):
            for i in range(chunks):
                k = i % 2
                act.wait_ge(lined, i + 1)
                if i >= 2:
                    act.wait_ge(gated, 2 * (i - 1))
                nc.scalar.activation(m.lg0[k][:], m.bank[2 * k][0:C, :], ACT.Identity, bias=m.blin[:, 0:1]).then_inc(biased, 1)

        @block.vector
        def _(dve):
            link = Link(dve, m.sem("lout_step"))
            for i in range(chunks):
                for k in (i % 2,):
                    now = slice(i * 512, (i + 1) * 512)
                    dve.wait_ge(biased, i + 1)
                    nc.vector.scalar_tensor_tensor(out=m.gt[k][:], in0=m.bank[2 * k + 1][0:C, :], scalar=m.blin[:, 1:2],
                                                   in1=m.lg0[k][:], op0=ALU.add, op1=ALU.is_gt).then_inc(gated, 1)
                    dve.wait_ge(gated, 2 * i + 1)
                    nc.vector.tensor_tensor(m.ta[:, now], m.gt[k][:], m.hist[:, now], ALU.mult).then_inc(gated, 1)
            dve.wait_ge(gated, 2 * chunks)
            link(nc.vector.memset(m.lg0[0][:], 1.0))
            with dve.Fori(0, B) as b:
                nc.vector.tensor_tensor_scan(m.tb[:, bass.ds(b * L, L)], m.lg0[0][:, 0:L], m.ta[:, bass.ds(b * L, L)],
                                             0.0, ALU.mult, ALU.add).then_inc(scanned, 1)
            dve.wait_ge(scanned, B)
            tb3 = m.tb[:].rearrange("c (b t) -> c b t", b=B)
            ta3 = m.ta[:].rearrange("c (b t) -> c b t", b=B)
            link(nc.vector.tensor_tensor(m.ta[:], m.tb[:], m.ta[:], ALU.subtract))
            link(nc.vector.scalar_tensor_tensor(out=m.hist[:], in0=m.ta[:], scalar=m.fwbw[:, 2:3], in1=m.hist[:],
                                                op0=ALU.mult, op1=ALU.add))
            link(nc.vector.tensor_tensor(ta3, tb3, tb3[:, :, L - 1:L].to_broadcast([C, B, L]), ALU.subtract))
            nc.vector.scalar_tensor_tensor(out=m.tb[:], in0=m.ta[:], scalar=m.fwbw[:, 3:4], in1=m.hist[:],
                                           op0=ALU.mult, op1=ALU.add).then_inc(ready, 1)
            for g in range(NT // 8):
                dve.wait_ge(turned, g + 1)
                hg = m.h[:, 8 * g:8 * g + 8, :]
                nc.vector.tensor_tensor(hg, hg, m.bank[4 + g][:].rearrange("p (j c) -> p j c", j=8), ALU.add).then_inc(added, 1)
            dve.wait_ge(added, NT // 8)


def add_messages(nc, m, s):
    with nc.Block() as block:

        @block.vector
        def _(dve):
            link = Link(dve, m.sem("msg_step"))
            link(nc.vector.tensor_tensor(m.h[:], m.h[:], m.msg[:], ALU.add))


def router(nc, m, s):
    NT, C, E, T = s.NT, s.C, s.EXPERTS, s.T
    xT = m.xseq

    def dest(g):
        return xT[0:C, g * 512:(g + 1) * 512], m.bank[g][0:C, :]

    with nc.Block() as block:
        turn_tokens(nc, m, s, block, "rin", True, dest)
    lined, copied, topped, found = (m.sem(f"router_{x}") for x in ("lined", "copied", "topped", "found"))
    difference, exponent = m.sem("router_diff"), m.sem("router_exp")
    with nc.Block() as block:

        @block.tensor
        def _(pe):
            for g in range(NT // 8):
                for j in range(8):
                    t = 8 * g + j
                    ins = nc.tensor.matmul(m.bank[g][:, j * E:(j + 1) * E], xT[:, t * P:(t + 1) * P], m.wr[:], start=True, stop=True)
                ins.then_inc(lined, 1)

        @block.scalar
        def _(act):
            for g in range(NT // 8):
                act.wait_ge(lined, g + 1)
                nc.scalar.copy(m.logits[:, 8 * g:8 * g + 8, :], m.bank[g][:, 0:8 * E].rearrange("p (j e) -> p j e", j=8)).then_inc(copied, 1)
            act.wait_ge(difference, 1)
            nc.scalar.activation(m.gtmp[:, 1, :], m.gtmp[:, 0, :], ACT.Exp).then_inc(exponent, 1)

        @block.vector
        def _(dve):
            link = Link(dve, m.sem("router_step"))
            dve.wait_ge(copied, NT // 8)
            for t in range(NT):
                nc.vector.max(m.top[:, t, :], m.logits[:, t, :]).then_inc(topped, 1)
            for t in range(NT):
                dve.wait_ge(topped, t + 1)
                nc.vector.max_index(m.topi[:, t, :], m.top[:, t, :], m.logits[:, t, :]).then_inc(found, 1)
            dve.wait_ge(found, NT)
            nc.vector.tensor_tensor(m.gtmp[:, 0, :], m.top[:, :, 1], m.top[:, :, 0], ALU.subtract).then_inc(difference, 1)
            link(nc.vector.tensor_copy(m.topf[:], m.topi[:, :, 0:2]))
            shape = [P, NT, E]
            n = NT * E
            for which, dst in ((0, m.first), (1, m.second)):
                link(nc.vector.tensor_tensor(dst[:].rearrange("p (t e) -> p t e", t=NT),
                                             m.topf[:, :, which:which + 1].to_broadcast(shape),
                                             m.iota[:, 0:E].unsqueeze(1).to_broadcast(shape), ALU.is_equal))
            link(nc.vector.tensor_tensor(m.mask[:, 0:n], m.first[:], m.second[:], ALU.add))
            dve.wait_ge(exponent, 1)
            link(nc.vector.tensor_scalar(m.gtmp[:, 2, :], m.gtmp[:, 1, :], 1.0, None, ALU.add))
            link(nc.vector.reciprocal(m.gate[:, 0, :], m.gtmp[:, 2, :]))
            link(nc.vector.tensor_tensor(m.gate[:, 1, :], m.gate[:, 0, :], m.gtmp[:, 1, :], ALU.mult))


def expert_positions(nc, m, s):
    with nc.Block() as block:

        @block.vector
        def _(dve):
            link = Link(dve, m.sem("expert_pos_step"))
            pick_positions(nc, m, s, s.EXPERTS, link, 0, m.first[:])
            pick_positions(nc, m, s, s.EXPERTS, link, 1, m.second[:])


def expert_blocks(nc, m, s, ins):
    NT, C, H, E = s.NT, s.C, s.HID, s.EXPERTS
    turns = s.expert_turns
    scattered = m.sem("exp_scattered")
    x_in = [m.sem(f"exp_x{k}") for k in range(2)]
    y_out = [m.sem(f"exp_y{k}") for k in range(2)]
    turned, copied, picked, up, active, down, kept = (
        m.sem(f"exp_{x}") for x in ("turned", "copied", "picked", "up", "active", "down", "kept"))
    gated, g_turned, g_copied, g_added, g_summed = (m.sem(f"bias_{x}") for x in ("gated", "turned", "copied", "added", "summed"))
    rows_in, rows_out = m.rows_in.ap(), m.rows_out.ap()
    gates = m.spread[:, 0:NT * E].rearrange("p (t e) -> p t e", t=NT)
    other = m.place[:, 0:NT * E].rearrange("p (t e) -> p t e", t=NT)
    groups = NT // 4
    with nc.Block() as block:

        @block.gpsimd
        def _(pool):
            for which in range(2):
                for t in range(NT):
                    index = bass.IndirectOffsetOnAxis(ap=m.pos_i[:, which, t:t + 1], axis=0)
                    pool.indirect_dma_start(rows_in, index, m.xc[:, t, :], None).then_inc(scattered, 16)

            def pick(turn, j):
                for k, e in enumerate(load_owners(nc, mybir.EngineType.Pool, m, turn * TURN, TURN, E)):
                    nc.gpsimd.tensor_copy(m.w1[j][:, k, :], m.w1_all[:, bass.ds(e, 1), :].rearrange("d a h -> d (a h)")).then_inc(picked, 1)

            pool.wait_ge(m.loaded_experts, 4 * 16)
            for j in range(2):
                pick(j, j)
            with pool.Fori(0, turns // 2) as i:
                for j in range(2):
                    pool.wait_ge(up, i * 2 + (j + 1))
                    pick(i * 2 + (j + 2), j)

        @block.sync
        def _(sp):
            sp.wait_ge(scattered, 2 * 16 * NT)
            load_turns(sp, m, turns, x_in, turned)
            for j in range(2):
                sp.wait_ge(x_in[j], 16 * (turns // 2 + 1))

        @block.tensor
        def _(pe):
            pe.wait_ge(m.loaded_experts, 4 * 16)
            pe.wait_ge(gated, 3)
            for g in range(groups):
                if g >= 2:
                    pe.wait_ge(g_copied, g - 1)
                for a in range(4):
                    ins_ = nc.tensor.transpose(m.bank[6 + g % 2][0:E, a * P:(a + 1) * P], gates[:, 4 * g + a, :], m.ident[:])
                ins_.then_inc(g_turned, 1)
                pe.wait_ge(g_copied, g + 1)
                if g >= 2:
                    pe.wait_ge(g_summed, g - 1)
                for a in range(4):
                    ins_ = nc.tensor.matmul(m.bank[4 + g % 2][:, a * C:(a + 1) * C], m.gT[g % 2][:, a * P:(a + 1) * P], m.b2_all[:],
                                            start=True, stop=True)
                ins_.then_inc(g_added, 1)

            def ups(j):
                for k in range(TURN):
                    ins_ = nc.tensor.matmul(m.bank[2 + j][:, k * P:(k + 1) * P], m.w1[j][:, k, :], m.xT[j][:, k, :], start=True, stop=True)
                ins_.then_inc(up, 1)

            for j in range(2):
                pe.wait_ge(x_in[j], 16)
                transpose_turn(nc, m, j, turned)
            pe.wait_ge(copied, 2)
            pe.wait_ge(picked, TURN)
            ups(0)
            with pe.Fori(0, turns // 2) as i:
                for j in range(2):
                    pe.wait_ge(x_in[j], i * 16 + 32)
                    transpose_turn(nc, m, j, turned)
                    pe.wait_ge(copied, i * 4 + (2 * j + 4))
                    pe.wait_ge(picked, i * (2 * TURN) + TURN * (j + 2))
                    ups(1 - j)
                    owners = load_owners(nc, mybir.EngineType.PE, m, i * (2 * TURN) + TURN * j, TURN, E)
                    pe.wait_ge(active, i * 2 + (j + 1))
                    pe.wait_ge(kept, i * 2 + (j + 1))
                    for k in range(TURN):
                        ins_ = nc.tensor.matmul(m.bank[4 + j][:, k * C:(k + 1) * C], m.hT[j][:, k, :],
                                                m.w2_all[:, bass.ds(owners[k], 1), :].rearrange("h a c -> h (a c)"), start=True, stop=True)
                    ins_.then_inc(down, 1)

        @block.scalar
        def _(act):
            for g in range(groups):
                act.wait_ge(g_turned, g + 1)
                if g >= 2:
                    act.wait_ge(g_added, g - 1)
                nc.scalar.copy(m.gT[g % 2][:], m.bank[6 + g % 2][0:E, :]).then_inc(g_copied, 1)
            for j in range(2):
                act.wait_ge(turned, j + 1)
                copy_turn(nc, m, s, j, copied)
            with act.Fori(0, turns // 2) as i:
                for j in range(2):
                    act.wait_ge(up, i * 2 + (j + 1))
                    act.wait_ge(turned, i * 2 + (j + 3))
                    copy_turn(nc, m, s, j, copied)
                    act.wait_ge(kept, i * 2 + (j + 3))
                    act.dma_start(turn_rows(rows_out, i * 2 + j), m.yb[j][:]).then_inc(y_out[j], 16)
            for j in range(2):
                act.wait_ge(y_out[j], 16 * (turns // 2 + 1))

        @block.vector
        def _(dve):
            wide = [P, NT, E]
            as3 = lambda ap: ap[:].rearrange("p (t e) -> p t e", t=NT)
            nc.vector.tensor_tensor(gates, as3(m.first), m.gate[:, 0, :].unsqueeze(2).to_broadcast(wide), ALU.mult).then_inc(gated, 1)
            nc.vector.tensor_tensor(other, as3(m.second), m.gate[:, 1, :].unsqueeze(2).to_broadcast(wide), ALU.mult).then_inc(gated, 1)
            dve.wait_ge(gated, 2)
            nc.vector.tensor_tensor(gates, gates, other, ALU.add).then_inc(gated, 1)
            for g in range(groups):
                dve.wait_ge(g_added, g + 1)
                hg = m.h[:, 4 * g:4 * g + 4, :]
                nc.vector.tensor_tensor(hg, hg, m.bank[4 + g % 2][:, 0:4 * C].rearrange("p (a c) -> p a c", a=4), ALU.add).then_inc(g_summed, 1)

            def relus(j):
                nc.vector.tensor_scalar(m.hT[j][:], m.bank[2 + j][:].rearrange("h (k p) -> h k p", k=TURN), 0.0, None, ALU.max).then_inc(active, 1)

            dve.sem_inc(kept, 2)
            dve.sem_inc(down, 1)
            for j in range(2):
                dve.sem_inc(y_out[j], 16)
            dve.wait_ge(up, 1)
            relus(0)
            with dve.Fori(0, turns // 2) as i:
                for j in range(2):
                    dve.wait_ge(up, i * 2 + (j + 2))
                    dve.wait_ge(down, i * 2 + (j + 1))
                    relus(1 - j)
                    dve.wait_ge(down, i * 2 + (j + 2))
                    dve.wait_ge(y_out[j], i * 16 + 16)
                    nc.vector.tensor_copy(m.yb[j][:], m.bank[4 + j][:, 0:TURN * C].rearrange("p (k c) -> p k c", k=TURN)).then_inc(kept, 1)


def combine(nc, m, s, out):
    NT, C = s.NT, s.C
    gathered, summed, stored = m.sem("comb_gathered"), m.sem("comb_summed"), m.sem("comb_stored")
    wide = [P, NT, C]
    ys = (m.msg, m.sq)
    with nc.Block() as block:

        @block.gpsimd
        def _(pool):
            for which in range(2):
                for t in range(NT):
                    index = bass.IndirectOffsetOnAxis(ap=m.pos_i[:, which, t:t + 1], axis=0)
                    pool.indirect_dma_start(ys[which][:, t, :], None, m.rows_out.ap()[0:s.expert_turns * s.TURN_ROWS, :], index).then_inc(gathered, 16)

        @block.vector
        def _(dve):
            link = Link(dve, m.sem("comb_step"))
            dve.wait_ge(gathered, 2 * 16 * NT)
            for which in range(2):
                y = ys[which]
                link(nc.vector.tensor_tensor(y[:], y[:], m.gate[:, which, :].unsqueeze(2).to_broadcast(wide), ALU.mult))
                ins = nc.vector.tensor_tensor(m.h[:], m.h[:], y[:], ALU.add)
                if which == 0:
                    link(ins)
            ins.then_inc(summed, 1)

        @block.sync
        def _(sp):
            sp.wait_ge(summed, 1)
            sp.dma_start(out.rearrange("b (h p) c -> p (b h) c", p=P), m.h[:]).then_inc(stored, 16)
            sp.wait_ge(stored, 16)


_INS = ["x", "L0_tok_base_embeddings", "L0_tok_rule_transform", "L0_tok_token_rules", "L0_attn_ln1_g", "L0_attn_ln1_b",
        "L0_attn_qkv_w", "L0_attn_qkv_b", "L0_attn_bias_table", "L0_attn_scale", "L0_attn_proj_w", "L0_attn_proj_b",
        "L0_attn_ln2_g", "L0_attn_ln2_b", "L0_ffn_W_ih", "L0_ffn_W_hh", "L0_ffn_b_ih", "L0_ffn_b_hh", "L0_ffn_W_lin",
        "L0_ffn_b_lin", "L0_ffn_fw_att", "L0_ffn_bw_att", "L1_attn_W", "L1_ffn_Wr", "L1_ffn_br", "L1_ffn_W1", "L1_ffn_b1",
        "L1_ffn_W2", "L1_ffn_b2"]


def kernel(**inputs):
    import numpy as _np
    import concourse.bacc as _bacc
    from concourse.bass_utils import run_bass_kernel_spmd as _run

    nc = _bacc.Bacc("TRN2", target_bir_lowering=False, num_devices=1)
    arrays, args = {}, {}
    for name in _INS:
        a = _np.ascontiguousarray(inputs[name])
        if a.ndim == 0:
            a = a.reshape(1)
        arrays[f"in_{name}"] = a
        args[name] = nc.dram_tensor(f"in_{name}", a.shape, mybir.dt.from_np(a.dtype), kind="ExternalInput").ap()
    shape = tuple(inputs["x"].shape) + (inputs["L0_tok_base_embeddings"].shape[1],)
    result = nc.dram_tensor("result", shape, F32, kind="ExternalOutput").ap()
    tower(nc, args, result)
    r = _run(nc, [arrays], core_ids=[0])
    return r.results[0]["result"]
```

```python
from contextlib import ExitStack

import concourse.bass as bass
from concourse import mybir

P = 128
ALU = mybir.AluOpType
ACT = mybir.ActivationFunctionType
AX = mybir.AxisListType.X
F32 = mybir.dt.float32
BF16 = mybir.dt.bfloat16
I32 = mybir.dt.int32
U32 = mybir.dt.uint32

EPS = 1e-5
DEPTH = 4
TURN = 4
STEPS = 32
AHEAD = 8
RING = 2 * AHEAD
GROUP = 8
SLOTS = 4
WARMERS = 4


def col(ap):
    return ap.rearrange("(c a) -> c a", a=1)


def row(ap):
    return ap.rearrange("(a c) -> a c", a=1)


def view(ap, offset, pattern):
    return bass.AP(tensor=ap.tensor, offset=ap.offset + offset, ap=pattern)


class Link:

    def __init__(self, engine, m):
        self.engine, self.m = engine, m

    def __call__(self, instruction):
        self.m.steps += 1
        instruction.then_inc(self.m.step, 1)
        self.engine.wait_ge(self.m.step, self.m.steps)


def wait_apart(engine, semaphore, value):
    engine.wait_ge(semaphore, value)
    engine.nop(nofuse=True)


def load_owners(nc, engine, m, first, count, choices):
    _, owners = nc.values_load_multi_w_load_instructions(
        m.owner_i[0:1, bass.ds(first, count)], engines=(engine,), min_val=0, max_val=choices - 1,
        skip_runtime_bounds_check_because="route() clamps the owners to the last choice")
    return owners


class Shapes:
    def __init__(self, x, base, rules, rule_of, bias_table, w1, w2):
        self.B, self.L = x.shape
        self.T = self.B * self.L
        self.NT = self.T // P
        self.VOCAB, self.C = base.shape
        self.RULES = rules.shape[0]
        self.EXPERTS, _, self.HID = w1.shape
        assert self.C == 64 and self.L == 2 * P and self.HID == P and self.NT == 32
        self.RULE_ROWS = 64
        rule_blocks = (self.T + self.RULES * (self.RULE_ROWS - 1)) // self.RULE_ROWS
        expert_blocks = (self.T + self.EXPERTS * (P - 1)) // P
        self.rule_turns = even_turns(rule_blocks * self.RULE_ROWS)
        self.choice_turns = DEPTH * -(-expert_blocks // (DEPTH * TURN))
        self.expert_turns = 2 * self.choice_turns
        self.TURN_ROWS = TURN * P
        self.ROWS = (max(self.rule_turns, self.expert_turns) + DEPTH) * self.TURN_ROWS
        self.RULE_BLOCKS = self.rule_turns * self.TURN_ROWS // self.RULE_ROWS
        self.CHOICE_BLOCKS = self.choice_turns * TURN
        self.RULE_ZEROS = (self.rule_turns + 2) * self.TURN_ROWS


def even_turns(rows):
    return 2 * -(-rows // (2 * TURN * P))


def tower(nc, ins, out):
    s = Shapes(ins["x"], ins["L0_tok_base_embeddings"], ins["L0_tok_rule_transform"],
               ins["L0_tok_token_rules"], ins["L0_attn_bias_table"], ins["L1_ffn_W1"], ins["L1_ffn_W2"])
    with ExitStack() as ctx:
        m = Memory(nc, ctx, s)
        constants_and_ids(nc, m, s, ins)
        gather_and_prepare(nc, m, s, ins)
        rule_blocks(nc, m, s, ins)
        attention(nc, m, s, ins, 0)
        after_attention0(nc, m, s)
        lstm(nc, m, s)
        lstm_output(nc, m, s)
        attention(nc, m, s, ins, 1)
        router(nc, m, s)
        expert_routes(nc, m, s)
        expert_blocks(nc, m, s, ins)
        combine(nc, m, s, out)


class Memory:

    def __init__(self, nc, ctx, s):
        self.nc, self.ctx = nc, ctx

        def sb(name, shape, dt=F32):
            return ctx.enter_context(nc.sbuf_tensor(name, shape, dt))

        NT, C, T, B = s.NT, s.C, s.T, s.B
        self.rows_in = nc.dram_tensor("rows_in", [s.ROWS, C], F32)
        self.rows_out = nc.dram_tensor("rows_out", [s.ROWS, C], F32)
        self.bank = [ctx.enter_context(nc.psum_tensor(f"bank{i}", [P, 512], F32)) for i in range(8)]
        self.ident = sb("ident", [P, P])
        self.anti = sb("anti", [P, P])
        self.upto = sb("upto", [P, P])
        self.ones = sb("ones", [P, P])
        self.ones_b = sb("ones_b", [P, P], BF16)
        self.before_b = sb("before_b", [P, P], BF16)
        self.iota = sb("iota", [P, 256])
        self.ids = sb("ids", [NT, P], I32)
        self.ids_f = sb("ids_f", [NT, P])
        self.ids_neg = sb("ids_neg", [NT, P])
        self.id_col = sb("id_col", [P, NT], I32)
        self.rule_i = sb("rule_i", [P, NT], I32)
        self.rule_f = sb("rule_f", [P, NT])
        W = max(NT * s.RULES, T)
        self.mask = sb("mask", [P, NT * s.RULES], BF16)
        self.first = sb("first", [P, NT * 64], BF16)
        self.second = sb("second", [P, NT * 64], BF16)
        self.spread = sb("spread", [P, W])
        self.place = sb("place", [P, W])
        self.count = sb("count", [P, NT])
        self.prefix = sb("prefix", [P, NT])
        self.ones_nt = sb("ones_nt", [P, NT])
        self.blocks_f = sb("blocks_f", [P, 4])
        self.blocks_i = sb("blocks_i", [P, 2], I32)
        self.offset = sb("offset", [P, NT])
        self.ended = sb("ended", [P, 256])
        self.owner_f = sb("owner_f", [1, 256])
        self.owner_i = sb("owner_i", [1, 256], I32)
        self.pos_f = sb("pos_f", [P, 2, NT])
        self.pos_i = sb("pos_i", [P, 2, NT], I32)
        self.h = sb("h", [P, NT, C])
        self.xc = sb("xc", [P, NT, C])
        self.sq = sb("sq", [P, NT, C])
        self.msg = sb("msg", [P, NT, C])
        self.mean = sb("mean", [P, NT])
        self.var = sb("var", [P, NT])
        self.std = sb("std", [P, NT])
        self.rstd = sb("rstd", [P, NT])
        self.eps = sb("eps", [P, 1])
        self.xb = [sb(f"xb{k}", [P, TURN, C]) for k in range(DEPTH)]
        self.xT = [sb(f"xT{k}", [P, TURN, P]) for k in range(2)]
        self.w1 = [sb(f"w1_{k}", [C + 1, TURN, P]) for k in range(2)]
        self.hT = [sb(f"hT{k}", [P, TURN, P]) for k in range(2)]
        self.y64 = [t[0:C, :, :].rearrange("p k (f c) -> p (k f) c", f=2) for t in self.hT]
        self.yb = [sb(f"yb{k}", [P, TURN, C]) for k in range(2)]
        late = sb("late", [P, s.EXPERTS * s.HID])
        self.rules = late[:, 0:s.RULES * C].rearrange("d (r c) -> d r c", c=C)
        self.hist = late[0:C, 0:T]
        self.w1_all = late[0:C + 1, :].rearrange("d (e h) -> d e h", h=s.HID)
        self.w2_all = sb("w2_all", [P, s.EXPERTS, C])
        self.b2_all = sb("b2_all", [s.EXPERTS, C])
        self.gT = [sb(f"gT{k}", [s.EXPERTS, 4 * P]) for k in range(2)]
        self.qkv = sb("qkv", [C + 1, 3 * C])
        self.fold = sb("fold", [C + 1, C + 1])
        self.g1 = sb("g1", [C, 1])
        self.b1 = sb("b1", [C, 1])
        self.wp = sb("wp", [C, C])
        self.qkvT = [sb(f"qkvT{k}", [C, C + 1]) for k in range(3)]
        self.mqk = [sb("mqk0", [C + 1, C + 1]), sb("mqk1", [C, C])]
        self.wvp = sb("wvp", [C + 1, C])
        self.hankel = sb("hankel", [P, 3 * P])
        self.relbias = sb("relbias", [P, 3 * P])
        self.scale = sb("scale", [P, 1])
        self.pbias = sb("pbias", [P, C])
        self.g2 = sb("g2", [P, C])
        self.b2ln = sb("b2ln", [P, C])
        self.an = [sb(f"an{k}", [P, 2, C]) for k in range(SLOTS)]
        self.aT = [sb(f"aT{k}", [C + 1, 2 * P]) for k in range(SLOTS)]
        self.qT = [sb(f"qT{k}", [C + 1, 2 * P]) for k in range(SLOTS)]
        self.v = [sb(f"v{k}", [P, 2, C]) for k in range(SLOTS)]
        self.stat = [sb(f"stat{k}", [P, 8]) for k in range(SLOTS)]
        weights = self.place[:, 0:SLOTS * 8 * P].rearrange("p (w k j n) -> p w k j n", w=2, k=SLOTS, j=2)
        self.pr = [weights[:, 0, k] for k in range(SLOTS)]
        self.pT = [weights[:, 1, k] for k in range(SLOTS)]
        self.wraw = [sb(f"wraw{k}", [P, 2, C]) for k in range(2)]
        self.wi = sb("wi", [C + 1, 4 * C])
        self.wh = sb("wh", [P, 4 * C])
        self.bsum = sb("bsum", [C + 1, 2, 4 * C])
        self.wlin = sb("wlin", [C, 2])
        self.wlinb = sb("wlinb", [C, 2, C])
        self.blin = sb("blin", [C, 2])
        self.fwbw = sb("fwbw", [C, 4])
        self.xseq = sb("xseq", [C + 1, T + AHEAD * B])
        self.ring = sb("ring", [P, RING, B])
        self.forget = sb("forget", [C, B])
        self.emit = sb("emit", [C, B])
        self.factors = sb("factors", [C, B, 2])
        self.terms = sb("terms", [C, B, 2])
        self.cells = sb("cells", [C, B, 2])
        self.tanc = sb("tanc", [C, B])
        part = lambda k: self.gT[0][:, k * AHEAD * B:(k + 1) * AHEAD * B].rearrange("c (b t) -> c b t", b=B)
        self.twice, self.gt = part(0), part(1)
        self.share = part(2)
        self.lg0 = self.gT[1][:, 0:AHEAD * B]
        self.keep = sb("keep", [C, B, 1 + AHEAD])
        self.add = sb("add", [C, B, 1 + AHEAD])
        self.sums = sb("sums", [C, B, 1 + AHEAD])
        self.ta, self.tb = self.place[0:C, 0:T], self.spread[0:C, 0:T]
        self.wr = sb("wr", [C + 1, s.EXPERTS])
        self.logits = self.place[:, 0:NT * s.EXPERTS].rearrange("p (t e) -> p t e", t=NT)
        self.top = sb("top", [P, NT, 8])
        self.topi = sb("topi", [P, NT, 8], U32)
        self.topf = sb("topf", [P, NT, 2])
        self.gate = sb("gate", [P, 2, NT])
        self.gtmp = sb("gtmp", [P, 3, NT])
        self.step, self.steps = self.sem("vector_step"), 0
        self.zeroed = self.sem("zeroed")
        self.loaded_rules = self.sem("loaded_rules")
        self.loaded_experts = self.sem("loaded_experts")
        self.loaded_w = self.sem("loaded_w")

    def sem(self, name):
        return self.ctx.enter_context(self.nc.semaphore(name))


def constants_and_ids(nc, m, s, ins):
    loaded = m.sem("ids_loaded")
    made, built = m.sem("const_made"), m.sem("const_built")
    turned = m.sem("ids_turned")
    with nc.Block() as block:

        @block.gpsimd
        def _(pool):
            nc.gpsimd.memset(m.ident[:], 0.0).then_inc(made, 1)
            nc.gpsimd.memset(m.anti[:], 0.0).then_inc(made, 1)
            nc.gpsimd.memset(m.upto[:], 1.0).then_inc(made, 1)
            nc.gpsimd.memset(m.before_b[:], 1.0).then_inc(made, 1)
            pool.wait_ge(made, 4)
            for mat, cmp, fill, base, mult, step_ in (
                    (m.ident, ALU.not_equal, 1.0, 0, 1, -1), (m.anti, ALU.not_equal, 1.0, -(P - 1), 1, 1),
                    (m.upto, ALU.is_ge, 0.0, 0, -1, 1), (m.before_b, ALU.is_gt, 0.0, 0, -1, 1)):
                nc.gpsimd.affine_select(out=mat[:], in_=mat[:], compare_op=cmp, fill=fill, base=base,
                                        pattern=[[step_, P]], channel_multiplier=mult).then_inc(built, 1)
            nc.gpsimd.iota(m.iota[:], pattern=[[1, 256]], base=0, channel_multiplier=0,
                           allow_small_or_imprecise_dtypes=True).then_inc(built, 1)

        @block.sync
        def _(sp):
            sp.dma_start(m.ids[:], ins["x"].rearrange("b (h p) -> (b h) p", p=P)).then_inc(loaded, 16)

        @block.vector
        def _(dve):
            link = Link(dve, m)
            dve.wait_ge(loaded, 16)
            link(nc.vector.tensor_copy(m.ids_f[:], m.ids[:]))
            link(nc.vector.tensor_scalar(m.ids_neg[:], m.ids_f[:], 0.0, float(s.VOCAB), ALU.is_lt, ALU.mult))
            link(nc.vector.tensor_tensor(m.ids_f[:], m.ids_f[:], m.ids_neg[:], ALU.add))
            link(nc.vector.tensor_scalar(m.ids_f[:], m.ids_f[:], 0.0, float(s.VOCAB - 1), ALU.max, ALU.min))
            dve.wait_ge(turned, 1)
            nc.vector.tensor_copy(m.id_col[:], m.bank[0][:, 0:s.NT]).then_inc(turned, 1)

        @block.tensor
        def _(pe):
            pe.wait_ge(m.step, 4)
            pe.wait_ge(built, 5)
            nc.tensor.transpose(m.bank[0][:, 0:s.NT], m.ids_f[:], m.ident[0:s.NT, 0:s.NT]).then_inc(turned, 1)


def prepare_weights_pe(nc, m, s, pe, pe_done, cp):
    C, bank = s.C, m.bank
    pe.wait_ge(m.loaded_w, 16 * m.n_loads)
    nc.tensor.matmul(bank[1][:, 0:3 * P], m.anti[:], m.hankel[:], start=True, stop=True).then_inc(pe_done, 1)
    for w in range(2):
        for k in range(2):
            nc.tensor.transpose(bank[2 + w][0:C, k * P:(k + 1) * P], m.wraw[w][:, k, :], m.ident[:]).then_inc(pe_done, 1)
    pe.wait_ge(cp, 1)
    for k in range(3):
        nc.tensor.matmul(bank[4][0:C, k * 65:(k + 1) * 65], m.qkv[:, k * C:(k + 1) * C], m.fold[:],
                         start=True, stop=True, skip_group_check=True).then_inc(pe_done, 1)
    pe.wait_ge(cp, 2)
    nc.tensor.matmul(bank[5][0:C + 1, 0:C + 1], m.qkvT[0][:], m.qkvT[1][:], start=True, stop=True).then_inc(pe_done, 1)
    nc.tensor.matmul(bank[6][0:C + 1, 0:C], m.qkvT[2][:], m.wp[:], start=True, stop=True).then_inc(pe_done, 1)


def prepare_weights_dve(nc, m, s, dve, pe_done, cp):
    C, bank = s.C, m.bank
    link = Link(dve, m)
    dve.wait_ge(m.loaded_w, 16 * m.n_loads)
    link(nc.vector.tensor_copy(m.fold[C:C + 1, :], m.ident[C:C + 1, 0:C + 1]))
    link(nc.vector.tensor_scalar(m.fold[0:C, 0:C], m.ident[0:C, 0:C], m.g1[:, 0:1], None, ALU.mult))
    nc.vector.tensor_copy(m.fold[0:C, C:C + 1], m.b1[:]).then_inc(cp, 1)
    dve.wait_ge(pe_done, 1)
    link(nc.vector.tensor_copy(m.relbias[:], bank[1][:, 0:3 * P]))
    dve.wait_ge(pe_done, 8)
    for k in range(3):
        ins_ = nc.vector.tensor_copy(m.qkvT[k][:], bank[4][0:C, k * 65:(k + 1) * 65])
        if k < 2:
            link(ins_)
    ins_.then_inc(cp, 1)
    link(nc.vector.tensor_tensor(m.bsum[C:C + 1, 0, :], m.bsum[C:C + 1, 0, :], m.bsum[C:C + 1, 1, :], ALU.add))
    for q, r in enumerate((1, 0, 2, 3)):
        link(nc.vector.tensor_copy(m.wi[0:C, q * C:(q + 1) * C], bank[2][0:C, r * C:(r + 1) * C]))
        link(nc.vector.tensor_copy(m.wh[0:C, q * C:(q + 1) * C], bank[3][0:C, r * C:(r + 1) * C]))
        link(nc.vector.tensor_copy(m.wi[C:C + 1, q * C:(q + 1) * C], m.bsum[C:C + 1, 0, r * C:(r + 1) * C]))
    for l in range(2):
        link(nc.vector.tensor_scalar(m.wlinb[:, l, :], m.ones[0:C, 0:C], m.wlin[:, l:l + 1], None, ALU.mult))
    link(nc.vector.tensor_scalar(m.fwbw[:, 2:3], m.fwbw[:, 0:1], 0.5, None, ALU.mult))
    link(nc.vector.tensor_scalar(m.fwbw[:, 3:4], m.fwbw[:, 1:2], -0.5, None, ALU.mult))
    dve.wait_ge(pe_done, 10)
    link(nc.vector.tensor_copy(m.mqk[0][:], bank[5][0:C + 1, 0:C + 1]))
    link(nc.vector.tensor_copy(m.wvp[:], bank[6][0:C + 1, 0:C]))


def gather_and_prepare(nc, m, s, ins):
    NT, R = s.NT, s.RULES
    rules_got, m.tokens_got = m.sem("rules_gathered"), m.sem("tokens_gathered")
    filled = m.sem("filled")
    routing = Routing(m, s, R, s.RULE_ROWS, s.RULE_BLOCKS, "rule", m.mask[:, 0:NT * R])
    with nc.Block() as block:

        @block.gpsimd
        def _(pool):
            for t in range(NT):
                index = bass.IndirectOffsetOnAxis(ap=m.id_col[:, t:t + 1], axis=0)
                pool.indirect_dma_start(m.rule_i[:, t:t + 1], None, col(ins["L0_tok_token_rules"]), index).then_inc(rules_got, 16)
            for t in range(NT):
                index = bass.IndirectOffsetOnAxis(ap=m.id_col[:, t:t + 1], axis=0)
                pool.indirect_dma_start(m.h[:, t, :], None, ins["L0_tok_base_embeddings"], index).then_inc(m.tokens_got, 16)

        @block.sync
        def _(sp):
            loads = [(m.qkv[0:s.C, :], ins["L0_attn_qkv_w"]), (m.qkv[s.C:s.C + 1, :], row(ins["L0_attn_qkv_b"])),
                     (m.wp[:], ins["L0_attn_proj_w"]), (m.mqk[1][:], ins["L1_attn_W"]),
                     (m.g1[:], col(ins["L0_attn_ln1_g"])), (m.b1[:], col(ins["L0_attn_ln1_b"])),
                     (m.hankel[:], view(ins["L0_attn_bias_table"], 0, [[1, P], [1, 3 * P]])),
                     (m.scale[:], view(ins["L0_attn_scale"], 0, [[0, P], [1, 1]])),
                     (m.pbias[:], view(ins["L0_attn_proj_b"], 0, [[0, P], [1, s.C]])),
                     (m.g2[:], view(ins["L0_attn_ln2_g"], 0, [[0, P], [1, s.C]])),
                     (m.b2ln[:], view(ins["L0_attn_ln2_b"], 0, [[0, P], [1, s.C]])),
                     (m.wraw[0][:], ins["L0_ffn_W_ih"].rearrange("(k p) c -> p k c", p=P)),
                     (m.wraw[1][:], ins["L0_ffn_W_hh"].rearrange("(k p) c -> p k c", p=P)),
                     (m.bsum[s.C:s.C + 1, 0, :], row(ins["L0_ffn_b_ih"])),
                     (m.bsum[s.C:s.C + 1, 1, :], row(ins["L0_ffn_b_hh"])),
                     (m.blin[:], view(ins["L0_ffn_b_lin"], 0, [[0, s.C], [1, 2]])),
                     (m.wlin[:, 0:1], view(ins["L0_ffn_W_lin"], 0, [[1, s.C], [1, 1]])),
                     (m.wlin[:, 1:2], view(ins["L0_ffn_W_lin"], s.C, [[1, s.C], [1, 1]])),
                     (m.fwbw[:, 0:1], view(ins["L0_ffn_fw_att"], 0, [[1, s.C], [1, 1]])),
                     (m.fwbw[:, 1:2], view(ins["L0_ffn_bw_att"], 0, [[1, s.C], [1, 1]])),
                     (m.wr[0:s.C, :], ins["L1_ffn_Wr"]), (m.wr[s.C:s.C + 1, :], row(ins["L1_ffn_br"]))]
            for dst, src in loads:
                sp.dma_start(dst, src).then_inc(m.loaded_w, 16)
            m.n_loads = len(loads)
            sp.wait_ge(rules_got, 16 * NT)
            sp.dma_start(m.rules[0:s.C, :, :], ins["L0_tok_rule_transform"].rearrange("r d c -> d r c")).then_inc(m.loaded_rules, 16)

        @block.scalar
        def _(act):
            act.wait_ge(filled, 1)
            act.wait_ge(rules_got, 16 * NT)
            quarters = m.rows_in.ap()[0:s.RULE_ZEROS, :].rearrange("(q p r) c -> q p (r c)", p=P, q=4)
            for q in range(4):
                act.dma_start(quarters[q], m.place[:, 0:s.RULE_ZEROS * s.C // P // 4]).then_inc(m.zeroed, 16)

        @block.tensor
        def _(pe):
            pe.wait_ge(routing.masked, 1)
            count_choices(nc, m, s, routing, range(NT))
            route_pe(nc, m, s, pe, routing)

        @block.vector
        def _(dve):
            nc.vector.memset(m.place[:], 0.0).then_inc(filled, 1)
            nc.vector.memset(m.ones[:], 1.0).then_inc(filled, 1)
            nc.vector.memset(m.eps[:], EPS).then_inc(filled, 1)
            nc.vector.memset(m.ones_b[:], 1.0).then_inc(filled, 1)
            nc.vector.memset(m.ones_nt[:], 1.0).then_inc(filled, 1)
            for k in range(SLOTS):
                nc.vector.memset(m.aT[k][s.C:s.C + 1, :], 1.0).then_inc(filled, 1)
            for k in range(2):
                nc.vector.memset(m.xT[k][s.C:P, :, :], 1.0).then_inc(filled, 1)
            nc.vector.memset(m.rules[s.C:P, :, :], 0.0).then_inc(filled, 1)
            nc.vector.memset(m.xseq[:], 1.0).then_inc(filled, 1)
            nc.vector.memset(m.factors[:], 0.0).then_inc(filled, 1)
            nc.vector.memset(m.add[:], 0.0).then_inc(filled, 1)
            nc.vector.memset(m.keep[:, :, 0:1], 0.0).then_inc(filled, 1)
            nc.vector.memset(m.keep[:, :, 1:], 1.0).then_inc(filled, 1)
            nc.vector.memset(m.cells[:], 0.0).then_inc(filled, 1)
            nc.vector.memset(m.wh[s.C:P, :], 0.0).then_inc(filled, 1)
            nc.vector.memset(m.ring[:], 0.0).then_inc(filled, 1)
            link = Link(dve, m)
            dve.wait_ge(rules_got, 16 * NT)
            link(nc.vector.tensor_copy(m.rule_f[:], m.rule_i[:]))
            shape = [P, NT, R]
            mask = m.mask[:, 0:NT * R]
            nc.vector.tensor_tensor(mask.rearrange("p (t r) -> p t r", t=NT), m.rule_f[:].unsqueeze(2).to_broadcast(shape),
                                    m.iota[:, 0:R].unsqueeze(1).to_broadcast(shape), ALU.is_equal).then_inc(routing.masked, 1)
            dve.wait_ge(routing.masked, 1)
            route_dve(nc, m, s, dve, routing)


class Routing:

    def __init__(self, m, s, E, rows, n_blocks, tag, mask, which=0, first_block=0, count_bank=0):
        self.count_bank = m.bank[count_bank]
        self.E, self.rows, self.n_blocks, self.tag, self.mask = E, rows, n_blocks, tag, mask
        self.which, self.first_block = which, first_block
        self.masked, self.counted, self.laid, self.placed, self.done = (
            m.sem(f"{tag}_{x}") for x in ("masked", "counted", "laid", "placed", "placed_read"))
        group = 512 // E if 512 // E < 8 else 8
        while s.NT % group:
            group -= 1
        self.groups = s.NT // group
        self.W = group * E


def count_choices(nc, m, s, r, tiles):
    for t in tiles:
        ins = nc.tensor.matmul(r.count_bank[0:r.E, t:t + 1], r.mask[:, t * r.E:(t + 1) * r.E], m.ones_b[:, 0:1],
                               start=True, stop=True, skip_group_check=True)
    if t == s.NT - 1:
        ins.then_inc(r.counted, 1)


def route_pe(nc, m, s, pe, r):
    NT, E, rows, n_blocks, groups, W = s.NT, r.E, r.rows, r.n_blocks, r.groups, r.W
    counted, laid, placed, done = r.counted, r.laid, r.placed, r.done
    mask = r.mask
    pe.wait_ge(laid, 1)
    nc.tensor.matmul(m.bank[1][0:E, 0:1], m.upto[0:E, 0:E], m.blocks_f[0:E, 0:1], start=True, stop=True).then_inc(counted, 1)
    pe.wait_ge(laid, 2)
    nc.tensor.matmul(m.bank[2][0:1, 0:n_blocks], m.ones[0:E, 0:1], m.ended[0:E, 0:n_blocks], start=True, stop=True).then_inc(counted, 1)
    for g in range(groups):
        pe.wait_ge(laid, g + 3)
        if g >= 2:
            pe.wait_ge(done, g - 1)
        b = m.bank[4 + g % 2]
        nc.tensor.matmul(b[:, 0:W], m.before_b[:], mask[:, g * W:(g + 1) * W], start=True, stop=False)
        nc.tensor.matmul(b[:, 0:W], m.ones[0:E, :], m.spread[0:E, g * W:(g + 1) * W], start=False, stop=True).then_inc(placed, 1)


def route_dve(nc, m, s, dve, r):
    NT, E, rows, n_blocks, groups, W = s.NT, r.E, r.rows, r.n_blocks, r.groups, r.W
    counted, laid, placed, done = r.counted, r.laid, r.placed, r.done
    diag = m.spread[0:E, 0:NT * E].rearrange("e (t f) -> e t f", t=NT)

    def add_positions(g):
        dve.wait_ge(done, g + 1)
        n = NT // groups
        link(nc.vector.tensor_reduce(m.pos_f[:, r.which, g * n:(g + 1) * n],
                                     m.place[:, g * W:(g + 1) * W].rearrange("p (t e) -> p t e", t=n), AX, ALU.add))

    shift = rows.bit_length() - 1
    link = Link(dve, m)
    dve.wait_ge(counted, 1)
    link(nc.vector.tensor_copy(m.count[0:E, :], r.count_bank[0:E, 0:NT]))
    link(nc.vector.tensor_tensor_scan(m.prefix[0:E, :], m.ones_nt[0:E, :], m.count[0:E, :], 0.0, ALU.mult, ALU.add))
    link(nc.vector.tensor_scalar(m.blocks_i[0:E, 0:1], m.prefix[0:E, NT - 1:NT], float(rows - 1), None, ALU.add))
    link(nc.vector.tensor_scalar(m.blocks_i[0:E, 1:2], m.blocks_i[0:E, 0:1], shift, None, ALU.arith_shift_right))
    nc.vector.tensor_copy(m.blocks_f[0:E, 0:1], m.blocks_i[0:E, 1:2]).then_inc(laid, 1)
    dve.wait_ge(counted, 2)
    link(nc.vector.tensor_copy(m.blocks_f[0:E, 1:2], m.bank[1][0:E, 0:1]))
    nc.vector.tensor_scalar(m.ended[0:E, 0:n_blocks], m.iota[0:E, 0:n_blocks], m.blocks_f[0:E, 1:2], None, ALU.is_ge).then_inc(laid, 1)
    link(nc.vector.tensor_tensor(m.blocks_f[0:E, 2:3], m.blocks_f[0:E, 1:2], m.blocks_f[0:E, 0:1], ALU.subtract))
    link(nc.vector.tensor_scalar(m.blocks_f[0:E, 3:4], m.blocks_f[0:E, 2:3], float(rows), float(r.first_block * rows), ALU.mult, ALU.add))
    link(nc.vector.tensor_tensor(m.offset[0:E, :], m.prefix[0:E, :], m.count[0:E, :], ALU.subtract))
    link(nc.vector.tensor_scalar(m.offset[0:E, :], m.offset[0:E, :], m.blocks_f[0:E, 3:4], None, ALU.add))
    for g in range(groups):
        n = NT // groups
        t = slice(g * n, (g + 1) * n)
        nc.vector.tensor_tensor(diag[:, t, :], m.ident[0:E, 0:E].unsqueeze(1).to_broadcast([E, n, E]),
                                m.offset[0:E, t].unsqueeze(2).to_broadcast([E, n, E]), ALU.mult).then_inc(laid, 1)
    dve.wait_ge(counted, 3)
    link(nc.vector.tensor_scalar(m.owner_f[:, 0:n_blocks], m.bank[2][0:1, 0:n_blocks], float(E - 1), None, ALU.min))
    link(nc.vector.tensor_copy(m.owner_i[:, r.first_block:r.first_block + n_blocks], m.owner_f[:, 0:n_blocks]))
    dve.wait_ge(m.zeroed, 4 * 16)
    for g in range(groups):
        dve.wait_ge(placed, g + 1)
        now = slice(g * W, (g + 1) * W)
        nc.vector.tensor_tensor(m.place[:, now], r.mask[:, now], m.bank[4 + g % 2][:, 0:W], ALU.mult).then_inc(done, 1)
        if g > 0:
            add_positions(g - 1)
    add_positions(groups - 1)
    link(nc.vector.tensor_copy(m.pos_i[:, r.which, :], m.pos_f[:, r.which, :]))


def turn_rows(rows, turn):
    return rows[bass.ds(turn * (TURN * P), TURN * P), :].rearrange("(k p) c -> p k c", p=P)


def load_turns(sp, m, turns, x_in, turned, first_part=None, later=None, later_count=0):
    rows_in = m.rows_in.ap()
    depth = len(x_in)
    for j in range(depth):
        sp.dma_start(m.xb[j][:], turn_rows(rows_in, j)).then_inc(x_in[j], 16)
    split = first_part // depth - 1 if first_part else 0
    for part in ((0, split), (split, turns // depth)):
        if part[0] == part[1]:
            continue
        if part[0] > 0:
            sp.wait_ge(later, later_count)
        with sp.Fori(*part) as i:
            for j in range(depth):
                sp.wait_ge(turned, i * depth + (j + 1))
                sp.dma_start(m.xb[j][:], turn_rows(rows_in, i * depth + (j + depth))).then_inc(x_in[j], 16)
    for j in range(depth):
        sp.wait_ge(x_in[j], 16 * (turns // depth + 1))


def warm(nc, m, count):
    for w in range(count):
        nc.tensor.matmul(m.bank[7][:], m.ones_b[:], m.mask[:, 0:512], start=True, stop=True)


def transpose_turn(nc, m, j, rows, turned):
    for a in range(TURN // 2):
        ins = nc.tensor.transpose(m.bank[j][:, a * P:(a + 1) * P], rows[:, 2 * a:2 * a + 2, :].rearrange("p k c -> p (k c)"),
                                  m.ident[:])
    ins.then_inc(turned, 1)


def copy_turn(nc, m, s, j, copied):
    for odd in range(2):
        src = m.bank[j][odd * s.C:(odd + 1) * s.C, 0:2 * P].rearrange("c (a p) -> c a p", a=2)
        nc.scalar.copy(m.xT[j][0:s.C, odd:TURN:2, :], src).then_inc(copied, 1)


def rule_blocks(nc, m, s, ins):
    NT, C = s.NT, s.C
    turns = s.rule_turns
    scattered = m.sem("rule_scattered")
    x_in = [m.sem(f"rule_x{k}") for k in range(2)]
    y_out = [m.sem(f"rule_y{k}") for k in range(2)]
    turned, copied, multiplied, kept = (m.sem(f"rule_{x}") for x in ("turned", "copied", "multiplied", "kept"))
    prep_done, prep_copied = m.sem("prep_product"), m.sem("prep_copied")
    rows_in, rows_out = m.rows_in.ap(), m.rows_out.ap()
    with nc.Block() as block:

        @block.gpsimd
        def _(pool):
            pool.wait_ge(m.tokens_got, 16 * NT)
            pool.wait_ge(m.zeroed, 4 * 16)
            for t in range(NT):
                index = bass.IndirectOffsetOnAxis(ap=m.pos_i[:, 0, t:t + 1], axis=0)
                pool.indirect_dma_start(rows_in, index, m.h[:, t, :], None).then_inc(scattered, 16)

        @block.sync
        def _(sp):
            sp.wait_ge(scattered, 16 * NT)
            load_turns(sp, m, turns, x_in, turned)

        @block.tensor
        def _(pe):
            prepare_weights_pe(nc, m, s, pe, prep_done, prep_copied)
            pe.wait_ge(m.loaded_rules, 16)
            for j in range(2):
                pe.wait_ge(x_in[j], 16)
                transpose_turn(nc, m, j, m.xb[j], turned)
            with pe.Fori(0, turns // 2) as i:
                for j in range(2):
                    owners = load_owners(nc, mybir.EngineType.PE, m, i * (4 * TURN) + 2 * TURN * j, 2 * TURN, s.RULES)
                    pe.wait_ge(copied, i * 4 + (2 * j + 2))
                    pe.wait_ge(kept, i * 2 + (j + 1))
                    for k in range(TURN):
                        for half in range(2):
                            e = owners[2 * k + half]
                            ins_ = nc.tensor.matmul(m.bank[2 + j][0:C, (2 * k + half) * C:(2 * k + half + 1) * C],
                                                    m.xT[j][:, k, half * C:(half + 1) * C],
                                                    m.rules[:, bass.ds(e, 1), :].rearrange("d a c -> d (a c)"), start=True, stop=True)
                    ins_.then_inc(multiplied, 1)
                    pe.wait_ge(x_in[j], i * 16 + 32)
                    transpose_turn(nc, m, j, m.xb[j], turned)

        @block.scalar
        def _(act):
            for j in range(2):
                act.wait_ge(turned, j + 1)
                copy_turn(nc, m, s, j, copied)
            with act.Fori(0, turns // 2) as i:
                for j in range(2):
                    act.wait_ge(multiplied, i * 2 + (j + 1))
                    act.wait_ge(turned, i * 2 + (j + 3))
                    copy_turn(nc, m, s, j, copied)
                    act.wait_ge(kept, i * 2 + (j + 3))
                    rows = rows_out[bass.ds((i * 2 + j) * s.TURN_ROWS, s.TURN_ROWS), :]
                    act.dma_start(rows.rearrange("(k p) c -> p k c", p=s.RULE_ROWS), m.y64[j][:]).then_inc(y_out[j], 16)
            for j in range(2):
                act.wait_ge(y_out[j], 16 * (turns // 2 + 1))

        @block.vector
        def _(dve):
            prepare_weights_dve(nc, m, s, dve, prep_done, prep_copied)
            dve.sem_inc(kept, 2)
            for j in range(2):
                dve.sem_inc(y_out[j], 16)
            with dve.Fori(0, turns // 2) as i:
                for j in range(2):
                    dve.wait_ge(multiplied, i * 2 + (j + 1))
                    dve.wait_ge(y_out[j], i * 16 + 16)
                    nc.vector.tensor_copy(m.y64[j][:], m.bank[2 + j][0:C, :].rearrange("p (k c) -> p k c", k=2 * TURN)).then_inc(kept, 1)


def centre(nc, m, s, link, x, tiles, part):
    C = s.C
    mean, xc, sq = m.mean[:, tiles], m.xc[:, tiles, :], m.sq[:, tiles, :]
    if part == 0:
        link(nc.vector.tensor_reduce(mean, x[:, tiles, :], AX, ALU.add))
        link(nc.vector.tensor_scalar(mean, mean, 1.0 / C, None, ALU.mult))
    if part == 1:
        link(nc.vector.tensor_tensor(xc, x[:, tiles, :], mean.unsqueeze(2).to_broadcast(list(xc.shape)), ALU.subtract))
    if part == 2:
        link(nc.vector.tensor_tensor(sq, xc, xc, ALU.mult))
    if part == 3:
        link(nc.vector.tensor_reduce(mean, sq, AX, ALU.add))


def normalised_twice(nc, m, s, dve, link, tiles, step, ready, rooted):
    C = s.C
    mean, var, std, rstd = m.mean[:, tiles], m.var[:, tiles], m.std[:, tiles], m.rstd[:, tiles]
    if step == 0:
        link(nc.vector.tensor_scalar(mean, mean, 1.0 / C, None, ALU.mult))
        nc.vector.tensor_scalar(var, mean, EPS, None, ALU.add).then_inc(ready, 1)
    if step == 1:
        link(nc.vector.reciprocal(rstd, std))
        link(nc.vector.tensor_tensor(mean, mean, rstd, ALU.mult))
        link(nc.vector.tensor_tensor(mean, mean, rstd, ALU.mult))
        nc.vector.tensor_scalar(var, mean, EPS, None, ALU.add).then_inc(ready, 1)
    if step == 2:
        link(nc.vector.reciprocal(mean, std))
        link(nc.vector.tensor_tensor(rstd, rstd, mean, ALU.mult))


class Norm:

    def __init__(self, m, s, x, tag):
        self.m, self.s, self.x = m, s, x
        self.centred, self.squared, self.summed, self.rooted, self.scaled = (
            m.sem(f"{tag}_{n}") for n in ("centred", "squared", "summed", "root", "scaled"))
        self.wide = [P, GROUP, s.C]

    def open(self, nc, link, g):
        m, t = self.m, tiles_of(g)
        link(nc.vector.tensor_reduce(m.mean[:, t], self.x[:, t, :], AX, ALU.add))
        nc.vector.scalar_tensor_tensor(out=m.xc[:, t, :], in0=m.mean[:, t].unsqueeze(2).to_broadcast(self.wide), scalar=1.0 / self.s.C,
                                       in1=self.x[:, t, :], op0=ALU.mult, op1=ALU.subtract).then_inc(self.centred, 1)

    def square(self, nc, act, g):
        m, t = self.m, tiles_of(g)
        act.wait_ge(self.centred, g + 1)
        nc.scalar.activation(m.sq[:, t, :], m.xc[:, t, :], ACT.Square).then_inc(self.squared, 1)

    def close(self, nc, dve, g):
        m, t = self.m, tiles_of(g)
        dve.wait_ge(self.squared, g + 1)
        nc.vector.tensor_reduce(m.var[:, t], m.sq[:, t, :], AX, ALU.add).then_inc(self.summed, 1)

    def root(self, nc, act, g):
        m, t = self.m, tiles_of(g)
        act.wait_ge(self.summed, g + 1)
        nc.scalar.activation(m.std[:, t], m.var[:, t], ACT.Sqrt, bias=m.eps[:, 0:1], scale=1.0 / self.s.C).then_inc(self.rooted, 1)

    def finish(self, nc, dve, link, g, scale):
        m, t = self.m, tiles_of(g)
        dve.wait_ge(self.rooted, g + 1)
        link(nc.vector.reciprocal(m.rstd[:, t], m.std[:, t]))
        if scale:
            nc.vector.scalar_tensor_tensor(out=m.xc[:, t, :], in0=m.xc[:, t, :], scalar=-1.0,
                                           in1=m.rstd[:, t].unsqueeze(2).to_broadcast(self.wide), op0=ALU.mult,
                                           op1=ALU.mult).then_inc(self.scaled, 1)
        else:
            link(nc.vector.tensor_scalar(m.rstd[:, t], m.rstd[:, t], -1.0, None, ALU.mult))


def tiles_of(g):
    return slice(g * GROUP, (g + 1) * GROUP)


def attention(nc, m, s, ins, layer):
    C, NT = s.C, s.NT
    K = C + 1 if layer == 0 else C
    norm = 1.0 if layer == 0 else 1.0 / float(C) ** 0.5
    tag = f"att{layer}"
    scaled, tA, eA, mQ, eQ, eV, mS, eM, xp, tP, eP, mO, rc, eO = (
        m.sem(f"{tag}_{x}") for x in ("scaled", "turned", "a_copied", "q_made", "q_copied", "v_copied",
                                      "scored", "maxed", "exped", "p_turned", "p_copied", "mixed", "recip", "kept"))
    mqk = m.mqk[layer]
    narrow, wide = m.bank[0:SLOTS], m.bank[SLOTS:2 * SLOTS]
    turned_at, q_at, v_at = slice(0, P), slice(P, 3 * P), slice(3 * P, 4 * P)
    slots = range(SLOTS)
    turns = s.B // SLOTS
    assert 2 * SLOTS == GROUP
    back = [m.sem(f"{tag}_back{g}") for g in range(turns)] if layer == 0 else []
    ready, rooted, normed = (m.sem(f"{tag}_{x}") for x in ("var", "root", "normed"))

    def each_turn(engine, turn):
        if layer == 0:
            for i in range(turns):
                turn(i)
        else:
            with engine.Fori(0, turns) as i:
                turn(i)

    def n(i, k):
        return i * SLOTS + (k + 1)

    with nc.Block() as block:

        @block.sync
        def _(sp):
            if layer == 0:
                sp.wait_ge(back[turns - 1], 16 * GROUP)
                sp.dma_start(m.w2_all[:], ins["L1_ffn_W2"].rearrange("e h c -> h e c")).then_inc(m.loaded_experts, 16)
                sp.dma_start(m.b2_all[:], ins["L1_ffn_b2"]).then_inc(m.loaded_experts, 16)
            else:
                sp.dma_start(m.w1_all[0:C, :, :], ins["L1_ffn_W1"].rearrange("e d h -> d e h")).then_inc(m.loaded_experts, 16)
                sp.dma_start(m.w1_all[C:C + 1, :, :], ins["L1_ffn_b1"].rearrange("(a e) h -> a e h", a=1)).then_inc(m.loaded_experts, 16)

        @block.gpsimd
        def _(pool):
            def gather(g):
                for t in range(g * GROUP, (g + 1) * GROUP):
                    index = bass.IndirectOffsetOnAxis(ap=m.pos_i[:, 0, t:t + 1], axis=0)
                    pool.indirect_dma_start(m.h[:, t, :], None, m.rows_out.ap()[0:s.rule_turns * s.TURN_ROWS, :], index).then_inc(back[g], 16)

            def turn(i):
                if layer == 0:
                    pool.wait_ge(normed, i + 1)
                for k in slots:
                    pool.wait_ge(mO, n(i, k))
                    tiles = bass.ds(i * (2 * SLOTS) + 2 * k, 2)
                    nc.gpsimd.tensor_tensor(m.an[k][:], m.xc[:, tiles, :], m.rstd[:, tiles].unsqueeze(2).to_broadcast([P, 2, C]),
                                            ALU.mult).then_inc(scaled, 1)
                if layer == 0 and i + 2 < turns:
                    gather(i + 2)

            pool.sem_inc(mO, SLOTS)
            if layer == 0:
                gather(0)
                gather(1)
            each_turn(pool, turn)

        @block.tensor
        def _(pe):
            pe.wait_ge(scaled, 1)
            for w in range(2 * WARMERS):
                nc.tensor.matmul(wide[0][:], m.ones_b[:], m.mask[:, 0:512], start=True, stop=True)
            with pe.Fori(0, s.B // SLOTS) as i:
                for k in slots:
                    pe.wait_ge(scaled, n(i, k))
                    pe.wait_ge(eO, n(i, k))
                    nc.tensor.transpose(narrow[k][:, turned_at], m.an[k][:].rearrange("p j c -> p (j c)"), m.ident[:]).then_inc(tA, 1)
                for k in slots:
                    wait_apart(pe, eA, i * (2 * SLOTS) + (2 * k + 2))
                    ins = nc.tensor.matmul(narrow[k][0:K, q_at], mqk[:], m.aT[k][0:K, :], start=True, stop=True)
                    if layer == 0:
                        for j in range(2):
                            ins = nc.tensor.matmul(narrow[k][:, v_at][:, j * C:(j + 1) * C], m.aT[k][:, j * P:(j + 1) * P], m.wvp[:],
                                                   start=True, stop=True)
                    ins.then_inc(mQ, 1)
                for k in slots:
                    wait_apart(pe, eQ, n(i, k))
                    for j in range(2):
                        ins = nc.tensor.matmul(wide[k][:, j * 2 * P:(j + 1) * 2 * P], m.qT[k][0:K, j * P:(j + 1) * P],
                                               m.aT[k][0:K, :], start=True, stop=True)
                    ins.then_inc(mS, 1)
                for k in slots:
                    pe.wait_ge(xp, n(i, k))
                    for j in range(2):
                        for c in range(2):
                            ins = nc.tensor.transpose(wide[k][:, c * 2 * P + j * P:c * 2 * P + (j + 1) * P],
                                                      m.pr[k][:, j, c * P:(c + 1) * P], m.ident[:])
                    ins.then_inc(tP, 1)
                for k in slots:
                    pe.wait_ge(eP, n(i, k))
                    if layer == 0:
                        pe.wait_ge(eV, n(i, k))
                    v = m.v[k] if layer == 0 else m.an[k]
                    for j in range(2):
                        for c in range(2):
                            ins = nc.tensor.matmul(narrow[k][:, turned_at][:, j * C:(j + 1) * C], m.pT[k][:, c, j * P:(j + 1) * P],
                                                   v[:, c, :], start=(c == 0), stop=(c == 1))
                    ins.then_inc(mO, 1)

        @block.vector
        def _(dve):
            link = Link(dve, m)

            def centre_ahead(g, part):
                if layer == 0 and g < turns:
                    if part == 0:
                        dve.wait_ge(back[g], 16 * GROUP)
                    centre(nc, m, s, link, m.h, tiles_of(g), part)
                    if part == 3:
                        normalised_twice(nc, m, s, dve, link, tiles_of(g), 0, ready, rooted)

            def norm_ahead(g, step):
                if layer == 0 and g < turns:
                    dve.wait_ge(rooted, 2 * g + step)
                    normalised_twice(nc, m, s, dve, link, tiles_of(g), step, ready, rooted)
                    if step == 2:
                        dve.sem_inc(normed, 1)

            def turn(i):
                if layer == 0 and i == 0:
                    for part in range(4):
                        centre_ahead(1, part)
                for k in slots:
                    dve.wait_ge(mQ, n(i, k))
                    nc.vector.tensor_copy(m.qT[k][0:K, :], narrow[k][0:K, q_at]).then_inc(eQ, 1)
                norm_ahead(i + 1, 1)
                for k in slots:
                    wait_apart(dve, mS, n(i, k))
                    st = m.stat[k]
                    if layer == 0:
                        for j in range(2):
                            ins = nc.vector.tensor_tensor_reduce(m.pr[k][:, j, :], wide[k][:, j * 2 * P:(j + 1) * 2 * P],
                                                                 m.relbias[:, (1 - j) * P:(3 - j) * P], 1.0, -3.0e38,
                                                                 ALU.add, ALU.max, st[:, j:j + 1])
                        ins.then_inc(eM, 1)
                    else:
                        nc.vector.tensor_reduce(st[:, 0:2], wide[k][:].rearrange("p (j n) -> p j n", j=2), AX, ALU.max).then_inc(eM, 1)
                    dve.wait_ge(eM, i * (2 * SLOTS) + 2 * k + 1)
                    nc.vector.tensor_scalar(st[:, 2:4], st[:, 0:2], -norm, None, ALU.mult).then_inc(eM, 1)
                norm_ahead(i + 1, 2)
                for k in slots:
                    dve.wait_ge(xp, n(i, k))
                    nc.vector.reciprocal(m.stat[k][:, 6:8], m.stat[k][:, 4:6]).then_inc(rc, 1)
                    dve.wait_ge(tP, n(i, k))
                    nc.vector.tensor_copy(m.pT[k], wide[k][:].rearrange("p (c n) -> p c n", c=2)).then_inc(eP, 1)
                for k in slots:
                    dve.wait_ge(rc, n(i, k))
                    dve.wait_ge(mO, i * SLOTS + (SLOTS + k + 1))
                    nc.vector.tensor_tensor(m.msg[:, bass.ds(i * (2 * SLOTS) + 2 * k, 2), :],
                                            narrow[k][:, turned_at].rearrange("p (j c) -> p j c", j=2),
                                            m.stat[k][:, 6:8].unsqueeze(2).to_broadcast([P, 2, C]), ALU.mult).then_inc(eO, 1)
                    if layer == 0:
                        centre_ahead(i + 2, k)

            dve.sem_inc(eO, SLOTS)
            for part in range(4):
                centre_ahead(0, part)
            for step in (1, 2):
                norm_ahead(0, step)
            each_turn(dve, turn)

        @block.scalar
        def _(act):
            def roots(g):
                if layer == 0 and g < turns:
                    for r in range(2):
                        act.wait_ge(ready, 2 * g + r + 1)
                        nc.scalar.activation(m.std[:, tiles_of(g)], m.var[:, tiles_of(g)], ACT.Sqrt).then_inc(rooted, 1)

            def turn(i):
                for k in slots:
                    act.wait_ge(tA, n(i, k))
                    for j in range(2):
                        nc.scalar.copy(m.aT[k][0:C, j * P:(j + 1) * P], narrow[k][j * C:(j + 1) * C, turned_at]).then_inc(eA, 1)
                if layer == 0:
                    for k in slots:
                        act.wait_ge(mQ, n(i, k))
                        act.wait_ge(eQ, n(i, k))
                        nc.scalar.copy(m.v[k][:].rearrange("p j c -> p (j c)"), narrow[k][:, v_at]).then_inc(eV, 1)
                roots(i + 1)
                for k in slots:
                    act.wait_ge(eM, i * (2 * SLOTS) + 2 * k + 2)
                    for j in range(2):
                        src = m.pr[k][:, j, :] if layer == 0 else wide[k][:, j * 2 * P:(j + 1) * 2 * P]
                        ins = nc.scalar.activation(m.pr[k][:, j, :], src, ACT.Exp, bias=m.stat[k][:, 2 + j:3 + j], scale=norm,
                                                   accum_out=m.stat[k][:, 4 + j:5 + j])
                    ins.then_inc(xp, 1)

            roots(0)
            each_turn(act, turn)


class Turning:

    def __init__(self, m, s, dest, tag):
        self.m, self.s, self.dest = m, s, dest
        self.turned, self.copied_v, self.copied_s = (m.sem(f"{tag}_{n}") for n in ("turned", "copied_v", "copied_s"))

    def turn(self, nc, pe, norm, g):
        m, s = self.m, self.s
        pe.wait_ge(norm.scaled, g + 1)
        for j in range(GROUP):
            ins = nc.tensor.transpose(m.bank[2 * g + j // 4][0:s.C, j % 4 * P:(j % 4 + 1) * P], m.xc[:, GROUP * g + j, :], m.ident[:])
        ins.then_inc(self.turned, 1)

    def copy_vector(self, nc, dve, g):
        dve.wait_ge(self.turned, g + 1)
        dst, src = self.dest(2 * g)
        nc.vector.tensor_copy(dst, src).then_inc(self.copied_v, 1)

    def copy_scalar(self, nc, act, g):
        act.wait_ge(self.turned, g + 1)
        dst, src = self.dest(2 * g + 1)
        nc.scalar.copy(dst, src).then_inc(self.copied_s, 1)


def after_attention0(nc, m, s):
    NT, C = s.NT, s.C
    groups = NT // GROUP
    second, third = Norm(m, s, m.msg, "ln2"), Norm(m, s, m.h, "ln_lstm")
    affine = m.sem("after0_affine")
    wide = [P, GROUP, C]
    having = lambda g: 0 <= g < groups

    def dest(b):
        dst = m.xseq[0:C, 0:s.T].rearrange("c (t b) -> c b t", b=s.B)[:, 2 * b:2 * b + 2, :]
        return dst, m.bank[b][0:C, :].rearrange("c (b t) -> c b t", b=2)

    turning = Turning(m, s, dest, "lin")
    with nc.Block() as block:

        @block.vector
        def _(dve):
            link = Link(dve, m)
            for n in range(groups + 6):
                if having(n):
                    msg = m.msg[:, tiles_of(n), :]
                    link(nc.vector.scalar_tensor_tensor(out=msg, in0=msg, scalar=m.scale[:, 0:1],
                                                        in1=m.pbias[:].unsqueeze(1).to_broadcast(wide), op0=ALU.mult, op1=ALU.add))
                    second.open(nc, link, n)
                if having(n - 1):
                    second.close(nc, dve, n - 1)
                if having(n - 2):
                    second.finish(nc, dve, link, n - 2, scale=True)
                if having(n - 4):
                    third.close(nc, dve, n - 4)
                if having(n - 3):
                    dve.wait_ge(affine, 3 * (n - 3) + 3)
                    third.open(nc, link, n - 3)
                if having(n - 5):
                    third.finish(nc, dve, link, n - 5, scale=True)
                if having(n - 6):
                    turning.copy_vector(nc, dve, n - 6)

        @block.gpsimd
        def _(pool):
            for g in range(groups):
                xc = m.xc[:, tiles_of(g), :]
                pool.wait_ge(second.scaled, g + 1)
                nc.gpsimd.tensor_tensor(xc, xc, m.g2[:].unsqueeze(1).to_broadcast(wide), ALU.mult).then_inc(affine, 1)
                pool.wait_ge(affine, 3 * g + 1)
                nc.gpsimd.tensor_tensor(xc, xc, m.b2ln[:].unsqueeze(1).to_broadcast(wide), ALU.add).then_inc(affine, 1)
                pool.wait_ge(affine, 3 * g + 2)
                nc.gpsimd.tensor_tensor(m.h[:, tiles_of(g), :], m.h[:, tiles_of(g), :], xc, ALU.add).then_inc(affine, 1)

        @block.scalar
        def _(act):
            for n in range(groups + 6):
                if having(n):
                    second.square(nc, act, n)
                if having(n - 1):
                    second.root(nc, act, n - 1)
                if having(n - 4):
                    third.root(nc, act, n - 4)
                if having(n - 3):
                    third.square(nc, act, n - 3)
                if having(n - 6):
                    turning.copy_scalar(nc, act, n - 6)

        @block.tensor
        def _(pe):
            for g in range(groups):
                turning.turn(nc, pe, third, g)


def lstm(nc, m, s):
    C, B = s.C, s.B
    summed, forgot, entered, celled, tanned, hidden, saved = (
        m.sem(f"lstm_{x}") for x in ("summed", "forgot", "entered", "cell", "tanh", "hidden", "saved"))
    lined, biased, weighted, scanned, noted, compared = (
        m.sem(f"lstm_{x}") for x in ("lined", "biased", "weighted", "scanned", "noted", "compared"))
    emptied = m.sem("lstm_emptied")
    turns = s.L // STEPS
    groups = STEPS // AHEAD
    last = s.L // AHEAD - 1

    def gate_bank(q, k):
        return m.bank[2 * q + k // AHEAD % 2]

    def gate_sums(q, k):
        at = k % AHEAD * B
        return gate_bank(q, k)[0:C, at:at + B]

    with nc.Block() as block:

        def project(k, first):
            for q in range(4):
                nc.tensor.matmul(gate_bank(q, k)[0:C, 0:AHEAD * B], m.wi[:, q * C:(q + 1) * C], m.xseq[:, first],
                                 start=True, stop=False, skip_group_check=True)

        def logit_sums(l, k):
            return gate_bank(3, k + AHEAD)[0:C, l * AHEAD * B:(l + 1) * AHEAD * B]

        def logits(k):
            half = (k // AHEAD + 1) % 2 * AHEAD
            for l in range(2):
                ins = nc.tensor.matmul(logit_sums(l, k), m.wlinb[:, l, :], m.ring[0:C, half:half + AHEAD, :], start=True,
                                       stop=True, skip_group_check=True)
            ins.then_inc(lined, 1)

        @block.tensor
        def _(pe):
            project(0, slice(0, AHEAD * B))
            with pe.Fori(0, turns) as i:
                for k in range(STEPS):
                    pe.wait_ge(hidden, i * STEPS + (k + 1))
                    for q in range(4):
                        nc.tensor.matmul(gate_sums(q, k), m.wh[:, q * C:(q + 1) * C], m.ring[:, (k - 1) % RING, :],
                                         start=False, stop=True, skip_group_check=True).then_inc(summed, 1)
                    if k % AHEAD == 0:
                        logits(k)
                    if k % AHEAD == AHEAD - 1:
                        project(k + 1, bass.ds(i * (STEPS * B) + (k + 1) * B, AHEAD * B))
                    else:
                        for w in range(WARMERS // 2 if k % AHEAD == 0 else WARMERS):
                            nc.tensor.matmul(gate_bank(w % 3, k + AHEAD)[0:C, :], m.ones_b[:, 0:C], m.mask[:, 0:512],
                                             start=True, stop=True, skip_group_check=True)

            pe.wait_ge(hidden, s.L + 1)
            logits(0)

        @block.scalar
        def _(act):
            def bias_logit(k):
                nc.scalar.activation(m.lg0, logit_sums(0, k), ACT.Identity, bias=m.blin[:, 0:1]).then_inc(biased, 1)

            with act.Fori(0, turns) as i:
                for k in range(STEPS):
                    n = lambda q: i * (4 * STEPS) + (4 * k + q + 1)
                    act.wait_ge(summed, n(0))
                    nc.scalar.activation(m.forget[:], gate_sums(0, k), ACT.Sigmoid).then_inc(forgot, 1)
                    act.wait_ge(summed, n(1))
                    nc.scalar.activation(m.factors[:, :, 1], gate_sums(1, k), ACT.Sigmoid).then_inc(entered, 1)
                    act.wait_ge(summed, n(2))
                    nc.scalar.activation(m.terms[:, :, 0], gate_sums(2, k), ACT.Tanh).then_inc(entered, 1)
                    act.wait_ge(summed, n(3))
                    nc.scalar.activation(m.emit[:], gate_sums(3, k), ACT.Sigmoid)
                    act.wait_ge(celled, i * STEPS + (k + 1))
                    nc.scalar.activation(m.tanc[:], m.cells[:, :, 1], ACT.Tanh).then_inc(tanned, 1)
                    if k % AHEAD == 1:
                        act.wait_ge(compared, i * groups + (k // AHEAD + 1))
                        act.wait_ge(lined, i * groups + (k // AHEAD + 1))
                        bias_logit(k)
            act.wait_ge(compared, last + 2)
            act.wait_ge(lined, last + 2)
            bias_logit(0)

        @block.vector
        def _(dve):
            def scan():
                flat = lambda t: t[:].rearrange("c b t -> c (b t)")
                nc.vector.tensor_tensor_scan(flat(m.sums), flat(m.keep), flat(m.add), 0.0, ALU.mult, ALU.add).then_inc(scanned, 1)

            def compare(k):
                by_row = lambda t: t.rearrange("c (t b) -> c b t", b=B)
                nc.vector.scalar_tensor_tensor(out=m.gt, in0=by_row(logit_sums(1, k)), scalar=m.blin[:, 1:2],
                                               in1=by_row(m.lg0), op0=ALU.add, op1=ALU.is_gt).then_inc(compared, 1)

            dve.sem_inc(hidden, 1)
            with dve.Fori(0, turns) as i:
                for k in range(STEPS):
                    if k % AHEAD == 0:
                        dve.wait_ge(saved, i * groups + (k // AHEAD + 1))
                    dve.wait_ge(forgot, i * STEPS + (k + 1))
                    nc.vector.tensor_tensor(m.terms[:, :, 1], m.forget[:], m.cells[:, :, 1], ALU.mult).then_inc(entered, 1)
                    dve.wait_ge(entered, i * (3 * STEPS) + (3 * k + 3))
                    nc.vector.tensor_tensor_scan(m.cells[:].rearrange("c b t -> c (b t)"), m.factors[:].rearrange("c b t -> c (b t)"),
                                                 m.terms[:].rearrange("c b t -> c (b t)"), 0.0, ALU.mult, ALU.add).then_inc(celled, 1)
                    dve.wait_ge(tanned, i * STEPS + (k + 1))
                    nc.vector.tensor_tensor(m.ring[0:C, k % RING, :], m.emit[:], m.tanc[:], ALU.mult).then_inc(hidden, 1)
                    if k % AHEAD == 3:
                        dve.wait_ge(biased, i * groups + (k // AHEAD + 1))
                        compare(k)
                    if k % AHEAD == AHEAD - 2:
                        dve.wait_ge(weighted, i * groups + (k // AHEAD + 1))
                        scan()
            dve.wait_ge(biased, last + 2)
            compare(0)
            dve.wait_ge(weighted, last + 2)
            scan()

        @block.sync
        def _(sp):
            sp.wait_ge(emptied, 1)
            halves = m.rows_in.ap()[s.RULE_ZEROS:s.ROWS, :].rearrange("(q p r) c -> q p (r c)", p=P, q=2)
            for q in range(2):
                sp.dma_start(halves[q], m.place[:, 0:(s.ROWS - s.RULE_ZEROS) * s.C // P // 2]).then_inc(emptied, 16)
            sp.wait_ge(emptied, 1 + 2 * 16)

        @block.gpsimd
        def _(pool):
            nc.gpsimd.memset(m.place[:], 0.0).then_inc(emptied, 1)
            hist = m.hist[:].rearrange("c (b t) -> c b t", b=B)
            sums = m.tb[:].rearrange("c (b t) -> c b t", b=B)
            NOTES = 4
            pool.sem_inc(saved, 2)
            pool.sem_inc(compared, 1)
            pool.sem_inc(weighted, 1)
            with pool.Fori(0, turns) as i:
                for g in range(groups):
                    half = g % 2 * AHEAD
                    group = lambda n: i * groups + (g + n)
                    note = lambda n: i * (groups * NOTES) + (g * NOTES + n)
                    steps = bass.ds(i * STEPS + g * AHEAD, AHEAD)
                    h = m.ring[0:C, half:half + AHEAD, :].rearrange("c t b -> c b t")
                    pool.wait_ge(hidden, i * STEPS + ((g + 1) * AHEAD + 1))
                    nc.gpsimd.tensor_tensor(m.twice, h, h, ALU.add).then_inc(saved, 1)
                    wait_apart(pool, scanned, group(1))
                    nc.gpsimd.tensor_copy(m.add[:, :, 0:1], m.sums[:, :, AHEAD:AHEAD + 1]).then_inc(noted, 1)
                    pool.wait_ge(compared, group(3))
                    pool.wait_ge(saved, group(3))
                    pool.wait_ge(noted, note(1))
                    nc.gpsimd.tensor_tensor(m.add[:, :, 1:], m.gt, m.twice, ALU.mult).then_inc(weighted, 1)
                    wait_apart(pool, scanned, group(2))
                    nc.gpsimd.tensor_copy(sums[:, :, steps], m.sums[:, :, 1:]).then_inc(noted, 1)
                    nc.gpsimd.tensor_scalar(m.share, m.sums[:, :, 0:AHEAD], m.fwbw[:, 2:3], None, ALU.mult).then_inc(noted, 1)
                    pool.wait_ge(noted, note(3))
                    nc.gpsimd.tensor_tensor(hist[:, :, steps], m.twice, m.share, ALU.add).then_inc(noted, 1)
                    pool.wait_ge(noted, note(4))


def lstm_output(nc, m, s):
    C, B, T, NT, L = s.C, s.B, s.T, s.NT, s.L
    ready, turned = m.sem("lout_ready"), m.sem("lout_turned")
    norm = Norm(m, s, m.h, "ln_attn1")
    groups = NT // GROUP
    rows = 512 // L
    chunks = B // rows
    tb3 = m.tb[:].rearrange("c (b t) -> c b t", b=B)
    with nc.Block() as block:

        @block.tensor
        def _(pe):
            for g in range(chunks):
                pe.wait_ge(ready, g + 1)
                for j in range(4):
                    ins = nc.tensor.transpose(m.bank[g][:, j * C:(j + 1) * C], m.ta[:, (4 * g + j) * P:(4 * g + j + 1) * P],
                                              m.ident[0:C, 0:C])
                ins.then_inc(turned, 1)

        @block.vector
        def _(dve):
            link = Link(dve, m)
            having = lambda g: 0 <= g < groups
            for n in range(2 * groups + 5):
                if n < chunks:
                    b = slice(n * rows, (n + 1) * rows)
                    now = slice(n * 512, (n + 1) * 512)
                    ta = m.ta[:, now].rearrange("c (b t) -> c b t", b=rows)
                    link(nc.vector.tensor_tensor(ta, tb3[:, b, :], tb3[:, b, L - 1:L].to_broadcast([C, rows, L]), ALU.subtract))
                    nc.vector.scalar_tensor_tensor(out=m.ta[:, now], in0=m.ta[:, now], scalar=m.fwbw[:, 3:4], in1=m.hist[:, now],
                                                   op0=ALU.mult, op1=ALU.add).then_inc(ready, 1)
                if 0 < n <= chunks:
                    dve.wait_ge(turned, n)
                    hg = m.h[:, 4 * (n - 1):4 * n, :]
                    link(nc.vector.tensor_tensor(hg, hg, m.bank[n - 1][:, 0:4 * C].rearrange("p (j c) -> p j c", j=4), ALU.add))
                if n >= 2 and n % 2 == 0:
                    g = n // 2 - 1
                    if having(g):
                        norm.open(nc, link, g)
                    if having(g - 1):
                        norm.close(nc, dve, g - 1)
                    if having(g - 2):
                        norm.finish(nc, dve, link, g - 2, scale=False)

        @block.scalar
        def _(act):
            for g in range(groups + 1):
                if g < groups:
                    norm.square(nc, act, g)
                if g > 0:
                    norm.root(nc, act, g - 1)


def router(nc, m, s):
    NT, C, E, T = s.NT, s.C, s.EXPERTS, s.T
    xT = m.xseq
    groups = NT // GROUP
    norm = Norm(m, s, m.h, "ln_moe")
    turning = Turning(m, s, lambda b: (xT[0:C, b * 512:(b + 1) * 512], m.bank[b][0:C, :]), "rin")
    lined, copied, topped, found = (m.sem(f"router_{x}") for x in ("lined", "copied", "topped", "found"))
    difference, exponent = m.sem("router_diff"), m.sem("router_exp")
    added = m.sem("router_added")
    having = lambda g: 0 <= g < groups
    first = Routing(m, s, E, P, s.CHOICE_BLOCKS, "first", m.first)
    second = Routing(m, s, E, P, s.CHOICE_BLOCKS + 2 * TURN, "second", m.second, which=1, first_block=s.CHOICE_BLOCKS, count_bank=3)
    m.routings = (first, second)

    def copy_logits(act, g):
        act.wait_ge(lined, g + 1)
        nc.scalar.copy(m.logits[:, tiles_of(g), :], m.bank[2 * g][:, 0:GROUP * E].rearrange("p (j e) -> p j e", j=GROUP)).then_inc(copied, 1)

    def best_two(dve, link, g):
        dve.wait_ge(copied, g + 1)
        t8 = tiles_of(g)
        for t in range(g * GROUP, (g + 1) * GROUP):
            nc.vector.max(m.top[:, t, :], m.logits[:, t, :]).then_inc(topped, 1)
        for t in range(g * GROUP, (g + 1) * GROUP):
            dve.wait_ge(topped, t + 1)
            nc.vector.max_index(m.topi[:, t, :], m.top[:, t, :], m.logits[:, t, :]).then_inc(found, 1)
        dve.wait_ge(found, (g + 1) * GROUP)
        link(nc.vector.tensor_copy(m.topf[:, t8, :], m.topi[:, t8, 0:2]))
        shape = [P, GROUP, E]
        flat = slice(g * GROUP * E, (g + 1) * GROUP * E)
        for which, r in enumerate((first, second)):
            nc.vector.tensor_tensor(r.mask[:, flat].rearrange("p (t e) -> p t e", t=GROUP),
                                    m.topf[:, t8, which:which + 1].to_broadcast(shape),
                                    m.iota[:, 0:E].unsqueeze(1).to_broadcast(shape), ALU.is_equal).then_inc(r.masked, 1)

    with nc.Block() as block:

        @block.gpsimd
        def _(pool):
            for g in range(groups):
                h = m.h[:, tiles_of(g), :]
                nc.gpsimd.tensor_tensor(h, h, m.msg[:, tiles_of(g), :], ALU.add).then_inc(added, 1)

        @block.tensor
        def _(pe):
            for n in range(groups + 1):
                if having(n):
                    turning.turn(nc, pe, norm, n)
                if having(n - 1):
                    g = n - 1
                    pe.wait_ge(turning.copied_v, g + 1)
                    pe.wait_ge(turning.copied_s, g + 1)
                    for j in range(GROUP):
                        t = GROUP * g + j
                        ins = nc.tensor.matmul(m.bank[2 * g][:, j * E:(j + 1) * E], xT[:, t * P:(t + 1) * P], m.wr[:], start=True, stop=True)
                    ins.then_inc(lined, 1)
            for g in range(groups):
                pe.wait_ge(first.masked, g + 1)
                count_choices(nc, m, s, first, range(g * GROUP, (g + 1) * GROUP))
                pe.wait_ge(second.masked, g + 1)
                count_choices(nc, m, s, second, range(g * GROUP, (g + 1) * GROUP))

        @block.scalar
        def _(act):
            for n in range(groups + 4):
                if having(n):
                    norm.square(nc, act, n)
                if having(n - 1):
                    norm.root(nc, act, n - 1)
                if having(n - 3):
                    turning.copy_scalar(nc, act, n - 3)
                if having(n - 4):
                    copy_logits(act, n - 4)
            act.wait_ge(difference, 1)
            nc.scalar.activation(m.gtmp[:, 1, :], m.gtmp[:, 0, :], ACT.Exp).then_inc(exponent, 1)

        @block.vector
        def _(dve):
            link = Link(dve, m)
            for n in range(groups + 5):
                if having(n):
                    dve.wait_ge(added, n + 1)
                    norm.open(nc, link, n)
                if having(n - 1):
                    norm.close(nc, dve, n - 1)
                if having(n - 2):
                    norm.finish(nc, dve, link, n - 2, scale=True)
                if having(n - 3):
                    turning.copy_vector(nc, dve, n - 3)
                if having(n - 5):
                    best_two(dve, link, n - 5)
            nc.vector.tensor_tensor(m.gtmp[:, 0, :], m.top[:, :, 1], m.top[:, :, 0], ALU.subtract).then_inc(difference, 1)
            dve.wait_ge(exponent, 1)
            link(nc.vector.tensor_scalar(m.gtmp[:, 2, :], m.gtmp[:, 1, :], 1.0, None, ALU.add))
            link(nc.vector.reciprocal(m.gate[:, 0, :], m.gtmp[:, 2, :]))
            link(nc.vector.tensor_tensor(m.gate[:, 1, :], m.gate[:, 0, :], m.gtmp[:, 1, :], ALU.mult))


def expert_routes(nc, m, s):
    routing = m.routings[0]
    with nc.Block() as block:

        @block.tensor
        def _(pe):
            route_pe(nc, m, s, pe, routing)

        @block.vector
        def _(dve):
            route_dve(nc, m, s, dve, routing)


def expert_blocks(nc, m, s, ins):
    NT, C, H, E = s.NT, s.C, s.HID, s.EXPERTS
    turns = s.expert_turns
    scattered = [m.sem(f"exp_scattered{k}") for k in range(2)]
    routed = m.sem("exp_routed")
    m.first_back = m.sem("exp_first_back")
    routing = m.routings[1]
    x_in = [m.sem(f"exp_x{k}") for k in range(DEPTH)]
    y_out = [m.sem(f"exp_y{k}") for k in range(2)]
    turned, copied, picked, up, active, down, kept = (
        m.sem(f"exp_{x}") for x in ("turned", "copied", "picked", "up", "active", "down", "kept"))
    gated, g_turned, g_copied, g_added, g_summed = (m.sem(f"bias_{x}") for x in ("gated", "turned", "copied", "added", "summed"))
    rows_in, rows_out = m.rows_in.ap(), m.rows_out.ap()
    gates = m.spread[:, 0:NT * E].rearrange("p (t e) -> p t e", t=NT)
    other = m.place[:, 0:NT * E].rearrange("p (t e) -> p t e", t=NT)
    groups = NT // 4

    def after(i, j, each, ahead=0):
        return i * (DEPTH * each) + each * (j + ahead + 1)

    with nc.Block() as block:

        @block.gpsimd
        def _(pool):
            for which in range(2):
                if which == 1:
                    pool.wait_ge(routed, 1)
                for t in range(NT):
                    index = bass.IndirectOffsetOnAxis(ap=m.pos_i[:, which, t:t + 1], axis=0)
                    pool.indirect_dma_start(rows_in, index, m.xc[:, t, :], None).then_inc(scattered[which], 16)
            for j in range(2):
                pool.wait_ge(y_out[j], 16 * (s.choice_turns // 2 + 1))
            for t in range(NT):
                index = bass.IndirectOffsetOnAxis(ap=m.pos_i[:, 0, t:t + 1], axis=0)
                pool.indirect_dma_start(m.msg[:, t, :], None, rows_out[0:s.choice_turns * s.TURN_ROWS, :], index).then_inc(m.first_back, 16)

        @block.sync
        def _(sp):
            sp.wait_ge(scattered[0], 16 * NT)
            load_turns(sp, m, turns, x_in, turned, s.choice_turns, scattered[1], 16 * NT)

        @block.tensor
        def _(pe):
            route_pe(nc, m, s, pe, routing)
            pe.wait_ge(m.loaded_experts, 4 * 16)
            for g in range(groups + 1):
                if g < groups:
                    pe.wait_ge(gated, 3 * (g + 1))
                    if g >= 2:
                        pe.wait_ge(g_copied, g - 1)
                    for a in range(4):
                        ins_ = nc.tensor.transpose(m.bank[6 + g % 2][0:E, a * P:(a + 1) * P], gates[:, 4 * g + a, :], m.ident[:])
                    ins_.then_inc(g_turned, 1)
                if g > 0:
                    b = g - 1
                    pe.wait_ge(g_copied, b + 1)
                    if b >= 2:
                        pe.wait_ge(g_summed, b - 1)
                    for a in range(4):
                        ins_ = nc.tensor.matmul(m.bank[4 + b % 2][:, a * C:(a + 1) * C], m.gT[b % 2][:, a * P:(a + 1) * P], m.b2_all[:],
                                                start=True, stop=True)
                    ins_.then_inc(g_added, 1)

            def ups(k2):
                for k in range(TURN):
                    ins_ = nc.tensor.matmul(m.bank[2 + k2][:, k * P:(k + 1) * P], m.w1[k2][:, k, :], m.xT[k2][0:C + 1, k, :], start=True, stop=True)
                ins_.then_inc(up, 1)

            pe.wait_ge(scattered[0], 16 * NT)
            warm(nc, m, 2 * WARMERS)
            for j in range(2):
                pe.wait_ge(x_in[j], 16)
                transpose_turn(nc, m, j, m.xb[j], turned)
            warm(nc, m, 2 * WARMERS)
            pe.wait_ge(copied, 2)
            pe.wait_ge(picked, TURN)
            ups(0)
            with pe.Fori(0, turns // DEPTH) as i:
                for j in range(DEPTH):
                    k2, ahead = j % 2, (j + 2) % DEPTH
                    pe.wait_ge(x_in[ahead], i * 16 + 16 * ((j + 2) // DEPTH + 1))
                    transpose_turn(nc, m, k2, m.xb[ahead], turned)
                    pe.wait_ge(copied, after(i, j, 2, ahead=1))
                    pe.wait_ge(picked, after(i, j, TURN, ahead=1))
                    ups(1 - k2)
                    owners = load_owners(nc, mybir.EngineType.PE, m, i * (DEPTH * TURN) + TURN * j, TURN, E)
                    pe.wait_ge(active, after(i, j, 1))
                    pe.wait_ge(kept, after(i, j, 1))
                    for k in range(TURN):
                        ins_ = nc.tensor.matmul(m.bank[4 + k2][:, k * C:(k + 1) * C], m.hT[k2][:, k, :],
                                                m.w2_all[:, bass.ds(owners[k], 1), :].rearrange("h a c -> h (a c)"), start=True, stop=True)
                    ins_.then_inc(down, 1)

        @block.scalar
        def _(act):
            for g in range(groups):
                act.wait_ge(g_turned, g + 1)
                if g >= 2:
                    act.wait_ge(g_added, g - 1)
                nc.scalar.copy(m.gT[g % 2][:], m.bank[6 + g % 2][0:E, :]).then_inc(g_copied, 1)
            for j in range(2):
                act.wait_ge(turned, j + 1)
                copy_turn(nc, m, s, j, copied)
            with act.Fori(0, turns // DEPTH) as i:
                for j in range(DEPTH):
                    k2 = j % 2
                    act.wait_ge(up, after(i, j, 1))
                    act.wait_ge(turned, after(i, j, 1, ahead=2))
                    copy_turn(nc, m, s, k2, copied)
                    act.wait_ge(kept, after(i, j, 1, ahead=2))
                    act.dma_start(turn_rows(rows_out, i * DEPTH + j), m.yb[k2][:]).then_inc(y_out[k2], 16)
            for j in range(2):
                act.wait_ge(y_out[j], 16 * (turns // 2 + 1))

        @block.vector
        def _(dve):
            route_dve(nc, m, s, dve, routing)
            dve.sem_inc(routed, 1)
            wide = [P, 4, E]
            as3 = lambda ap: ap[:].rearrange("p (t e) -> p t e", t=NT)
            for g in range(groups + 2):
                if g < groups:
                    t = slice(4 * g, 4 * g + 4)
                    nc.vector.tensor_tensor(gates[:, t, :], as3(m.first)[:, t, :], m.gate[:, 0, t].unsqueeze(2).to_broadcast(wide),
                                            ALU.mult).then_inc(gated, 1)
                    nc.vector.tensor_tensor(other[:, t, :], as3(m.second)[:, t, :], m.gate[:, 1, t].unsqueeze(2).to_broadcast(wide),
                                            ALU.mult).then_inc(gated, 1)
                    dve.wait_ge(gated, 3 * g + 2)
                    nc.vector.tensor_tensor(gates[:, t, :], gates[:, t, :], other[:, t, :], ALU.add).then_inc(gated, 1)
                if g >= 2:
                    b = g - 2
                    dve.wait_ge(g_added, b + 1)
                    hg = m.h[:, 4 * b:4 * b + 4, :]
                    nc.vector.tensor_tensor(hg, hg, m.bank[4 + b % 2][:, 0:4 * C].rearrange("p (a c) -> p a c", a=4), ALU.add).then_inc(g_summed, 1)

            def owners_of(turn):
                return load_owners(nc, mybir.EngineType.DVE, m, turn * TURN, TURN, E)

            def pick(owners, k2):
                for k, e in enumerate(owners):
                    nc.vector.tensor_copy(m.w1[k2][:, k, :], m.w1_all[:, bass.ds(e, 1), :].rearrange("d a h -> d (a h)")).then_inc(picked, 1)

            def relus(k2):
                nc.vector.tensor_scalar(m.hT[k2][:], m.bank[2 + k2][:].rearrange("h (k p) -> h k p", k=TURN), 0.0, None, ALU.max).then_inc(active, 1)

            dve.wait_ge(m.loaded_experts, 4 * 16)
            for j in range(2):
                pick(owners_of(j), j)
            dve.sem_inc(kept, 2)
            dve.sem_inc(down, 1)
            for j in range(2):
                dve.sem_inc(y_out[j], 16)
            dve.wait_ge(up, 1)
            relus(0)
            with dve.Fori(0, turns // DEPTH) as i:
                for j in range(DEPTH):
                    k2 = j % 2
                    owners = owners_of(i * DEPTH + (j + 2))
                    dve.wait_ge(up, after(i, j, 1))
                    pick(owners, k2)
                    dve.wait_ge(up, after(i, j, 1, ahead=1))
                    dve.wait_ge(down, after(i, j, 1))
                    relus(1 - k2)
                    dve.wait_ge(down, after(i, j, 1, ahead=1))
                    dve.wait_ge(y_out[k2], i * (16 * DEPTH // 2) + 16 * (j // 2 + 1))
                    nc.vector.tensor_copy(m.yb[k2][:], m.bank[4 + k2][:, 0:TURN * C].rearrange("p (k c) -> p k c", k=TURN)).then_inc(kept, 1)


def combine(nc, m, s, out):
    NT, C = s.NT, s.C
    groups = NT // GROUP
    gathered = [m.sem(f"comb_gathered{g}") for g in range(groups)]
    summed, stored = m.sem("comb_summed"), m.sem("comb_stored")
    with nc.Block() as block:

        @block.gpsimd
        def _(pool):
            for t in range(NT):
                index = bass.IndirectOffsetOnAxis(ap=m.pos_i[:, 1, t:t + 1], axis=0)
                pool.indirect_dma_start(m.sq[:, t, :], None, m.rows_out.ap()[0:s.expert_turns * s.TURN_ROWS, :],
                                        index).then_inc(gathered[t // GROUP], 16)

        @block.vector
        def _(dve):
            link = Link(dve, m)

            def gate(which, y, t):
                link(nc.vector.tensor_tensor(y, y, m.gate[:, which, t].unsqueeze(2).to_broadcast([P, t.stop - t.start, C]), ALU.mult))
                return nc.vector.tensor_tensor(m.h[:, t, :], m.h[:, t, :], y, ALU.add)

            dve.wait_ge(m.first_back, 16 * NT)
            link(gate(0, m.msg[:], slice(0, NT)))
            for g in range(groups):
                dve.wait_ge(gathered[g], 16 * GROUP)
                gate(1, m.sq[:, tiles_of(g), :], tiles_of(g)).then_inc(summed, 1)

        @block.sync
        def _(sp):
            rows = out.rearrange("b (h p) c -> p (b h) c", p=P)
            for g in range(groups):
                sp.wait_ge(summed, g + 1)
                sp.dma_start(rows[:, tiles_of(g), :], m.h[:, tiles_of(g), :]).then_inc(stored, 16)
            sp.wait_ge(stored, 16 * groups)


_INS = ["x", "L0_tok_base_embeddings", "L0_tok_rule_transform", "L0_tok_token_rules", "L0_attn_ln1_g", "L0_attn_ln1_b",
        "L0_attn_qkv_w", "L0_attn_qkv_b", "L0_attn_bias_table", "L0_attn_scale", "L0_attn_proj_w", "L0_attn_proj_b",
        "L0_attn_ln2_g", "L0_attn_ln2_b", "L0_ffn_W_ih", "L0_ffn_W_hh", "L0_ffn_b_ih", "L0_ffn_b_hh", "L0_ffn_W_lin",
        "L0_ffn_b_lin", "L0_ffn_fw_att", "L0_ffn_bw_att", "L1_attn_W", "L1_ffn_Wr", "L1_ffn_br", "L1_ffn_W1", "L1_ffn_b1",
        "L1_ffn_W2", "L1_ffn_b2"]


def kernel(**inputs):
    import numpy as _np
    import concourse.bacc as _bacc
    from concourse.bass_utils import run_bass_kernel_spmd as _run

    nc = _bacc.Bacc("TRN2", target_bir_lowering=False, num_devices=1)
    arrays, args = {}, {}
    for name in _INS:
        a = _np.ascontiguousarray(inputs[name])
        if a.ndim == 0:
            a = a.reshape(1)
        arrays[f"in_{name}"] = a
        args[name] = nc.dram_tensor(f"in_{name}", a.shape, mybir.dt.from_np(a.dtype), kind="ExternalInput").ap()
    shape = tuple(inputs["x"].shape) + (inputs["L0_tok_base_embeddings"].shape[1],)
    result = nc.dram_tensor("result", shape, F32, kind="ExternalOutput").ap()
    tower(nc, args, result)
    r = _run(nc, [arrays], core_ids=[0])
    return r.results[0]["result"]
```
